# Optimizing a Trainium2 kernel written in Bass

```python
import numpy as np
import jax
import jax.numpy as jnp

def _softmax(x, axis=-1):
    return jax.nn.softmax(x, axis=axis)

def _gelu(x):
    return jax.nn.gelu(x, approximate=True)

def _silu(x):
    return jax.nn.silu(x)

def _sigmoid(x):
    return jax.nn.sigmoid(x)

def _layernorm(x, axis=-1, eps=1e-05):
    m = jnp.mean(x, axis=axis, keepdims=True)
    v = jnp.var(x, axis=axis, keepdims=True)
    return (x - m) / jnp.sqrt(v + eps)

def _scatter_add(tgt, idx, src, axis=0):
    return tgt.at[idx].add(src)

def _segment_sum(src, seg, n):
    return jax.ops.segment_sum(src, seg, n)
kernel_name = 'mk_gnn_preln_d4_gnn_r32_3cae65'

def setup_inputs(seed: int=0):
    np.random.seed(seed)
    _w = jnp.asarray

    def _rec_inputs():
        import jax
        import jax.numpy as jnp
        _gk = jax.random.key(seed)
        x = -0.0003713 + 1 * jax.random.normal(jax.random.fold_in(_gk, 1), (3125, 128), jnp.float32)
        src = jax.random.randint(jax.random.fold_in(_gk, 2), (50000,), 0, 3125, jnp.int32)
        dst = jnp.minimum((3125 * jax.random.uniform(jax.random.fold_in(_gk, 3), (50000,)) ** 2.0).astype(jnp.int32), 99999)
        _o = jnp.argsort(dst, stable=True)
        src = src[_o]
        dst = dst[_o]
        edge_attr_64 = 0.000155561 + 1.00019 * jax.random.normal(jax.random.fold_in(_gk, 12), (50000, 64), jnp.float32)
        edge_weight = jax.random.uniform(jax.random.fold_in(_gk, 14), (50000,), jnp.float32, 0.0, 0.999999)
        return (x, src, dst, edge_attr_64, edge_weight)
    x, src, dst, edge_attr_64, edge_weight = _rec_inputs()

    def _L0_gnn_setup():
        import jax, jax.numpy as jnp
        import numpy as np
        N = 3125
        E = 50000
        IN = 128
        H = 128
        L = 2
        EPS = 1e-05

        def _bn(h, gamma, beta):
            m = jnp.mean(h, axis=0)
            v = jnp.var(h, axis=0)
            return (h - m) * jax.lax.rsqrt(v + EPS) * gamma + beta

        def _aggregate(h, row, col, edge_weight):
            d = jax.ops.segment_sum(jnp.ones_like(edge_weight), col, num_segments=N)
            val = edge_weight * jax.lax.rsqrt(d[col]) * jax.lax.rsqrt(d[row])
            val = jnp.nan_to_num(val, nan=0.0, posinf=0.0, neginf=0.0)
            return jax.ops.segment_sum(val[:, None] * h[row], col, num_segments=N)
        key = jax.random.key(seed)
        ks = jax.random.split(key, 8)
        x = jax.random.normal(ks[0], (N, IN), dtype=jnp.float32)
        edge_index = jax.random.randint(ks[1], (2, E), 0, N, dtype=jnp.int32)
        edge_weight = jax.random.uniform(ks[2], (E,), dtype=jnp.float32)
        s_in = 1.0 / np.sqrt(IN)
        s_h = 1.0 / np.sqrt(H)
        fc_w = jax.random.uniform(ks[3], (IN, H), jnp.float32, -s_in, s_in)
        fc_b = jax.random.uniform(ks[4], (H,), jnp.float32, -s_in, s_in)
        conv_w = jax.random.uniform(ks[5], (L, H, H), jnp.float32, -s_h, s_h)
        conv_b = jax.random.uniform(ks[6], (L, H), jnp.float32, -s_h, s_h)
        bn_gamma = jnp.ones((L + 1, H), jnp.float32)
        bn_beta = jnp.zeros((L + 1, H), jnp.float32)
        return {'x': x, 'edge_index': edge_index, 'edge_weight': edge_weight, 'fc_w': fc_w, 'fc_b': fc_b, 'conv_w': conv_w, 'conv_b': conv_b, 'bn_gamma': bn_gamma, 'bn_beta': bn_beta}
    _L0_gnn_all = _L0_gnn_setup()
    _L0_gnn_in = {k: v for k, v in _L0_gnn_all.items() if k in ('fc_w', 'fc_b', 'conv_w', 'conv_b', 'bn_gamma', 'bn_beta')}
    del _L0_gnn_all

    def _L1_gnn_setup():
        import jax, jax.numpy as jnp
        import numpy as np
        N_NODES, N_EDGES = (50000, 18750)
        NODE_DIM, EDGE_DIM = (128, 64)
        H, HD = (4, 32)
        key = jax.random.key(seed)
        k = jax.random.split(key, 6)
        node_features = jax.random.normal(k[0], (N_NODES, NODE_DIM), jnp.float32)
        edge_indices = jax.random.randint(k[1], (2, N_EDGES), 0, N_NODES, jnp.int32)
        edge_features = jax.random.normal(k[2], (N_EDGES, EDGE_DIM), jnp.float32)
        W_node = jax.random.normal(k[3], (H * HD, NODE_DIM), jnp.float32) / np.sqrt(NODE_DIM).astype(np.float32)
        W_edge = jax.random.normal(k[4], (H * HD, EDGE_DIM), jnp.float32) / np.sqrt(EDGE_DIM).astype(np.float32)
        a = jax.random.normal(k[5], (H, 3 * HD), jnp.float32)
        return {'node_features': node_features, 'edge_indices': edge_indices, 'edge_features': edge_features, 'W_node': W_node, 'W_edge': W_edge, 'a': a}
    _L1_gnn_all = _L1_gnn_setup()
    _L1_gnn_in = {k: v for k, v in _L1_gnn_all.items() if k in ('W_node', 'W_edge', 'a')}
    del _L1_gnn_all

    def _L2_gnn_setup():
        import jax, jax.numpy as jnp
        import numpy as np
        N = 50000
        E = 25000
        D = 128
        H = 8
        DK = D // H
        key = jax.random.key(seed)
        ks = jax.random.split(key, 12)
        s = 1.0 / np.sqrt(D)
        return {'h': jax.random.normal(ks[0], (N, D), dtype=jnp.float32), 'Wq': jax.random.normal(ks[1], (D, D), dtype=jnp.float32) * s, 'bq': jnp.zeros((D,), dtype=jnp.float32), 'Wk': jax.random.normal(ks[2], (D, D), dtype=jnp.float32) * s, 'bk': jnp.zeros((D,), dtype=jnp.float32), 'Wv': jax.random.normal(ks[3], (D, D), dtype=jnp.float32) * s, 'bv': jnp.zeros((D,), dtype=jnp.float32), 'Wo': jax.random.normal(ks[4], (D, D), dtype=jnp.float32) * s, 'bo': jnp.zeros((D,), dtype=jnp.float32), 'src': jax.random.randint(ks[5], (E,), 0, N, dtype=jnp.int64) if jax.config.jax_enable_x64 else jax.random.randint(ks[5], (E,), 0, N, dtype=jnp.int32), 'dst': jax.random.randint(ks[6], (E,), 0, N, dtype=jnp.int32)}
    _L2_gnn_all = _L2_gnn_setup()
    _L2_gnn_in = {k: v for k, v in _L2_gnn_all.items() if k in ('Wq', 'bq', 'Wk', 'bk', 'Wv', 'bv', 'Wo', 'bo')}
    del _L2_gnn_all

    def _L3_gnn_setup():
        import jax, jax.numpy as jnp
        import numpy as np
        N_NODES = 50000
        N_EDGES = 18750
        DIM = 128
        N_LAYERS = 2

        def _fa_layer(h, row, col, Wt_l, bt_l, Wg_l, bg_l):
            h = h @ Wt_l.T + bt_l
            n = h.shape[0]
            ones = jnp.ones(row.shape, dtype=h.dtype)
            deg = jnp.clip(jax.ops.segment_sum(ones, row, num_segments=n), 1.0)
            dinv = deg ** (-0.5)
            g = jnp.tanh(h[row] @ Wg_l + bg_l)
            norm = g * dinv[row] * dinv[col]
            msg = norm[:, None] * h[row]
            out = jax.ops.segment_sum(msg, col, num_segments=n)
            return out + h
        key = jax.random.key(seed)
        ks = jax.random.split(key, 4)
        x = jax.random.normal(ks[0], (N_NODES, DIM), dtype=jnp.float32)
        edge_index = jax.random.randint(ks[1], (2, N_EDGES), 0, N_NODES, dtype=jnp.int32)
        Wt = jax.random.normal(ks[2], (N_LAYERS, DIM, DIM), dtype=jnp.float32) * (1.414 * (2.0 / (2 * DIM)) ** 0.5)
        Wg = jax.random.normal(ks[3], (N_LAYERS, DIM), dtype=jnp.float32) * (1.414 * (2.0 / (DIM + 1)) ** 0.5)
        bt = jnp.zeros((N_LAYERS, DIM), dtype=jnp.float32)
        bg = jnp.zeros((N_LAYERS,), dtype=jnp.float32)
        return {'x': x, 'edge_index': edge_index, 'Wt': Wt, 'bt': bt, 'Wg': Wg, 'bg': bg}
    _L3_gnn_all = _L3_gnn_setup()
    _L3_gnn_in = {k: v for k, v in _L3_gnn_all.items() if k in ('Wt', 'bt', 'Wg', 'bg')}
    del _L3_gnn_all
    return {'x': x, 'src': src, 'dst': dst, 'edge_attr_64': edge_attr_64, 'edge_weight': edge_weight, 'L0_gnn_fc_w': _L0_gnn_in['fc_w'], 'L0_gnn_fc_b': _L0_gnn_in['fc_b'], 'L0_gnn_conv_w': _L0_gnn_in['conv_w'], 'L0_gnn_conv_b': _L0_gnn_in['conv_b'], 'L0_gnn_bn_gamma': _L0_gnn_in['bn_gamma'], 'L0_gnn_bn_beta': _L0_gnn_in['bn_beta'], 'L1_gnn_W_node': _L1_gnn_in['W_node'], 'L1_gnn_W_edge': _L1_gnn_in['W_edge'], 'L1_gnn_a': _L1_gnn_in['a'], 'L2_gnn_Wq': _L2_gnn_in['Wq'], 'L2_gnn_bq': _L2_gnn_in['bq'], 'L2_gnn_Wk': _L2_gnn_in['Wk'], 'L2_gnn_bk': _L2_gnn_in['bk'], 'L2_gnn_Wv': _L2_gnn_in['Wv'], 'L2_gnn_bv': _L2_gnn_in['bv'], 'L2_gnn_Wo': _L2_gnn_in['Wo'], 'L2_gnn_bo': _L2_gnn_in['bo'], 'L3_gnn_Wt': _L3_gnn_in['Wt'], 'L3_gnn_bt': _L3_gnn_in['bt'], 'L3_gnn_Wg': _L3_gnn_in['Wg'], 'L3_gnn_bg': _L3_gnn_in['bg']}

def reference(x, src, dst, edge_attr_64, edge_weight, L0_gnn_fc_w, L0_gnn_fc_b, L0_gnn_conv_w, L0_gnn_conv_b, L0_gnn_bn_gamma, L0_gnn_bn_beta, L1_gnn_W_node, L1_gnn_W_edge, L1_gnn_a, L2_gnn_Wq, L2_gnn_bq, L2_gnn_Wk, L2_gnn_bk, L2_gnn_Wv, L2_gnn_bv, L2_gnn_Wo, L2_gnn_bo, L3_gnn_Wt, L3_gnn_bt, L3_gnn_Wg, L3_gnn_bg):
    import jax
    import jax.numpy as jnp

    def _L0_gnn_ref(x, edge_index, edge_weight, fc_w, fc_b, conv_w, conv_b, bn_gamma, bn_beta):
        import jax, jax.numpy as jnp
        import numpy as np
        N = 3125
        E = 50000
        IN = 128
        H = 128
        L = 2
        EPS = 1e-05

        def _bn(h, gamma, beta):
            m = jnp.mean(h, axis=0)
            v = jnp.var(h, axis=0)
            return (h - m) * jax.lax.rsqrt(v + EPS) * gamma + beta

        def _aggregate(h, row, col, edge_weight):
            d = jax.ops.segment_sum(jnp.ones_like(edge_weight), col, num_segments=N)
            val = edge_weight * jax.lax.rsqrt(d[col]) * jax.lax.rsqrt(d[row])
            val = jnp.nan_to_num(val, nan=0.0, posinf=0.0, neginf=0.0)
            return jax.ops.segment_sum(val[:, None] * h[row], col, num_segments=N)
        row, col = (edge_index[0], edge_index[1])
        h = jax.nn.relu(_bn(x @ fc_w + fc_b, bn_gamma[0], bn_beta[0]))
        for i in range(L):
            z = _aggregate(h, row, col, edge_weight) @ conv_w[i] + conv_b[i]
            z = jax.nn.relu(_bn(z, bn_gamma[i + 1], bn_beta[i + 1]))
            h = z + h
        return h

    def _L1_gnn_ref(node_features, edge_indices, edge_features, W_node, W_edge, a):
        import jax, jax.numpy as jnp
        import numpy as np
        N_NODES, N_EDGES = (50000, 18750)
        NODE_DIM, EDGE_DIM = (128, 64)
        H, HD = (4, 32)
        num_nodes = node_features.shape[0]
        num_edges = edge_indices.shape[1]
        h = (node_features @ W_node.T).reshape(num_nodes, H, HD)
        e = (edge_features @ W_edge.T).reshape(num_edges, H, HD)
        src, tgt = (edge_indices[0], edge_indices[1])
        h_src = h[src]
        h_tgt = h[tgt]
        att_in = jnp.concatenate([h_src, h_tgt, e], axis=-1)
        att = jnp.sum(att_in * a, axis=-1)
        att = jnp.where(att > 0, att, 0.2 * att)
        m = jnp.maximum(jax.ops.segment_max(att, tgt, num_segments=num_nodes), 0.0)
        ex = jnp.exp(att - m[tgt])
        ones = jnp.ones((num_edges,), node_features.dtype)
        deg = jax.ops.segment_sum(ones, tgt, num_segments=num_nodes)
        denom = jax.ops.segment_sum(ex, tgt, num_segments=num_nodes) + (num_edges - deg)[:, None] * jnp.exp(-m)
        w = ex / denom[tgt]
        h_prime = jax.ops.segment_sum(w[:, :, None] * h_src, tgt, num_segments=num_nodes)
        return h_prime.reshape(num_nodes, H * HD)

    def _L2_gnn_ref(h, Wq, bq, Wk, bk, Wv, bv, Wo, bo, src, dst):
        import jax, jax.numpy as jnp
        import numpy as np
        N = 50000
        E = 25000
        D = 128
        H = 8
        DK = D // H
        n = h.shape[0]
        scale = jnp.asarray(np.sqrt(DK), dtype=h.dtype)
        q = (h @ Wq.T + bq).reshape(n, H, DK)
        k = (h @ Wk.T + bk).reshape(n, H, DK)
        v = (h @ Wv.T + bv).reshape(n, H, DK)
        score = jnp.einsum('ehd,ehd->eh', q[dst], k[src]) / scale
        m = jax.ops.segment_max(score, dst, num_segments=n)
        ex = jnp.exp(score - m[dst])
        denom = jax.ops.segment_sum(ex, dst, num_segments=n)
        alpha = ex / denom[dst]
        msg = v[src] * alpha[:, :, None]
        att = jax.ops.segment_sum(msg, dst, num_segments=n).reshape(n, D)
        return att @ Wo.T + bo

    def _L3_gnn_ref(x, edge_index, Wt, bt, Wg, bg):
        import jax, jax.numpy as jnp
        import numpy as np
        N_NODES = 50000
        N_EDGES = 18750
        DIM = 128
        N_LAYERS = 2

        def _fa_layer(h, row, col, Wt_l, bt_l, Wg_l, bg_l):
            h = h @ Wt_l.T + bt_l
            n = h.shape[0]
            ones = jnp.ones(row.shape, dtype=h.dtype)
            deg = jnp.clip(jax.ops.segment_sum(ones, row, num_segments=n), 1.0)
            dinv = deg ** (-0.5)
            g = jnp.tanh(h[row] @ Wg_l + bg_l)
            norm = g * dinv[row] * dinv[col]
            msg = norm[:, None] * h[row]
            out = jax.ops.segment_sum(msg, col, num_segments=n)
            return out + h
        row, col = (edge_index[0], edge_index[1])
        h = x
        for l in range(N_LAYERS):
            h = _fa_layer(h, row, col, Wt[l], bt[l], Wg[l], bg[l])
            h = jax.nn.relu(h)
        return h
    edge_index = jnp.stack([src, dst])
    h = jnp.maximum(_layernorm(x, axis=-1), 0.0)
    x = x + _L0_gnn_ref(h, edge_index, edge_weight, L0_gnn_fc_w, L0_gnn_fc_b, L0_gnn_conv_w, L0_gnn_conv_b, L0_gnn_bn_gamma, L0_gnn_bn_beta)
    h = jnp.maximum(_layernorm(x, axis=-1), 0.0)
    x = x + _L1_gnn_ref(h, edge_index, edge_attr_64, L1_gnn_W_node, L1_gnn_W_edge, L1_gnn_a)
    h = jnp.maximum(_layernorm(x, axis=-1), 0.0)
    x = x + _L2_gnn_ref(h, L2_gnn_Wq, L2_gnn_bq, L2_gnn_Wk, L2_gnn_bk, L2_gnn_Wv, L2_gnn_bv, L2_gnn_Wo, L2_gnn_bo, src, dst)
    h = jnp.maximum(_layernorm(x, axis=-1), 0.0)
    x = x + _L3_gnn_ref(h, edge_index, L3_gnn_Wt, L3_gnn_bt, L3_gnn_Wg, L3_gnn_bg)
    return x

_drawn_inputs = setup_inputs


def setup_inputs(seed=0):
    import zlib

    import numpy as np

    out = dict(_drawn_inputs(seed))
    spreads = {'L0_gnn_bn_gamma': (1.0, 0.2),
     'L0_gnn_bn_beta': (0.0, 0.1),
     'L2_gnn_bq': (0.0, 0.8),
     'L2_gnn_bk': (0.0, 0.8),
     'L2_gnn_bv': (0.0, 0.1),
     'L2_gnn_bo': (0.0, 0.1),
     'L3_gnn_bt': (0.0, 0.1),
     'L3_gnn_bg': (0.0, 0.39)}
    factors = {'L0_gnn_fc_b': 8.0, 'L0_gnn_conv_b': 8.0}
    for name, (base, spread) in spreads.items():
        noise = np.random.default_rng([zlib.crc32(name.encode()), seed]).standard_normal(out[name].shape)
        drawn = base * np.exp(spread * noise) if base else spread * noise
        out[name] = jnp.asarray(drawn.astype(out[name].dtype))
    for name, factor in factors.items():
        out[name] = (out[name] * factor).astype(out[name].dtype)
    return out
```

```python
import concourse.bass as bass
from concourse import mybir
from contextlib import ExitStack

F32 = mybir.dt.float32
BF16 = mybir.dt.bfloat16
I32 = mybir.dt.int32
U32 = mybir.dt.uint32
ALU = mybir.AluOpType
ACT = mybir.ActivationFunctionType
AX = mybir.AxisListType.X

P = 128
D = 128
N = 3125
E = 50000
NB = (N + P - 1) // P
NP = NB * P
TAIL = N - (NB - 1) * P
LANES = 125
COLS = E // LANES
TILES = (E // P + NB + 15) // 16 * 16
G = 8
ITERS = TILES // (2 * G)
REC = 8
R_SRC, R_DST, R_W, R_E = 0, 1, 2, 4
H = 8
AW = D + H
BIG = 1.0e30
EPS = 1e-5
F_MAX = 3.4028234e38

PASSES = ["sum", "sum", "score", "attn", "score", "attn", "sum", "sum"]


def groups_before(k, kinds):
    return sum(2 * ITERS for q in PASSES[:k] if q in kinds)


def steps(eng, n):
    yield 0
    with eng.Fori(1, n, 1) as i:
        yield i


def gnn_kernel(nc, x, src, dst, edge_attr, edge_weight, fc_w, fc_b, conv_w, conv_b, bn_gamma, bn_beta,
               W_node, W_edge, a_vec, Wq, bq, Wk, bk, Wv, bv, Wo, bo, Wt, bt, Wg, bg, out):
    ctx = ExitStack()
    with ctx:
        def sb(name, shape, dt=F32):
            return ctx.enter_context(nc.sbuf_tensor(name, shape, dt))

        def sem(name):
            return ctx.enter_context(nc.semaphore(name))

        rec_dram = nc.dram_tensor("rec_dram", (P * TILES, REC), F32).ap()
        tab_dram = [nc.dram_tensor(f"tab{k}_dram", (N, 4 if k == 2 else D), F32).ap() for k in range(len(PASSES))]

        iota_i = sb("iota_i", [P, 512], I32)
        lane_i = sb("lane_i", [P, 1], I32)
        iota = sb("iota", [P, 512])
        lane = sb("lane", [P, 1])
        ident = sb("ident", [P, P])
        tri = sb("tri", [P, P])
        ones = sb("ones", [P, P])
        X = sb("X", [P, NB, D])
        HN = sb("HN", [P, NB, D])
        FT = sb("FT", [P, NP])
        big = sb("big", [P, 3 * NB * D + NB * 8])
        ZT = big[:, 0:NP]
        HT = big[:, NP:2 * NP]
        TAB = big[:, 2 * NP:2 * NP + NB * AW].rearrange("p (b f) -> p b f", b=NB)
        QKV = big[:, 0:3 * NP].rearrange("p (b f) -> p b f", b=NB)
        ACC = sb("ACC", [P, NB * AW])
        acc3 = ACC[:, :].rearrange("p (b f) -> p b f", b=NB)
        M = sb("M", [P, NB * H])
        m3 = M[:, :].rearrange("p (b h) -> p b h", b=NB)
        stat = sb("stat", [P, 8, NB])
        bnst = sb("bnst", [P, 7, 6])
        bnv = sb("bnv", [P, 8])
        hist = sb("hist", [P, 2, NB])
        dinv_in = sb("dinv_in", [P, NB])
        dinv_out = sb("dinv_out", [P, NB])
        wraw = sb("wraw", [P, 7, D])
        wT = sb("wT", [P, 8, D])
        wfc = sb("wfc", [P, 3, D])
        ust = sb("ust", [P, 8])
        wedge = sb("wedge", [P, 2, 64])
        abd = sb("abd", [P, 12])
        ue2 = sb("ue2", [P, 8])
        cols = sb("cols", [P, 9])
        brow = sb("brow", [1, 6, D])
        wgb = sb("wgb", [P, 2, D])
        bgb = sb("bgb", [P, 2])
        recS = sb("recS", [P, TILES, REC])
        S = sb("S", [P, TILES * H])
        recU = S[:, :].rearrange("p (t r) -> p t r", r=REC)
        key = sb("key", [P, TILES])
        blk_i = sb("blk_i", [P, TILES], I32)
        rec = sb("rec", [LANES, COLS, REC])
        e_dst = sb("e_dst", [LANES, COLS], I32)
        e_src = sb("e_src", [LANES, COLS], I32)
        e_w = sb("e_w", [LANES, COLS])
        e_int = sb("e_int", [LANES, COLS], I32)
        e_blk = ACC[0:LANES, 0 * COLS:1 * COLS]
        e_sblk = ACC[0:LANES, 1 * COLS:2 * COLS]
        e_sloc = ACC[0:LANES, 2 * COLS:3 * COLS]
        e_pos = ACC[0:LANES, 3 * COLS:4 * COLS]
        e_rank = ACC[0:LANES, 4 * COLS:5 * COLS]
        e_row = ACC[0:LANES, 5 * COLS:6 * COLS]
        tot = sb("tot", [LANES, NB])
        base_pos = sb("base_pos", [LANES, NB])
        tcount = sb("tcount", [P, 4, NB])
        tcount_i = sb("tcount_i", [P, NB], I32)
        tblk = sb("tblk", [P, TILES])
        ea = sb("ea", [LANES, 2, 8 * 64])
        eaT = sb("eaT", [P, 2, 4 * LANES])
        stg = sb("stg", [P, 2, G], U32)
        stg_rec = sb("stg_rec", [LANES, 2, G, REC])
        rows = sb("rows", [P, 2, G, D])
        OH = sb("OH", [P, 2, G, P])
        OHT = sb("OHT", [P, G, P])
        msg = sb("msg", [P, G, AW])
        sg16 = sb("sg16", [P, 2 * G, H])
        dl16 = sb("dl16", [P, 2 * G, H])
        dlT = sb("dlT", [P, P])
        edge_of = sb("edge_of", [P, P + 1])
        rst = sb("rst", [P, P])
        fwd = sb("fwd", [P, P])
        runmax = sb("runmax", [P, P])
        ms9 = sb("ms9", [P, 2 * G, H + 1])
        pen = sb("pen", [P, 2 * G])
        mt = sb("mt", [P, 2 * G, H])
        sm = sb("sm", [P, G, H])
        ohlo = OH[0:LANES, :, :, :].rearrange("p a g n -> p (a g n)").bitcast(BF16)
        ohhi = sb("ohhi", [LANES, 2, G, NB], BF16)

        bank = [ctx.enter_context(nc.psum_tensor(f"bank{i}", [P, 512], F32)) for i in range(8)]

        s_iota = sem("s_iota")
        s_load_x = sem("s_load_x")
        s_load_w = sem("s_load_w")
        s_load_e = sem("s_load_e")
        s_consts = sem("s_consts")
        s_abd0 = sem("s_abd0")
        s_tot = sem("s_tot")
        s_pre = sem("s_pre")
        s_rank = sem("s_rank")
        s_masked = sem("s_masked")
        s_placed = sem("s_placed")
        s_recbase = sem("s_recbase")
        s_recinit = sem("s_recinit")
        s_recdef = sem("s_recdef")
        s_uemm = sem("s_uemm")
        s_ue = sem("s_ue")
        s_ea = [sem(f"s_ea{i}") for i in range(2)]
        s_eaT = sem("s_eaT")
        s_eaTc = sem("s_eaTc")
        s_es = sem("s_es")
        s_esc = sem("s_esc")
        s_sstage = sem("s_sstage")
        s_scat = [sem(f"s_scat{i}") for i in range(2)]
        s_hoh = sem("s_hoh")
        s_hmm = sem("s_hmm")
        s_hacc = sem("s_hacc")
        s_recl = sem("s_recl")
        s_dg = sem("s_dg")
        s_keyb = sem("s_keyb")
        s_cmp = sem("s_cmp")
        s_rk = sem("s_rk")
        s_perm = sem("s_perm")
        s_sorted = sem("s_sorted")
        s_recs = sem("s_recs")
        s_pe_chunk = sem("s_pe_chunk")
        s_ev_chunk = sem("s_ev_chunk")
        s_table = sem("s_table")
        s_stored = [sem(f"s_stored{k}") for k in range(len(PASSES))]
        s_stage = sem("s_stage")
        s_gate = sem("s_gate")
        s_rows = [sem(f"s_rows{i}") for i in range(2)]
        s_rowfree = sem("s_rowfree")
        s_oh = sem("s_oh")
        s_ohw = sem("s_ohw")
        s_part = sem("s_part")
        s_acc = sem("s_acc")
        s_tp = sem("s_tp")
        s_oht = sem("s_oht")
        s_got = sem("s_got")
        s_prod = sem("s_prod")
        s_sg = sem("s_sg")
        s_sl = sem("s_sl")
        s_dl = sem("s_dl")
        s_rowT = sem("s_rowT")
        s_dlT = sem("s_dlT")
        s_edge = sem("s_edge")
        s_fwd = sem("s_fwd")
        s_runT = sem("s_runT")
        s_runTT = sem("s_runTT")
        s_ms9 = sem("s_ms9")
        s_mpart = sem("s_mpart")
        s_pen = sem("s_pen")
        s_mt = sem("s_mt")
        s_mx = sem("s_mx")
        s_sm = sem("s_sm")
        s_ex = sem("s_ex")
        s_msg = sem("s_msg")
        s_pass = sem("s_pass")
        s_feat = sem("s_feat")
        s_sq_in = sem("s_sq_in")
        s_sq_out = sem("s_sq_out")
        s_dve = sem("s_dve")
        s_act = sem("s_act")
        s_out = sem("s_out")
        s_scorecopy = sem("s_scorecopy")

        block = ctx.enter_context(nc.Block())

        def bcast(ap, shape):
            return ap.to_broadcast(shape)

        T_CH = [(c, min(4, NB - 4 * c)) for c in range((NB + 3) // 4)]
        L1_CH = [(c, min(3, NB - 3 * c)) for c in range((NB + 2) // 3)]
        STAGES = [("wT", 2), ("T", 7), ("Z", 7), ("T", 7),
                  ("T", 7), ("Z", 7), ("T", 7),
                  ("T", 7), ("Z", 7), ("T", 7),
                  ("T", 7), ("L1", len(L1_CH)),
                  ("T", 7), ("QKV", NB),
                  ("T", 7), ("O", 7),
                  ("T", 7), ("O", 7),
                  ("T", 7), ("O", 7)]
        CH0 = [sum(n for _, n in STAGES[:k]) for k in range(len(STAGES) + 1)]

        @block.sync
        def _(sp):
            sp.dma_start(e_dst[:, :], dst.rearrange("(p c) -> p c", p=LANES)).then_inc(s_load_e, 16)
            sp.dma_start(e_src[:, :], src.rearrange("(p c) -> p c", p=LANES)).then_inc(s_load_e, 16)
            sp.dma_start(e_w[:, :], edge_weight.rearrange("(p c) -> p c", p=LANES)).then_inc(s_load_e, 16)
            for k in range(2):
                sp.dma_start(wedge[:, k, :], W_edge).then_inc(s_load_w, 16)
            sp.wait_ge(s_abd0, 1)
            for part in range(3):
                for h in range(4):
                    sp.dma_start(abd[32 * h:32 * h + 32, 4 * part + h:4 * part + h + 1],
                                 a_vec[h, 32 * part:32 * part + 32].rearrange("(p o) -> p o", o=1)).then_inc(s_load_w, 16)
            for k, w in enumerate([W_node, Wq, Wk, Wv, Wo, Wt[0], Wt[1]]):
                sp.dma_start(wraw[:, k, :], w).then_inc(s_load_w, 16)
            for k, w in enumerate([fc_w, conv_w[0], conv_w[1]]):
                sp.dma_start(wfc[:, k, :], w).then_inc(s_load_w, 16)
            for k, v in enumerate([fc_b, conv_b[0], conv_b[1], bn_gamma[0], bn_gamma[1], bn_gamma[2],
                                   bn_beta[0], bn_beta[1], bn_beta[2]]):
                sp.dma_start(cols[:, k:k + 1], v.rearrange("(p o) -> p o", o=1)).then_inc(s_load_w, 16)
            for k, v in enumerate([bq, bk, bv, bo, bt[0], bt[1]]):
                sp.dma_start(brow[:, k, :], v.rearrange("(o f) -> o f", o=1)).then_inc(s_load_w, 16)
            for k in range(2):
                sp.dma_start(wgb[:, k, :], Wg[k].rearrange("(o f) -> o f", o=1).broadcast_to([P, D])).then_inc(s_load_w, 16)
            sp.dma_start(bgb[:, :], bg.rearrange("(o f) -> o f", o=1).broadcast_to([P, 2])).then_inc(s_load_w, 16)
            sp.wait_ge(s_consts, 1)
            sp.dma_start(X[:, 0:NB - 1, :], x[0:(NB - 1) * P, :].rearrange("(b p) f -> p b f", p=P)).then_inc(s_load_x, 16)
            sp.dma_start(X[0:TAIL, NB - 1, :], x[(NB - 1) * P:N, :]).then_inc(s_load_x, 16)
            sp.wait_ge(s_recdef, 1)
            sp.dma_start(rec_dram.rearrange("(p t) r -> p (t r)", p=P), recS[:, :, :].rearrange("p t r -> p (t r)")).then_inc(s_recinit, 16)
            ea_v = edge_attr.rearrange("(p c) f -> p (c f)", p=LANES)
            for i in steps(sp, COLS // 16):
                for half in range(2):
                    if not isinstance(i, int):
                        sp.wait_ge(s_eaT, 2 * i + half - 1)
                    sp.dma_start(ea[:, half, :], ea_v[:, bass.ds(i * 1024 + half * 512, 512)]).then_inc(s_ea[half], 16)
            for half in range(2):
                sp.wait_ge(s_scat[half], 16 * G * (COLS // 16))
            sp.dma_start(recU.rearrange("p t r -> p (t r)"), rec_dram.rearrange("(p t) r -> p (t r)", p=P)).then_inc(s_recl, 16)
            TABS = {0: TAB[:, :, 0:D], 1: TAB[:, :, 0:D], 2: TAB[:, :, D:D + 4], 3: TAB[:, :, 0:D],
                    4: QKV[:, :, D:2 * D], 5: QKV[:, :, 2 * D:3 * D], 6: TAB[:, :, 0:D], 7: TAB[:, :, 0:D]}
            for k in range(len(PASSES)):
                sp.wait_ge(s_table, k + 1)
                t = TABS[k]
                sp.dma_start(tab_dram[k][0:(NB - 1) * P, :].rearrange("(b p) f -> p b f", p=P), t[:, 0:NB - 1, :]).then_inc(s_stored[k], 16)
                sp.dma_start(tab_dram[k][(NB - 1) * P:N, :], t[0:TAIL, NB - 1, :]).then_inc(s_stored[k], 16)
            sp.wait_ge(s_table, len(PASSES) + 1)
            sp.dma_start(out[0:(NB - 1) * P, :].rearrange("(b p) f -> p b f", p=P), X[:, 0:NB - 1, :]).then_inc(s_out, 16)
            sp.dma_start(out[(NB - 1) * P:N, :], X[0:TAIL, NB - 1, :]).then_inc(s_out, 16)
            sp.wait_ge(s_out, 32)
            for k in range(len(PASSES)):
                sp.wait_ge(s_stored[k], 32)

        @block.gpsimd
        def _(pool):
            nc.gpsimd.iota(iota_i[:, :], pattern=[[1, 512]], base=0, channel_multiplier=0).then_inc(s_iota, 1)
            nc.gpsimd.iota(lane_i[:, :], pattern=[[0, 1]], base=0, channel_multiplier=1).then_inc(s_iota, 1)
            pool.wait_ge(s_recinit, 16)
            for i in steps(pool, COLS // 16):
                for half in range(2):
                    pool.wait_ge(s_sstage, 2 * i + half + 1)
                    pool.sem_inc(s_gate, 1)
                    for j in range(G):
                        nc.gpsimd.indirect_dma_start(
                            rec_dram, bass.IndirectOffsetOnAxis(ap=stg[0:LANES, half, j:j + 1], axis=0),
                            stg_rec[:, half, j, :], None).then_inc(s_scat[half], 16)
            for k in range(len(PASSES)):
                pool.wait_ge(s_stored[k], 32)
                if k == 0:
                    pool.wait_ge(s_recs, 1)
                width = 4 if k == 2 else D
                for i in steps(pool, ITERS):
                    for half in range(2):
                        if k or not isinstance(i, int):
                            pool.wait_ge(s_rowfree, k * 2 * ITERS + 2 * i + half - 1)
                            pool.wait_ge(s_rows[half], 16 * G * (k * ITERS + i))
                            pool.sem_inc(s_gate, 1)
                        nc.gpsimd.tensor_copy(stg[:, half, :], recS[:, bass.ds(G * (2 * i + half), G), R_SRC]).then_inc(s_stage, 1)
                        pool.wait_ge(s_stage, k * 2 * ITERS + 2 * i + half + 1)
                        pool.sem_inc(s_gate, 1)
                        for j in range(G):
                            nc.gpsimd.indirect_dma_start(
                                rows[:, half, j, 0:width], None, tab_dram[k],
                                bass.IndirectOffsetOnAxis(ap=stg[:, half, j:j + 1], axis=0)).then_inc(s_rows[half], 16)

        @block.scalar
        def _(act):
            done = [0]
            chunks = [0]

            def link(ins):
                done[0] += 1
                ins.then_inc(s_act, 1)
                act.wait_ge(s_act, done[0])

            def evac(dst_ap, src_ap, func=ACT.Copy, **kw):
                act.wait_ge(s_pe_chunk, chunks[0] + 1)
                nc.scalar.activation(dst_ap, src_ap, func, **kw).then_inc(s_ev_chunk, 1)
                chunks[0] += 1

            def bank_of():
                return bank[chunks[0] % 2]

            def transposes(to):
                for c, n in T_CH:
                    evac(to(c, n), bank_of()[:, 0:n * P])

            def feat(c, n):
                return FT[:, c * 512:c * 512 + n * P]

            def back(c, n):
                return HN[:, 4 * c:4 * c + n, :].rearrange("p b f -> p (b f)")

            act.wait_ge(s_uemm, 1)
            act.wait_ge(s_consts, 1)
            link(nc.scalar.activation(ue2[0:64, 0:4], bank[7][0:64, 0:4], ACT.Copy))
            link(nc.scalar.activation(ue2[64:128, 4:8], bank[7][64:128, 0:4], ACT.Copy))
            act.sem_inc(s_ue, 1)
            for i in steps(act, COLS // 16):
                for half in range(2):
                    g = 2 * i + half
                    act.wait_ge(s_eaT, g + 1)
                    nc.scalar.activation(eaT[:, half, :], bank[half][:, 0:4 * LANES], ACT.Copy).then_inc(s_eaTc, 1)
                    act.wait_ge(s_es, g + 1)
                    act.sem_inc(s_gate, 1)
                    nc.scalar.activation(rec[:, bass.ds(G * g, G), R_E:R_E + 4],
                                         bank[2 + half][0:LANES, 0:32].rearrange("p (c h) -> p c h", h=4), ACT.Copy).then_inc(s_esc, 1)
            act.wait_ge(s_placed, 1)
            act.wait_ge(s_esc, 2 * (COLS // 16))
            for i in steps(act, COLS // 16):
                for half in range(2):
                    if not isinstance(i, int):
                        act.wait_ge(s_scat[half], 16 * G * i)
                        act.sem_inc(s_gate, 1)
                    nc.scalar.activation(stg_rec[:, half, :, :], rec[:, bass.ds(G * (2 * i + half), G), :], ACT.Copy).then_inc(s_scorecopy, 1)
                    nc.scalar.activation(stg[0:LANES, half, :], e_row[:, bass.ds(G * (2 * i + half), G)], ACT.Copy).then_inc(s_scorecopy, 1)
                    act.wait_ge(s_scorecopy, 2 * (2 * i + half) + 2)
                    act.sem_inc(s_sstage, 1)
            copies0 = 4 * (COLS // 16)
            for i in steps(act, ITERS):
                for half in range(2):
                    g = 2 * i + half
                    act.wait_ge(s_sorted, g + 1)
                    act.sem_inc(s_gate, 1)
                    nc.scalar.activation(recS[:, bass.ds(G * g, G), :],
                                         bank[4 + half][:, 0:G * REC].rearrange("p (t r) -> p t r", r=REC), ACT.Copy).then_inc(s_perm, 1)
            act.wait_ge(s_perm, 2 * ITERS)
            act.sem_inc(s_recs, 1)

            asks = [0]

            def answer(dst_ap, src_ap, func, **kw):
                act.wait_ge(s_sq_in, asks[0] + 1)
                nc.scalar.activation(dst_ap, src_ap, func, **kw).then_inc(s_sq_out, 1)
                asks[0] += 1

            def root():
                answer(stat[:, 3, :], stat[:, 2, :], ACT.Sqrt)

            def oht_copies(k, g):
                b = groups_before(k, ("score", "attn"))
                act.wait_ge(s_tp, b + g + 1)
                if b or not isinstance(g, int) or g > 0:
                    act.wait_ge(s_got, b + g)
                act.sem_inc(s_gate, 1)
                for q in range(2):
                    nc.scalar.activation(OHT[:, 4 * q:4 * q + 4, :].rearrange("p t n -> p (t n)"), bank[q][:, :],
                                         ACT.Copy).then_inc(s_oht, 1)

            def score_pass(k):
                b16 = groups_before(k, ("score",)) // 2
                for i in steps(act, ITERS):
                    for half in range(2):
                        oht_copies(k, 2 * i + half)
                    act.wait_ge(s_sg, 2 * (b16 + i) + 2)
                    act.sem_inc(s_gate, 1)
                    nc.scalar.activation(S[:, bass.ds(2 * G * H * i, 2 * G * H)], sg16[:, :, :].rearrange("p t h -> p (t h)"),
                                         ACT.Copy).then_inc(s_sl, 1)
                    act.wait_ge(s_rowT, b16 + i + 1)
                    nc.scalar.activation(dlT[:, :], bank[3][:, 0:P], ACT.Copy).then_inc(s_dlT, 1)
                    act.wait_ge(s_runTT, b16 + i + 1)
                    nc.scalar.activation(ms9[:, :, 0:H], bank[3][:, 2 * P:3 * P].rearrange("p (t h) -> p t h", h=H),
                                         ACT.Copy).then_inc(s_ms9, 1)

            def attn_pass(k):
                b = groups_before(k, ("attn",))
                for i in steps(act, ITERS):
                    for half in range(2):
                        g = 2 * i + half
                        oht_copies(k, g)
                        act.wait_ge(s_sm, b + g + 1)
                        nc.scalar.activation(msg[:, :, D:AW], sm[:, :, :], ACT.Exp).then_inc(s_ex, 1)

            for c, n in enumerate([4, 3]):
                evac(wT[:, 4 * c:4 * c + n, :].rearrange("p b f -> p (b f)"), bank_of()[:, 0:n * P])
            root(); root()
            root()
            transposes(feat)
            for layer in range(3):
                for c, n in T_CH:
                    evac(ZT[:, c * 512:c * 512 + n * P], bank_of()[:, 0:n * P], ACT.Identity, bias=cols[:, layer:layer + 1])
                answer(bnv[:, 3:4], bnv[:, 2:3], ACT.Sqrt)
                answer(HT if layer == 0 else FT[:, :], ZT, ACT.Relu, scale=bnv[:, 5:6], bias=bnv[:, 6:7])
                transposes(back)
                if layer < 2:
                    transposes(feat)
            root()
            transposes(feat)
            for c, n in L1_CH:
                evac(TAB[:, 3 * c:3 * c + n, :].rearrange("p b f -> p (b f)"), bank_of()[:, 0:n * AW])
            score_pass(2)
            attn_pass(3)
            answer(stat[:, 4:8, :].rearrange("p h b -> p b h"), m3[:, :, 0:4], ACT.Exp, scale=-1.0)
            root()
            transposes(feat)
            for c in range(NB):
                act.wait_ge(s_pe_chunk, chunks[0] + 1)
                link(nc.scalar.activation(QKV[:, c, 0:D], bank_of()[:, 0:D], ACT.Copy, scale=0.25))
                nc.scalar.activation(QKV[:, c, D:3 * D], bank_of()[:, D:3 * D], ACT.Copy).then_inc(s_ev_chunk, 1)
                chunks[0] += 1
            score_pass(4)
            attn_pass(5)
            transposes(feat)
            for c, n in T_CH:
                evac(HN[:, 4 * c:4 * c + n, :].rearrange("p b f -> p (b f)"), bank_of()[:, 0:n * P])
            root()
            for layer in range(2):
                transposes(feat)
                for c, n in T_CH:
                    evac(HN[:, 4 * c:4 * c + n, :].rearrange("p b f -> p (b f)"), bank_of()[:, 0:n * P])
                answer(stat[:, 1, :], stat[:, 0, :], ACT.Tanh, bias=bgb[:, layer:layer + 1])
            assert chunks[0] == CH0[-1]

        @block.tensor
        def _(pe):
            chunks = [0]

            def chunk(fill):
                if chunks[0] >= 2:
                    pe.wait_ge(s_ev_chunk, chunks[0] - 1)
                fill(bank[chunks[0] % 2]).then_inc(s_pe_chunk, 1)
                chunks[0] += 1

            feats = [0]

            def need_feat():
                feats[0] += 1
                pe.wait_ge(s_feat, feats[0])

            def transposes(src_of):
                for c, n in T_CH:
                    def fill(b):
                        for q in range(n):
                            last = nc.tensor.transpose(b[:, q * P:(q + 1) * P], src_of(4 * c + q), ident[:, :])
                        return last
                    chunk(fill)

            def node(b):
                return HN[:, b, :]

            def product_T(w):
                pe.wait_ge(s_ev_chunk, chunks[0])
                for c, n in T_CH:
                    chunk(lambda b: nc.tensor.matmul(b[:, 0:n * P], w, FT[:, c * 512:c * 512 + n * P], start=True, stop=True))

            def fblock(b):
                return FT[:, b * P:(b + 1) * P]

            def product_bias(w, bias):
                pe.wait_ge(s_ev_chunk, chunks[0])
                for c, n in T_CH:
                    def fill(b):
                        for q in range(n):
                            nc.tensor.matmul(b[:, q * P:(q + 1) * P], fblock(4 * c + q), w, start=True, stop=False)
                            last = nc.tensor.matmul(b[:, q * P:(q + 1) * P], ones[0:1, :], bias, start=False, stop=True)
                        return last
                    chunk(fill)

            pe.wait_ge(s_tot, NB)
            pe.wait_ge(s_consts, 1)
            nc.tensor.matmul(bank[6][:, 0:NB], tri[0:LANES, :], tot[:, :], start=True, stop=True)
            nc.tensor.matmul(bank[6][:, 32:32 + NB], ones[0:LANES, :], tot[:, :], start=True, stop=True).then_inc(s_pre, 1)
            pe.wait_ge(s_load_w, 16 * 42)
            nc.tensor.matmul(bank[7][:, 0:4], wedge[:, :, :].rearrange("p a f -> p (a f)"), abd[:, 8:12], start=True, stop=True).then_inc(s_uemm, 1)
            pe.wait_ge(s_ue, 1)
            for i in steps(pe, COLS // 16):
                for half in range(2):
                    g = 2 * i + half
                    pe.wait_ge(s_ea[half], 16 * i + 16)
                    if not isinstance(i, int):
                        pe.wait_ge(s_eaTc, g - 1)
                    for j in range(4):
                        last = nc.tensor.transpose(bank[half][:, j * LANES:(j + 1) * LANES],
                                                   ea[:, half, j * P:(j + 1) * P], ident[0:LANES, 0:LANES])
                    last.then_inc(s_eaT, 1)
                    pe.wait_ge(s_eaTc, g + 1)
                    if not isinstance(i, int):
                        pe.wait_ge(s_esc, g - 1)
                    for j in range(4):
                        last = nc.tensor.matmul(bank[2 + half][0:LANES, 8 * j:8 * j + 8],
                                                eaT[:, half, j * LANES:(j + 1) * LANES], ue2[:, :], start=True, stop=True)
                    last.then_inc(s_es, 1)
            for i in steps(pe, COLS // G // 2):
                for both in range(2):
                    for kind in range(2):
                        pe.wait_ge(s_hoh, 4 * i + 2 * both + kind + 1)
                        if kind == 0 and both + (0 if isinstance(i, int) else 1):
                            pe.wait_ge(s_hacc, 2 * i + both)
                        for j in range(G):
                            last = nc.tensor.matmul(bank[6][:, kind * 32 + 64:kind * 32 + 64 + NB],
                                                    ohlo[:, kind * 1024 + j * P:kind * 1024 + (j + 1) * P],
                                                    ohhi[:, kind, j, :], start=(j == 0), stop=(j == G - 1))
                        last.then_inc(s_hmm, 1)
            for i in steps(pe, ITERS):
                for half in range(2):
                    g = 2 * i + half
                    pe.wait_ge(s_dg, g + 1)
                    for q in range(2):
                        last = nc.tensor.matmul(bank[2 * half + q][:, :], ones[:, :], OHT[:, 4 * q:4 * q + 4, :].rearrange("p t n -> p (t n)"),
                                                start=True, stop=True)
                    last.then_inc(s_keyb, 1)
                    pe.wait_ge(s_rk, g + 1)
                    if not isinstance(i, int):
                        pe.wait_ge(s_perm, g - 1)
                    for j in range(G):
                        last = nc.tensor.matmul(bank[4 + half][:, REC * j:REC * (j + 1)], OH[:, half, j, :],
                                                recU[:, bass.ds(G * g + j, 1), :].rearrange("p t r -> p (t r)"), start=True, stop=True)
                    last.then_inc(s_sorted, 1)

            def onehot_transposes(k, g, half):
                b = groups_before(k, ("score", "attn"))
                pe.wait_ge(s_oh, 2 * ITERS * k + g + 1)
                if b or not isinstance(g, int) or g > 0:
                    pe.wait_ge(s_oht, 2 * (b + g))
                for j in range(G):
                    last = nc.tensor.transpose(bank[j // 4][:, (j % 4) * P:(j % 4 + 1) * P], OH[:, half, j, :], ident[:, :])
                last.then_inc(s_tp, 1)
                pe.wait_ge(s_oht, 2 * (b + g) + 2)

            def block_regs(g):
                _, vals = nc.values_load_multi_w_load_instructions(
                    blk_i[0:1, bass.ds(G * g, G)], engines=[pe.engine], min_val=0, max_val=NB - 1, skip_runtime_bounds_check_because="the table holds min(count of blocks, NB - 1)")
                return vals

            def sum_pass(k):
                b = 2 * ITERS * k
                own = groups_before(k, ("sum",))
                for i in steps(pe, ITERS):
                    for half in range(2):
                        g = 2 * i + half
                        pe.wait_ge(s_ohw, own + g + 1)
                        pe.wait_ge(s_rows[half], 16 * G * (k * ITERS + i + 1))
                        pe.wait_ge(s_rows[half], 16 * G * (k * ITERS + i + 1))
                        for j in range(G):
                            last = nc.tensor.matmul(bank[4 + 2 * half + j // 4][:, (j % 4) * P:(j % 4 + 1) * P], OH[:, half, j, :],
                                                    rows[:, half, j, :], start=True, stop=True)
                        last.then_inc(s_part, 1)

            def score_pass(k):
                b16 = groups_before(k, ("score",)) // 2
                bg_ = groups_before(k, ("score", "attn"))
                for i in steps(pe, ITERS):
                    for half in range(2):
                        g = 2 * i + half
                        vals = block_regs(g)
                        onehot_transposes(k, g, half)
                        pe.wait_ge(s_prod, 2 * b16 + g) if (b16 or not isinstance(i, int) or half) else None
                        for j in range(G):
                            if k == 2:
                                last = nc.tensor.matmul(bank[2][:, 4 * j:4 * j + 4], OHT[:, j, :],
                                                        TAB[:, bass.ds(vals[j], 1), D + 4:D + 8].rearrange("p b f -> p (b f)"), start=True, stop=True)
                            else:
                                last = nc.tensor.matmul(bank[4 + j // 4][:, (j % 4) * P:(j % 4 + 1) * P], OHT[:, j, :],
                                                        QKV[:, bass.ds(vals[j], 1), 0:D].rearrange("p b f -> p (b f)"), start=True, stop=True)
                        last.then_inc(s_got, 1)
                    pe.wait_ge(s_dl, b16 + i + 1)
                    pe.wait_ge(s_sg, 2 * (b16 + i) + 2)
                    nc.tensor.transpose(bank[3][:, 0:P], dl16[:, :, :].rearrange("p t h -> p (t h)"), ident[:, :])
                    nc.tensor.transpose(bank[3][:, P:2 * P], sg16[:, :, :].rearrange("p t h -> p (t h)"), ident[:, :]).then_inc(s_rowT, 1)
                    pe.wait_ge(s_runT, b16 + i + 1)
                    nc.tensor.transpose(bank[3][:, 2 * P:3 * P], runmax[:, :], ident[:, :]).then_inc(s_runTT, 1)
                    pe.wait_ge(s_ms9, b16 + i + 1)
                    for j in range(2 * G):
                        last = nc.tensor.matmul(bank[7][:, 9 * j:9 * j + 9], OH[:, j // G, j % G, :], ms9[:, j, :], start=True, stop=True)
                    last.then_inc(s_mpart, 1)

            def attn_pass(k):
                b = groups_before(k, ("attn",))
                for i in steps(pe, ITERS):
                    for half in range(2):
                        g = 2 * i + half
                        vals = block_regs(g)
                        onehot_transposes(k, g, half)
                        if b or not isinstance(i, int) or half:
                            pe.wait_ge(s_sm, b + g)
                        for j in range(G):
                            last = nc.tensor.matmul(bank[2][:, H * j:H * j + H], OHT[:, j, :],
                                                    M[:, bass.ds(vals[j] * H, H)], start=True, stop=True)
                        last.then_inc(s_got, 1)
                        pe.wait_ge(s_msg, b + g + 1)
                        for j in range(G):
                            last = nc.tensor.matmul(bank[4 + j // 3][:, (j % 3) * AW:(j % 3 + 1) * AW], OH[:, half, j, :],
                                                    msg[:, j, :], start=True, stop=True)
                        last.then_inc(s_part, 1)

            pe.wait_ge(s_consts, 1)
            for c, n in enumerate([4, 3]):
                def fill(b):
                    for q in range(n):
                        last = nc.tensor.transpose(b[:, q * P:(q + 1) * P], wraw[:, 4 * c + q, :], ident[:, :])
                    return last
                chunk(fill)
            nc.tensor.matmul(bank[7][:, 8:16], wraw[:, 0, :], abd[:, 0:8], start=True, stop=True).then_inc(s_uemm, 1)
            need_feat()
            transposes(node)
            for layer in range(3):
                product_T(wfc[:, layer, :])
                need_feat()
                transposes(lambda b: HT[:, b * P:(b + 1) * P])
                if layer < 2:
                    sum_pass(layer)
                    need_feat()
                    transposes(node)
            need_feat()
            transposes(node)
            pe.wait_ge(s_ev_chunk, chunks[0])
            for c, n in L1_CH:
                def fill(b):
                    for q in range(n):
                        nc.tensor.matmul(b[:, q * AW:q * AW + D], fblock(3 * c + q), wT[:, 0, :], start=True, stop=True)
                        last = nc.tensor.matmul(b[:, q * AW + D:(q + 1) * AW], fblock(3 * c + q), ust[:, :], start=True, stop=True)
                    return last
                chunk(fill)
            pe.wait_ge(s_ev_chunk, chunks[0])
            score_pass(2)
            need_feat()
            attn_pass(3)
            need_feat()
            transposes(node)
            pe.wait_ge(s_ev_chunk, chunks[0])
            for c in range(NB):
                def fill(b):
                    nc.tensor.matmul(b[:, 0:3 * D], fblock(c), wT[:, 1:4, :].rearrange("p a f -> p (a f)"), start=True, stop=False)
                    return nc.tensor.matmul(b[:, 0:3 * D], ones[0:1, :], brow[:, 0:3, :].rearrange("p a f -> p (a f)"), start=False, stop=True)
                chunk(fill)
            pe.wait_ge(s_ev_chunk, chunks[0])
            score_pass(4)
            need_feat()
            attn_pass(5)
            need_feat()
            transposes(node)
            product_bias(wT[:, 4, :], brow[:, 3, :])
            for layer in range(2):
                need_feat()
                transposes(node)
                product_bias(wT[:, 5 + layer, :], brow[:, 4 + layer, :])
                sum_pass(6 + layer)
            assert chunks[0] == CH0[-1]

        @block.vector
        def _(dve):
            done = [0]
            asked = [0]
            v = nc.vector

            def link(ins):
                done[0] += 1
                ins.then_inc(s_dve, 1)
                dve.wait_ge(s_dve, done[0])

            def ask():
                dve.sem_inc(s_sq_in, 1)
                asked[0] += 1
                dve.wait_ge(s_sq_out, asked[0])

            link(v.memset(abd[:, :], 0.0))
            dve.sem_inc(s_abd0, 1)
            dve.wait_ge(s_iota, 2)
            link(v.tensor_copy(iota[:, :], iota_i[:, :]))
            link(v.tensor_copy(lane[:, :], lane_i[:, :]))
            link(v.tensor_scalar(ident[:, :], iota[:, 0:P], lane[:, 0:1], None, ALU.is_equal))
            link(v.tensor_scalar(tri[:, :], iota[:, 0:P], lane[:, 0:1], None, ALU.is_gt))
            link(v.memset(ones[:, :], 1.0))
            link(v.memset(ue2[:, :], 0.0))
            link(v.memset(X[:, NB - 1, :], 0.0))
            link(v.memset(edge_of[:, :], 1.0))
            link(v.memset(ms9[:, :, H:H + 1], 1.0))
            link(v.memset(sg16[:, :, :], 0.0))
            link(v.memset(hist[:, :, :], 0.0))
            dve.sem_inc(s_consts, 1)
            link(v.memset(recS[:, :, :], 0.0))
            link(v.memset(recS[:, :, R_DST], float(P)))
            dve.sem_inc(s_recdef, 1)

            dve.wait_ge(s_load_e, 48)
            link(v.memset(rec[:, :, :], 0.0))
            for ends, blk, loc in ((e_dst, e_blk[:, :], rec[:, :, R_DST]), (e_src, e_sblk[:, :], e_sloc[:, :])):
                link(v.tensor_single_scalar(e_int[:, :], ends[:, :], 7, ALU.arith_shift_right))
                link(v.tensor_copy(blk, e_int[:, :]))
                link(v.tensor_copy(e_rank[:, :], ends[:, :]))
                link(v.scalar_tensor_tensor(loc, blk, -float(P), e_rank[:, :], ALU.mult, ALU.add))
            link(v.tensor_copy(rec[:, :, R_SRC], e_rank[:, :]))
            link(v.tensor_scalar(e_rank[:, :], e_w[:, :], F_MAX, None, ALU.is_le))
            link(v.scalar_tensor_tensor(e_int[:, :], e_w[:, :], -F_MAX, e_rank[:, :], ALU.is_ge, ALU.mult))
            link(v.copy_predicated(rec[:, :, R_W], e_int[:, :], e_w[:, :]))
            with dve.Fori(0, NB, 1) as b:
                v.tensor_scalar(e_rank[:, :], e_blk[:, :], iota[0:LANES, bass.ds(b, 1)], 0.0, ALU.is_equal, ALU.add,
                                accum_out=tot[:, bass.ds(b, 1)]).then_inc(s_tot, 1)
                dve.wait_ge(s_tot, b + 1)
            dve.wait_ge(s_pre, 1)
            link(v.tensor_scalar(tcount_i[:, :], bank[6][:, 32:32 + NB], float(P - 1), None, ALU.add))
            link(v.tensor_single_scalar(tcount_i[:, :], tcount_i[:, :], 7, ALU.arith_shift_right))
            link(v.tensor_copy(tcount[:, 0, :], tcount_i[:, :]))
            link(v.memset(tcount[:, 3, :], 0.0))
            link(v.tensor_tensor_scan(tcount[:, 1, :], tcount[:, 3, :], tcount[:, 0, :], 0.0, ALU.add, ALU.add))
            link(v.tensor_tensor(tcount[:, 2, :], tcount[:, 1, :], tcount[:, 0, :], ALU.subtract))
            link(v.tensor_scalar(tcount[:, 2, :], tcount[:, 2, :], float(P), -1.0, ALU.mult, ALU.add))
            link(v.tensor_tensor(base_pos[:, :], bank[6][0:LANES, 0:NB], tcount[0:LANES, 2, :], ALU.add))
            link(v.memset(e_pos[:, :], 0.0))
            link(v.memset(e_w[:, :], 0.0))
            with dve.Fori(0, NB, 1) as b:
                v.tensor_scalar(e_int[:, :], e_blk[:, :], iota[0:LANES, bass.ds(b, 1)], None, ALU.is_equal).then_inc(s_rank, 1)
                dve.wait_ge(s_rank, b * 3 + 1)
                v.tensor_tensor_scan(e_rank[:, :], e_w[:, :], e_int[:, :], base_pos[:, bass.ds(b, 1)], ALU.add, ALU.add).then_inc(s_rank, 1)
                dve.wait_ge(s_rank, b * 3 + 2)
                dve.sem_inc(s_gate, 1)
                v.copy_predicated(e_pos[:, :], e_int[:, :], e_rank[:, :]).then_inc(s_rank, 1)
                dve.wait_ge(s_rank, b * 3 + 3)
            link(v.tensor_copy(e_int[:, :], e_pos[:, :]))
            link(v.tensor_single_scalar(e_int[:, :], e_int[:, :], 7, ALU.arith_shift_right))
            link(v.tensor_copy(e_rank[:, :], e_int[:, :]))
            link(v.scalar_tensor_tensor(e_pos[:, :], e_rank[:, :], -float(P), e_pos[:, :], ALU.mult, ALU.add))
            link(v.scalar_tensor_tensor(e_row[:, :], e_pos[:, :], float(TILES), e_rank[:, :], ALU.mult, ALU.add))
            dve.sem_inc(s_placed, 1)
            link(v.memset(tblk[:, :], 0.0))
            with dve.Fori(0, NB, 1) as b:
                v.scalar_tensor_tensor(tblk[:, :], iota[:, 0:TILES], tcount[:, 1, bass.ds(b, 1)], tblk[:, :],
                                       ALU.is_ge, ALU.add).then_inc(s_masked, 1)
                dve.wait_ge(s_masked, b + 1)
            link(v.tensor_scalar(tblk[:, :], tblk[:, :], float(NB - 1), None, ALU.min))
            link(v.tensor_copy(blk_i[:, :], tblk[:, :]))

            for i in steps(dve, COLS // G // 2):
                for both in range(2):
                    g = 2 * i + both
                    for kind, (blk, loc) in enumerate(((e_blk[:, :], rec[:, :, R_DST]), (e_sblk[:, :], e_sloc[:, :]))):
                        if both + (0 if isinstance(i, int) else 1):
                            dve.wait_ge(s_hmm, 2 * g - 1 + kind)
                        v.tensor_tensor(ohlo[:, kind * 1024:(kind + 1) * 1024].rearrange("p (g n) -> p g n", g=G),
                                        iota[0:LANES, 0:P].unsqueeze(1).to_broadcast([LANES, G, P]),
                                        loc[:, bass.ds(G * g, G)].unsqueeze(2).to_broadcast([LANES, G, P]), ALU.is_equal).then_inc(s_rank, 1)
                        v.tensor_tensor(ohhi[:, kind, :, :],
                                        iota[0:LANES, 0:NB].unsqueeze(1).to_broadcast([LANES, G, NB]),
                                        blk[:, bass.ds(G * g, G)].unsqueeze(2).to_broadcast([LANES, G, NB]), ALU.is_equal).then_inc(s_rank, 1)
                        dve.wait_ge(s_rank, 3 * NB + 4 * g + 2 * kind + 2)
                        dve.sem_inc(s_hoh, 1)
                    dve.wait_ge(s_hmm, 2 * g + 2)
                    v.tensor_tensor(hist[:, :, :], hist[:, :, :],
                                    bank[6][:, 64:128].rearrange("p (k b) -> p k b", k=2)[:, :, 0:NB], ALU.add).then_inc(s_hacc, 1)
                    dve.wait_ge(s_hacc, g + 1)

            dve.wait_ge(s_recl, 16)
            link(v.tensor_scalar(key[:, :], recU[:, :, R_DST], float(P), lane[:, 0:1], ALU.mult, ALU.add))
            for i in steps(dve, ITERS):
                for half in range(2):
                    g = 2 * i + half
                    kg = key[:, bass.ds(G * g, G)].unsqueeze(2).to_broadcast([P, G, P])
                    if half + (0 if isinstance(i, int) else 1):
                        dve.wait_ge(s_keyb, g)
                    v.tensor_tensor(OHT[:, :, :], ident[:, :].unsqueeze(1).to_broadcast([P, G, P]), kg, ALU.mult).then_inc(s_dg, 1)
                    dve.wait_ge(s_keyb, g + 1)
                    if not isinstance(i, int):
                        dve.wait_ge(s_sorted, g - 1)
                    for q in range(2):
                        v.tensor_tensor(OH[:, half, 4 * q:4 * q + 4, :], bank[2 * half + q][:, :].rearrange("p (g n) -> p g n", g=4),
                                        key[:, bass.ds(G * g + 4 * q, 4)].unsqueeze(2).to_broadcast([P, 4, P]), ALU.is_lt).then_inc(s_cmp, 1)
                    dve.wait_ge(s_cmp, 3 * g + 2)
                    v.tensor_reduce(pen[:, half * G:(half + 1) * G], OH[:, half, :, :], AX, ALU.add).then_inc(s_cmp, 1)
                    dve.wait_ge(s_cmp, 3 * g + 3)
                    v.tensor_tensor(OH[:, half, :, :], iota[:, 0:P].unsqueeze(1).to_broadcast([P, G, P]),
                                    pen[:, half * G:(half + 1) * G].unsqueeze(2).to_broadcast([P, G, P]), ALU.is_equal).then_inc(s_rk, 1)

            link(v.tensor_scalar(stat[:, 2, :], hist[:, 0, :], 1.0, None, ALU.max))
            ask()
            link(v.reciprocal(stat[:, 0, :], stat[:, 3, :]))
            link(v.tensor_scalar(stat[:, 1, :], hist[:, 0, :], 0.0, None, ALU.is_gt))
            link(v.tensor_tensor(dinv_in[:, :], stat[:, 0, :], stat[:, 1, :], ALU.mult))
            link(v.tensor_scalar(stat[:, 2, :], hist[:, 1, :], 1.0, None, ALU.max))
            ask()
            link(v.reciprocal(dinv_out[:, :], stat[:, 3, :]))

            def per_node(s):
                return s.unsqueeze(2).to_broadcast([P, NB, D])

            ft3 = FT[:, :].rearrange("p (b f) -> p b f", b=NB)

            def layernorm():
                link(v.tensor_reduce(stat[:, 0, :], X[:, :, :], AX, ALU.add))
                link(v.tensor_scalar(stat[:, 0, :], stat[:, 0, :], 1.0 / D, None, ALU.mult))
                link(v.tensor_tensor(HN[:, :, :], X[:, :, :], per_node(stat[:, 0, :]), ALU.subtract))
                link(v.tensor_tensor(ft3, HN[:, :, :], HN[:, :, :], ALU.mult))
                link(v.tensor_reduce(stat[:, 1, :], ft3, AX, ALU.add))
                link(v.tensor_scalar(stat[:, 2, :], stat[:, 1, :], 1.0 / D, EPS, ALU.mult, ALU.add))
                ask()
                link(v.reciprocal(stat[:, 4, :], stat[:, 3, :]))
                link(v.tensor_tensor(HN[:, :, :], HN[:, :, :], per_node(stat[:, 4, :]), ALU.mult))
                link(v.tensor_scalar(HN[:, :, :], HN[:, :, :], 0.0, None, ALU.max))
                dve.sem_inc(s_feat, 1)

            def onehots(k, g, half):
                v.tensor_tensor(OH[:, half, :, :], iota[:, 0:P].unsqueeze(1).to_broadcast([P, G, P]),
                                recS[:, bass.ds(G * g, G), R_DST].unsqueeze(2).to_broadcast([P, G, P]),
                                ALU.is_equal).then_inc(s_oh, 1)

            def block_regs(g):
                _, vals = nc.values_load_multi_w_load_instructions(
                    blk_i[0:1, bass.ds(G * g, G)], engines=[dve.engine], min_val=0, max_val=NB - 1, skip_runtime_bounds_check_because="the table holds min(count of blocks, NB - 1)")
                return vals

            parts_sum = [0]

            def sum_pass(k, weighted):
                own = groups_before(k, ("sum",))
                parts = groups_before(k, ("sum", "attn"))
                link(v.memset(ACC[:, :], 0.0))
                for i in steps(dve, ITERS):
                    for half in range(2):
                        g = 2 * i + half
                        vals = block_regs(g)
                        onehots(k, g, half)
                        dve.wait_ge(s_oh, 2 * ITERS * k + g + 1)
                        if weighted:
                            v.tensor_tensor(OH[:, half, :, :], OH[:, half, :, :],
                                            recS[:, bass.ds(G * g, G), R_W].unsqueeze(2).to_broadcast([P, G, P]),
                                            ALU.mult).then_inc(s_ohw, 1)
                        else:
                            dve.sem_inc(s_ohw, 1)
                        dve.wait_ge(s_part, parts + g + 1)
                        dve.sem_inc(s_rowfree, 1)
                        for j in range(G):
                            acc = ACC[:, bass.ds(vals[j] * AW, D)]
                            v.tensor_tensor(acc, acc, bank[4 + 2 * half + j // 4][:, (j % 4) * P:(j % 4 + 1) * P], ALU.add).then_inc(s_acc, 1)
                            dve.wait_ge(s_acc, G * (parts + g) + j + 1)

            def score_pass(k):
                b16 = groups_before(k, ("score",)) // 2
                bg_ = groups_before(k, ("score", "attn"))
                link(v.memset(M[:, :], 0.0 if k == 2 else -BIG))
                for i in steps(dve, ITERS):
                    for half in range(2):
                        g = 2 * i + half
                        onehots(k, g, half)
                        r = rows[:, half, :, :]
                        dve.wait_ge(s_got, bg_ + g + 1)
                        dve.wait_ge(s_rows[half], 16 * G * (k * ITERS + i + 1))
                        if half == 0 and (b16 or not isinstance(i, int)):
                            dve.wait_ge(s_sl, b16 + i)
                        if k == 2:
                            v.tensor_tensor(sm[:, :, 0:4], bank[2][:, 0:32].rearrange("p (t h) -> p t h", h=4), r[:, :, 0:4], ALU.add).then_inc(s_prod, 1)
                            dve.sem_inc(s_rowfree, 1) if False else None
                            dve.wait_ge(s_prod, 2 * b16 + g + 1)
                            dve.sem_inc(s_rowfree, 1)
                            v.tensor_tensor(sm[:, :, 4:8], sm[:, :, 0:4], recS[:, bass.ds(G * g, G), R_E:R_E + 4], ALU.add).then_inc(s_edge, 1)
                            dve.wait_ge(s_edge, g + 1)
                            v.scalar_tensor_tensor(sg16[:, half * G:half * G + G, 0:4], sm[:, :, 4:8], 0.2, sm[:, :, 4:8],
                                                   ALU.mult, ALU.max).then_inc(s_sg, 1)
                        else:
                            for q in range(2):
                                v.tensor_tensor(msg[:, 4 * q:4 * q + 4, 0:D], bank[4 + q][:, :].rearrange("p (t f) -> p t f", t=4),
                                                r[:, 4 * q:4 * q + 4, :], ALU.mult).then_inc(s_cmp, 1)
                            dve.wait_ge(s_cmp, 6 * ITERS + 2 * g + 2)
                            dve.sem_inc(s_prod, 1)
                            dve.sem_inc(s_rowfree, 1)
                            v.tensor_reduce(sg16[:, half * G:half * G + G, :],
                                            msg[:, :, 0:D].rearrange("p t (h d) -> p t h d", h=H), AX, ALU.add).then_inc(s_sg, 1)
                    n = b16 + i
                    v.tensor_copy(dl16[:, :, :], recS[:, bass.ds(2 * G * i, 2 * G), R_DST].unsqueeze(2).to_broadcast([P, 2 * G, H])).then_inc(s_dl, 1)
                    dve.wait_ge(s_dlT, n + 1)
                    v.tensor_tensor(edge_of[:, 1:P], dlT[:, 1:P], dlT[:, 0:P - 1], ALU.not_equal).then_inc(s_fwd, 1)
                    dve.wait_ge(s_fwd, 3 * n + 1)
                    v.tensor_scalar(rst[:, :], edge_of[:, 0:P], -BIG, None, ALU.mult).then_inc(s_fwd, 1)
                    dve.wait_ge(s_fwd, 3 * n + 2)
                    v.tensor_tensor_scan(fwd[:, :], rst[:, :], bank[3][:, P:2 * P], 0.0, ALU.add, ALU.max).then_inc(s_fwd, 1)
                    dve.wait_ge(s_fwd, 3 * n + 3)
                    v.tensor_tensor(runmax[:, :], fwd[:, :], edge_of[:, 1:P + 1], ALU.mult).then_inc(s_runT, 1)
                    dve.wait_ge(s_mpart, n + 1)
                    mp = bank[7][:, 0:2 * G * 9].rearrange("p (t h) -> p t h", h=9)
                    v.tensor_scalar(pen[:, :], mp[:, :, H], 1.0, -1.0, ALU.min, ALU.add).then_inc(s_pen, 1)
                    dve.wait_ge(s_pen, n + 1)
                    v.scalar_tensor_tensor(mt[:, :, :], pen[:, :].unsqueeze(2).to_broadcast([P, 2 * G, H]), BIG, mp[:, :, 0:H],
                                           ALU.mult, ALU.add).then_inc(s_mt, 1)
                    dve.wait_ge(s_mt, n + 1)
                    for half in range(2):
                        vals = block_regs(2 * i + half)
                        for j in range(G):
                            mb = M[:, bass.ds(vals[j] * H, H)]
                            v.tensor_tensor(mb, mb, mt[:, half * G + j, :], ALU.max).then_inc(s_mx, 1)
                            dve.wait_ge(s_mx, 2 * G * n + half * G + j + 1)
                dve.sem_inc(s_feat, 1)

            def attn_pass(k):
                b = groups_before(k, ("attn",))
                bg_ = groups_before(k, ("score", "attn"))
                parts = groups_before(k, ("sum", "attn"))
                heads = 4 if k == 3 else 8
                link(v.memset(ACC[:, :], 0.0))
                for i in steps(dve, ITERS):
                    for half in range(2):
                        g = 2 * i + half
                        vals = block_regs(g)
                        onehots(k, g, half)
                        dve.wait_ge(s_got, bg_ + g + 1)
                        v.tensor_tensor(sm[:, :, :], S[:, bass.ds(G * H * g, G * H)].rearrange("p (t h) -> p t h", h=H),
                                        bank[2][:, 0:G * H].rearrange("p (t h) -> p t h", h=H), ALU.subtract).then_inc(s_edge, 1)
                        dve.wait_ge(s_edge, 2 * ITERS + b + g + 1)
                        v.tensor_scalar(sm[:, :, :], sm[:, :, :], 60.0, None, ALU.min).then_inc(s_sm, 1)
                        dve.wait_ge(s_ex, b + g + 1)
                        dve.wait_ge(s_rows[half], 16 * G * (k * ITERS + i + 1))
                        dve.sem_inc(s_gate, 1)
                        w = D // heads
                        v.tensor_tensor(msg[:, :, 0:D].rearrange("p t (h d) -> p t h d", h=heads),
                                        rows[:, half, :, :].rearrange("p t (h d) -> p t h d", h=heads),
                                        msg[:, :, D:D + heads].unsqueeze(3).to_broadcast([P, G, heads, w]), ALU.mult).then_inc(s_msg, 1)
                        dve.wait_ge(s_part, parts + g + 1)
                        dve.sem_inc(s_rowfree, 1)
                        for j in range(G):
                            acc = ACC[:, bass.ds(vals[j] * AW, AW)]
                            v.tensor_tensor(acc, acc, bank[4 + j // 3][:, (j % 3) * AW:(j % 3 + 1) * AW], ALU.add).then_inc(s_acc, 1)
                            dve.wait_ge(s_acc, G * (parts + g) + j + 1)

            dve.wait_ge(s_load_x, 32)
            dve.wait_ge(s_load_w, 16 * 42)
            dve.wait_ge(s_uemm, 2)
            link(v.tensor_copy(ust[:, :], bank[7][:, 8:16]))
            layernorm()
            ev = lambda stage: dve.wait_ge(s_ev_chunk, CH0[stage + 1])
            for layer in range(3):
                ev(2 + 3 * layer)
                for c in range(7):
                    link(v.bn_stats(bnst[:, c, :], ZT[:, c * 512:min(N, c * 512 + 512)]))
                link(v.bn_aggr(bnv[:, 0:2], bnst[:, :, :].rearrange("p a b -> p (a b)")))
                link(v.tensor_scalar(bnv[:, 2:3], bnv[:, 1:2], EPS, None, ALU.add))
                ask()
                link(v.reciprocal(bnv[:, 4:5], bnv[:, 3:4]))
                link(v.tensor_tensor(bnv[:, 5:6], bnv[:, 4:5], cols[:, 3 + layer:4 + layer], ALU.mult))
                link(v.tensor_tensor(bnv[:, 7:8], bnv[:, 0:1], bnv[:, 5:6], ALU.mult))
                link(v.tensor_tensor(bnv[:, 6:7], cols[:, 6 + layer:7 + layer], bnv[:, 7:8], ALU.subtract))
                ask()
                if layer:
                    link(v.tensor_tensor(HT, HT, FT[:, :], ALU.add))
                dve.sem_inc(s_feat, 1)
                ev(3 + 3 * layer)
                if layer < 2:
                    link(v.tensor_tensor(TAB[:, :, 0:D], HN[:, :, :], per_node(dinv_in[:, :]), ALU.mult))
                    dve.sem_inc(s_table, 1)
                    sum_pass(layer, True)
                    link(v.tensor_tensor(HN[:, :, :], acc3[:, :, 0:D], per_node(dinv_in[:, :]), ALU.mult))
                    dve.sem_inc(s_feat, 1)
            link(v.tensor_tensor(X[:, :, :], X[:, :, :], HN[:, :, :], ALU.add))
            layernorm()
            ev(11)
            dve.sem_inc(s_table, 1)
            dve.sem_inc(s_table, 1)
            score_pass(2)
            attn_pass(3)
            ask()
            link(v.tensor_scalar(stat[:, 0, :], hist[:, 0, :], -1.0, float(E), ALU.mult, ALU.add))
            link(v.tensor_tensor(stat[:, 4:8, :], stat[:, 4:8, :], stat[:, 0, :].unsqueeze(1).to_broadcast([P, 4, NB]), ALU.mult))
            den = acc3[:, :, D:D + 4]
            link(v.tensor_tensor(den, den, stat[:, 4:8, :].rearrange("p h b -> p b h"), ALU.add))
            link(v.reciprocal(den, den))
            for h in range(4):
                link(v.tensor_tensor(HN[:, :, 32 * h:32 * h + 32], acc3[:, :, 32 * h:32 * h + 32],
                                     acc3[:, :, D + h:D + h + 1].to_broadcast([P, NB, 32]), ALU.mult))
            link(v.tensor_tensor(X[:, :, :], X[:, :, :], HN[:, :, :], ALU.add))
            layernorm()
            ev(13)
            dve.sem_inc(s_table, 1)
            dve.sem_inc(s_table, 1)
            score_pass(4)
            attn_pass(5)
            den = acc3[:, :, D:AW]
            link(v.tensor_scalar(den, den, 1.0e-30, None, ALU.max))
            link(v.reciprocal(den, den))
            for h in range(8):
                link(v.tensor_tensor(HN[:, :, 16 * h:16 * h + 16], acc3[:, :, 16 * h:16 * h + 16],
                                     acc3[:, :, D + h:D + h + 1].to_broadcast([P, NB, 16]), ALU.mult))
            dve.sem_inc(s_feat, 1)
            ev(15)
            link(v.tensor_tensor(X[:, :, :], X[:, :, :], HN[:, :, :], ALU.add))
            layernorm()
            for layer in range(2):
                ev(17 + 2 * layer)
                link(v.tensor_tensor(ft3, HN[:, :, :], wgb[:, layer:layer + 1, :].to_broadcast([P, NB, D]), ALU.mult))
                link(v.tensor_reduce(stat[:, 0, :], ft3, AX, ALU.add))
                ask()
                link(v.tensor_tensor(stat[:, 1, :], stat[:, 1, :], dinv_out[:, :], ALU.mult))
                link(v.tensor_tensor(TAB[:, :, 0:D], HN[:, :, :], per_node(stat[:, 1, :]), ALU.mult))
                dve.sem_inc(s_table, 1)
                sum_pass(6 + layer, False)
                link(v.tensor_tensor(ft3, acc3[:, :, 0:D], per_node(dinv_out[:, :]), ALU.mult))
                link(v.tensor_tensor(HN[:, :, :], HN[:, :, :], ft3, ALU.add))
                link(v.tensor_scalar(HN[:, :, :], HN[:, :, :], 0.0, None, ALU.max))
                dve.sem_inc(s_feat, 1)
            link(v.tensor_tensor(X[:, :, :], X[:, :, :], HN[:, :, :], ALU.add))
            dve.sem_inc(s_table, 1)


_INS = ['x', 'src', 'dst', 'edge_attr_64', 'edge_weight', 'L0_gnn_fc_w', 'L0_gnn_fc_b', 'L0_gnn_conv_w', 'L0_gnn_conv_b',
        'L0_gnn_bn_gamma', 'L0_gnn_bn_beta', 'L1_gnn_W_node', 'L1_gnn_W_edge', 'L1_gnn_a', 'L2_gnn_Wq', 'L2_gnn_bq',
        'L2_gnn_Wk', 'L2_gnn_bk', 'L2_gnn_Wv', 'L2_gnn_bv', 'L2_gnn_Wo', 'L2_gnn_bo', 'L3_gnn_Wt', 'L3_gnn_bt',
        'L3_gnn_Wg', 'L3_gnn_bg']


def kernel(**inputs):
    import numpy as _np
    import concourse.bacc as _bacc
    from concourse import mybir as _mybir
    from concourse.bass_utils import run_bass_kernel_spmd as _run

    nc = _bacc.Bacc("TRN2", target_bir_lowering=False, num_devices=1)
    arrays, args = {}, []
    for name in _INS:
        a = _np.ascontiguousarray(inputs[name])
        arrays[f"in_{name}_dram"] = a
        args.append(nc.dram_tensor(f"in_{name}_dram", a.shape, _mybir.dt.from_np(a.dtype), kind="ExternalInput").ap())
    args.append(nc.dram_tensor("out_dram", (N, D), _mybir.dt.float32, kind="ExternalOutput").ap())
    gnn_kernel(nc, *args)
    r = _run(nc, [arrays], core_ids=[0])
    return r.results[0]["out_dram"]
```

```python
import concourse.bass as bass
from concourse import mybir
from contextlib import ExitStack

F32 = mybir.dt.float32
BF16 = mybir.dt.bfloat16
I32 = mybir.dt.int32
U32 = mybir.dt.uint32
ALU = mybir.AluOpType
ACT = mybir.ActivationFunctionType
AX = mybir.AxisListType.X

P = 128
D = 128
N = 3125
E = 50000
NB = (N + P - 1) // P
NP = NB * P
TAIL = N - (NB - 1) * P
LANES = 125
COLS = E // LANES
TILES = (E // P + NB + 15) // 16 * 16
G = 8
PAIRS = TILES // (2 * G)
GROUPS = TILES // G
RING = 4
ITERS = GROUPS // RING
REC = 8
R_SRC, R_DST, R_W, R_E = 0, 1, 2, 4
H = 8
AW = D + H
BIG = 1.0e30
EPS = 1e-5
F_MAX = 3.4028234e38

PASSES = ["sum", "sum", "score", "attn", "score", "attn", "sum", "sum"]


def groups_before(k, kinds):
    return sum(GROUPS for q in PASSES[:k] if q in kinds)


def steps(eng, n):
    yield 0
    with eng.Fori(1, n, 1) as i:
        yield i


def rounds(eng, n):
    yield 0
    with eng.Fori(1, n - 1, 1) as i:
        yield i
    yield n - 1


def there(g, before=GROUPS):
    return not isinstance(g, int) or 0 <= g < before


def gnn_kernel(nc, x, src, dst, edge_attr, edge_weight, fc_w, fc_b, conv_w, conv_b, bn_gamma, bn_beta,
               W_node, W_edge, a_vec, Wq, bq, Wk, bk, Wv, bv, Wo, bo, Wt, bt, Wg, bg, out):
    ctx = ExitStack()
    with ctx:
        def sb(name, shape, dt=F32):
            return ctx.enter_context(nc.sbuf_tensor(name, shape, dt))

        def sem(name):
            return ctx.enter_context(nc.semaphore(name))

        rec_dram = nc.dram_tensor("rec_dram", (P * TILES, REC), F32).ap()
        tab_dram = [nc.dram_tensor(f"tab{k}_dram", (N, 4 if k == 2 else D), F32).ap() for k in range(len(PASSES))]

        iota_i = sb("iota_i", [P, 512], I32)
        lane_i = sb("lane_i", [P, 1], I32)
        iota = sb("iota", [P, 512])
        lane = sb("lane", [P, 1])
        ident = sb("ident", [P, P])
        tri = sb("tri", [P, P])
        ones = sb("ones", [P, P])
        X = sb("X", [P, NB, D])
        HN = sb("HN", [P, NB, D])
        FT = sb("FT", [P, NP])
        big = sb("big", [P, 3 * NB * D + NB * 8])
        ZT = big[:, 0:NP]
        HT = big[:, NP:2 * NP]
        TAB = big[:, 2 * NP:2 * NP + NB * AW].rearrange("p (b f) -> p b f", b=NB)
        QKV = big[:, 0:3 * NP].rearrange("p (b f) -> p b f", b=NB)
        ACC = sb("ACC", [P, NB * AW])
        acc3 = ACC[:, :].rearrange("p (b f) -> p b f", b=NB)
        M = sb("M", [P, NB * H])
        m3 = M[:, :].rearrange("p (b h) -> p b h", b=NB)
        stat = sb("stat", [P, 8, NB])
        bnst = sb("bnst", [P, 7, 6])
        bnv = sb("bnv", [P, 8])
        hist = sb("hist", [P, 2, NB])
        dinv_in = sb("dinv_in", [P, NB])
        dinv_out = sb("dinv_out", [P, NB])
        wraw = sb("wraw", [P, 7, D])
        wT = sb("wT", [P, 8, D])
        wfc = sb("wfc", [P, 3, D])
        ust = sb("ust", [P, 8])
        wedge = sb("wedge", [P, 2, 64])
        abd = sb("abd", [P, 12])
        ue2 = sb("ue2", [P, 8])
        cols = sb("cols", [P, 9])
        brow = sb("brow", [1, 6, D])
        wgb = sb("wgb", [P, 2, D])
        bgb = sb("bgb", [P, 2])
        recS = sb("recS", [P, TILES, REC])
        S = sb("S", [P, TILES * H])
        recU = S[:, :].rearrange("p (t r) -> p t r", r=REC)
        key = sb("key", [P, TILES])
        blk_i = sb("blk_i", [P, TILES], I32)
        MT = sb("MT", [P, TILES * H])
        rec = MT[0:LANES, 0:COLS * REC].rearrange("p (c r) -> p c r", r=REC)
        e_dst = FT[0:LANES, 0:COLS].bitcast(I32)
        e_src = FT[0:LANES, COLS:2 * COLS].bitcast(I32)
        e_w = FT[0:LANES, 2 * COLS:3 * COLS]
        e_int = FT[0:LANES, 3 * COLS:4 * COLS].bitcast(I32)
        e_blk = ACC[0:LANES, 0 * COLS:1 * COLS]
        e_sblk = ACC[0:LANES, 1 * COLS:2 * COLS]
        e_sloc = ACC[0:LANES, 2 * COLS:3 * COLS]
        e_pos = ACC[0:LANES, 3 * COLS:4 * COLS]
        e_rank = ACC[0:LANES, 4 * COLS:5 * COLS]
        e_row = ACC[0:LANES, 5 * COLS:6 * COLS]
        tot = sb("tot", [LANES, NB])
        base_pos = sb("base_pos", [LANES, NB])
        tcount = sb("tcount", [P, 4, NB])
        tcount_i = sb("tcount_i", [P, NB], I32)
        tblk = sb("tblk", [P, TILES])
        hn1 = HN[:, :, :].rearrange("p b f -> p (b f)")
        ea = hn1[0:LANES, 0:1024].rearrange("p (a f) -> p a f", a=2)
        eaT = hn1[:, 1024:1024 + 8 * LANES].rearrange("p (a f) -> p a f", a=2)
        stg = sb("stg", [P, RING, G], U32)
        stg_rec = sb("stg_rec", [LANES, 2, G, REC])
        rows = sb("rows", [P, RING, G, D])
        OH = sb("OH", [P, RING, G, P])
        OHT32 = sb("OHT32", [P, G, P])
        OHT = OHT32[:, :, :].rearrange("p t n -> p (t n)").bitcast(BF16)[:, 0:G * P].rearrange("p (t n) -> p t n", n=P)
        ohw = OH[:, :, :, :].rearrange("p a t n -> p (a t n)").bitcast(BF16)
        OHB = ohw[:, 0:2 * G * P].rearrange("p (a t n) -> p a t n", a=2, n=P)
        OH16 = ohw[:, 2 * G * P:4 * G * P].rearrange("p (t n) -> p t n", n=P)
        identb = sb("identb", [P, P], BF16)
        at3 = sb("at3", [P, NB, 3, 4], BF16)
        m3p = sb("m3p", [P, NB, 3, H], BF16)
        ms3 = sb("ms3", [P, 2 * G, 3, H], BF16)
        res1 = sb("res1", [P, 2 * G * H])
        cnt1 = sb("cnt1", [P, 1], BF16)
        q3 = [FT[:, 0:NP // 2].bitcast(BF16), FT[:, NP // 2:NP].bitcast(BF16), hn1[:, 0:NP // 2].bitcast(BF16)]
        mreset = sb("mreset", [P, TILES])
        tlast_i = sb("tlast_i", [P, NB], I32)
        msg = sb("msg", [P, G, AW])
        sg16 = sb("sg16", [P, 2, 2 * G, H])
        dl16 = sb("dl16", [P, 2 * G, H])
        dlT = sb("dlT", [P, P])
        edge_of = sb("edge_of", [P, P + 1])
        rst = sb("rst", [P, P])
        fwd = sb("fwd", [P, P])
        runmax = sb("runmax", [P, P])
        pen = sb("pen", [P, 2 * G])
        mt = sb("mt", [P, 2 * G, H])
        sm = sb("sm", [P, G, H])
        sm3 = sb("sm3", [P, G, H])
        ohlo = ohw[0:LANES, :]
        ohhi = sb("ohhi", [LANES, 2, G, NB], BF16)

        bank = [ctx.enter_context(nc.psum_tensor(f"bank{i}", [P, 512], F32)) for i in range(8)]

        s_iota = sem("s_iota")
        s_load_x = sem("s_load_x")
        s_load_w = sem("s_load_w")
        s_load_e = sem("s_load_e")
        s_consts = sem("s_consts")
        s_abd0 = sem("s_abd0")
        s_tot = sem("s_tot")
        s_pre = sem("s_pre")
        s_rank = sem("s_rank")
        s_masked = sem("s_masked")
        s_placed = sem("s_placed")
        s_recbase = sem("s_recbase")
        s_recinit = sem("s_recinit")
        s_recdef = sem("s_recdef")
        s_uemm = sem("s_uemm")
        s_ue = sem("s_ue")
        s_ea = [sem(f"s_ea{i}") for i in range(2)]
        s_eaT = sem("s_eaT")
        s_eaTc = sem("s_eaTc")
        s_es = sem("s_es")
        s_esc = sem("s_esc")
        s_sstage = sem("s_sstage")
        s_scat = [sem(f"s_scat{i}") for i in range(2)]
        s_hoh = sem("s_hoh")
        s_hmm = sem("s_hmm")
        s_hacc = sem("s_hacc")
        s_recl = sem("s_recl")
        s_dg = sem("s_dg")
        s_keyb = sem("s_keyb")
        s_cmp = sem("s_cmp")
        s_rk = sem("s_rk")
        s_perm = sem("s_perm")
        s_sorted = sem("s_sorted")
        s_recs = sem("s_recs")
        s_pe_chunk = sem("s_pe_chunk")
        s_ev_chunk = sem("s_ev_chunk")
        s_table = sem("s_table")
        s_stored = [sem(f"s_stored{k}") for k in range(len(PASSES))]
        s_stage = sem("s_stage")
        s_gate = sem("s_gate")
        s_rows = [sem(f"s_rows{i}") for i in range(RING)]
        s_rowfree = sem("s_rowfree")
        s_oh = sem("s_oh")
        s_ohw = sem("s_ohw")
        s_part = sem("s_part")
        s_acc = sem("s_acc")
        s_tp = sem("s_tp")
        s_oht = sem("s_oht")
        s_got = sem("s_got")
        s_prod = sem("s_prod")
        s_sg = sem("s_sg")
        s_sl = sem("s_sl")
        s_dl = sem("s_dl")
        s_rowT = sem("s_rowT")
        s_dlT = sem("s_dlT")
        s_edge = sem("s_edge")
        s_fwd = sem("s_fwd")
        s_runT = sem("s_runT")
        s_runTT = sem("s_runTT")
        s_ms3 = sem("s_ms3")
        s_split = sem("s_split")
        s_d16 = sem("s_d16")
        s_scan = sem("s_scan")
        s_mall = sem("s_mall")
        s_oh16 = sem("s_oh16")
        s_mpart = sem("s_mpart")
        s_pen = sem("s_pen")
        s_mt = sem("s_mt")
        s_mx = sem("s_mx")
        s_sm = sem("s_sm")
        s_ex = sem("s_ex")
        s_msg = sem("s_msg")
        s_pass = sem("s_pass")
        s_feat = sem("s_feat")
        s_sq_in = sem("s_sq_in")
        s_sq_out = sem("s_sq_out")
        s_dve = sem("s_dve")
        s_act = sem("s_act")
        s_out = sem("s_out")
        s_scorecopy = sem("s_scorecopy")

        block = ctx.enter_context(nc.Block())

        def bcast(ap, shape):
            return ap.to_broadcast(shape)

        def transposed(k, q):
            if PASSES[k] == "score":
                return bank[q][:, 0:2 * P].bitcast(BF16)
            return bank[q][:, :]

        T_CH = [(c, min(4, NB - 4 * c)) for c in range((NB + 3) // 4)]
        L1_CH = [(c, min(3, NB - 3 * c)) for c in range((NB + 2) // 3)]
        STAGES = [("wT", 2), ("T", 7), ("Z", 7), ("T", 7),
                  ("T", 7), ("Z", 7), ("T", 7),
                  ("T", 7), ("Z", 7), ("T", 7),
                  ("T", 7), ("L1", len(L1_CH)),
                  ("T", 7), ("QKV", NB),
                  ("T", 7), ("O", 7),
                  ("T", 7), ("O", 7),
                  ("T", 7), ("O", 7)]
        CH0 = [sum(n for _, n in STAGES[:k]) for k in range(len(STAGES) + 1)]

        @block.sync
        def _(sp):
            sp.dma_start(e_dst[:, :], dst.rearrange("(p c) -> p c", p=LANES)).then_inc(s_load_e, 16)
            sp.dma_start(e_src[:, :], src.rearrange("(p c) -> p c", p=LANES)).then_inc(s_load_e, 16)
            sp.dma_start(e_w[:, :], edge_weight.rearrange("(p c) -> p c", p=LANES)).then_inc(s_load_e, 16)
            for k in range(2):
                sp.dma_start(wedge[:, k, :], W_edge).then_inc(s_load_w, 16)
            sp.wait_ge(s_abd0, 1)
            for part in range(3):
                for h in range(4):
                    sp.dma_start(abd[32 * h:32 * h + 32, 4 * part + h:4 * part + h + 1],
                                 a_vec[h, 32 * part:32 * part + 32].rearrange("(p o) -> p o", o=1)).then_inc(s_load_w, 16)
            for k, w in enumerate([W_node, Wq, Wk, Wv, Wo, Wt[0], Wt[1]]):
                sp.dma_start(wraw[:, k, :], w).then_inc(s_load_w, 16)
            for k, w in enumerate([fc_w, conv_w[0], conv_w[1]]):
                sp.dma_start(wfc[:, k, :], w).then_inc(s_load_w, 16)
            for k, v in enumerate([fc_b, conv_b[0], conv_b[1], bn_gamma[0], bn_gamma[1], bn_gamma[2],
                                   bn_beta[0], bn_beta[1], bn_beta[2]]):
                sp.dma_start(cols[:, k:k + 1], v.rearrange("(p o) -> p o", o=1)).then_inc(s_load_w, 16)
            for k, v in enumerate([bq, bk, bv, bo, bt[0], bt[1]]):
                sp.dma_start(brow[:, k, :], v.rearrange("(o f) -> o f", o=1)).then_inc(s_load_w, 16)
            for k in range(2):
                sp.dma_start(wgb[:, k, :], Wg[k].rearrange("(o f) -> o f", o=1).broadcast_to([P, D])).then_inc(s_load_w, 16)
            sp.dma_start(bgb[:, :], bg.rearrange("(o f) -> o f", o=1).broadcast_to([P, 2])).then_inc(s_load_w, 16)
            sp.wait_ge(s_consts, 1)
            sp.dma_start(X[:, 0:NB - 1, :], x[0:(NB - 1) * P, :].rearrange("(b p) f -> p b f", p=P)).then_inc(s_load_x, 16)
            sp.dma_start(X[0:TAIL, NB - 1, :], x[(NB - 1) * P:N, :]).then_inc(s_load_x, 16)
            sp.wait_ge(s_recdef, 1)
            sp.dma_start(rec_dram.rearrange("(p t) r -> p (t r)", p=P), recS[:, :, :].rearrange("p t r -> p (t r)")).then_inc(s_recinit, 16)
            ea_v = edge_attr.rearrange("(p c) f -> p (c f)", p=LANES)
            for i in steps(sp, COLS // 16):
                for half in range(2):
                    if not isinstance(i, int):
                        sp.wait_ge(s_eaT, 2 * i + half - 1)
                    sp.dma_start(ea[:, half, :], ea_v[:, bass.ds(i * 1024 + half * 512, 512)]).then_inc(s_ea[half], 16)
            for half in range(2):
                sp.wait_ge(s_scat[half], 16 * G * (COLS // 16))
            sp.dma_start(recU.rearrange("p t r -> p (t r)"), rec_dram.rearrange("(p t) r -> p (t r)", p=P)).then_inc(s_recl, 16)
            TABS = {0: TAB[:, :, 0:D], 1: TAB[:, :, 0:D], 2: TAB[:, :, D:D + 4], 3: TAB[:, :, 0:D],
                    4: QKV[:, :, D:2 * D], 5: QKV[:, :, 2 * D:3 * D], 6: TAB[:, :, 0:D], 7: TAB[:, :, 0:D]}
            for k in range(len(PASSES)):
                sp.wait_ge(s_table, k + 1)
                t = TABS[k]
                sp.dma_start(tab_dram[k][0:(NB - 1) * P, :].rearrange("(b p) f -> p b f", p=P), t[:, 0:NB - 1, :]).then_inc(s_stored[k], 16)
                sp.dma_start(tab_dram[k][(NB - 1) * P:N, :], t[0:TAIL, NB - 1, :]).then_inc(s_stored[k], 16)
            sp.wait_ge(s_table, len(PASSES) + 1)
            sp.dma_start(out[0:(NB - 1) * P, :].rearrange("(b p) f -> p b f", p=P), X[:, 0:NB - 1, :]).then_inc(s_out, 16)
            sp.dma_start(out[(NB - 1) * P:N, :], X[0:TAIL, NB - 1, :]).then_inc(s_out, 16)
            sp.wait_ge(s_out, 32)
            for k in range(len(PASSES)):
                sp.wait_ge(s_stored[k], 32)

        @block.gpsimd
        def _(pool):
            nc.gpsimd.iota(iota_i[:, :], pattern=[[1, 512]], base=0, channel_multiplier=0).then_inc(s_iota, 1)
            nc.gpsimd.iota(lane_i[:, :], pattern=[[0, 1]], base=0, channel_multiplier=1).then_inc(s_iota, 1)
            pool.wait_ge(s_recinit, 16)
            for i in steps(pool, COLS // 16):
                for half in range(2):
                    pool.wait_ge(s_sstage, 2 * i + half + 1)
                    pool.sem_inc(s_gate, 1)
                    for j in range(G):
                        nc.gpsimd.indirect_dma_start(
                            rec_dram, bass.IndirectOffsetOnAxis(ap=stg[0:LANES, half, j:j + 1], axis=0),
                            stg_rec[:, half, j, :], None).then_inc(s_scat[half], 16)
            for k in range(len(PASSES)):
                pool.wait_ge(s_stored[k], 32)
                if k == 0:
                    pool.wait_ge(s_recs, 1)
                width = 4 if k == 2 else D
                for i in steps(pool, ITERS):
                    for q in range(RING):
                        g = RING * i + q
                        if k or not isinstance(i, int):
                            pool.wait_ge(s_rowfree, k * GROUPS + g - RING + 1)
                            pool.wait_ge(s_rows[q], 16 * G * (k * ITERS + i))
                            pool.sem_inc(s_gate, 1)
                        nc.gpsimd.tensor_copy(stg[:, q, :], recS[:, bass.ds(G * g, G), R_SRC]).then_inc(s_stage, 1)
                        pool.wait_ge(s_stage, k * GROUPS + g + 1)
                        pool.sem_inc(s_gate, 1)
                        for j in range(G):
                            nc.gpsimd.indirect_dma_start(
                                rows[:, q, j, 0:width], None, tab_dram[k],
                                bass.IndirectOffsetOnAxis(ap=stg[:, q, j:j + 1], axis=0)).then_inc(s_rows[q], 16)

        @block.scalar
        def _(act):
            done = [0]
            chunks = [0]

            def link(ins):
                done[0] += 1
                ins.then_inc(s_act, 1)
                act.wait_ge(s_act, done[0])

            def evac(dst_ap, src_ap, func=ACT.Copy, **kw):
                act.wait_ge(s_pe_chunk, chunks[0] + 1)
                nc.scalar.activation(dst_ap, src_ap, func, **kw).then_inc(s_ev_chunk, 1)
                chunks[0] += 1

            def bank_of():
                return bank[chunks[0] % 2]

            def transposes(to):
                for c, n in T_CH:
                    evac(to(c, n), bank_of()[:, 0:n * P])

            def feat(c, n):
                return FT[:, c * 512:c * 512 + n * P]

            def back(c, n):
                return HN[:, 4 * c:4 * c + n, :].rearrange("p b f -> p (b f)")

            act.wait_ge(s_uemm, 1)
            act.wait_ge(s_consts, 1)
            link(nc.scalar.activation(ue2[0:64, 0:4], bank[7][0:64, 0:4], ACT.Copy))
            link(nc.scalar.activation(ue2[64:128, 4:8], bank[7][64:128, 0:4], ACT.Copy))
            act.sem_inc(s_ue, 1)
            for i in steps(act, COLS // 16):
                for half in range(2):
                    g = 2 * i + half
                    act.wait_ge(s_eaT, g + 1)
                    nc.scalar.activation(eaT[:, half, :], bank[half][:, 0:4 * LANES], ACT.Copy).then_inc(s_eaTc, 1)
                    act.wait_ge(s_es, g + 1)
                    act.sem_inc(s_gate, 1)
                    nc.scalar.activation(rec[:, bass.ds(G * g, G), R_E:R_E + 4],
                                         bank[2 + half][0:LANES, 0:32].rearrange("p (c h) -> p c h", h=4), ACT.Copy).then_inc(s_esc, 1)
            act.wait_ge(s_placed, 1)
            act.wait_ge(s_esc, 2 * (COLS // 16))
            for i in steps(act, COLS // 16):
                for half in range(2):
                    if not isinstance(i, int):
                        act.wait_ge(s_scat[half], 16 * G * i)
                        act.sem_inc(s_gate, 1)
                    nc.scalar.activation(stg_rec[:, half, :, :], rec[:, bass.ds(G * (2 * i + half), G), :], ACT.Copy).then_inc(s_scorecopy, 1)
                    nc.scalar.activation(stg[0:LANES, half, :], e_row[:, bass.ds(G * (2 * i + half), G)], ACT.Copy).then_inc(s_scorecopy, 1)
                    act.wait_ge(s_scorecopy, 2 * (2 * i + half) + 2)
                    act.sem_inc(s_sstage, 1)
            copies0 = 4 * (COLS // 16)
            for i in steps(act, PAIRS):
                for half in range(2):
                    g = 2 * i + half
                    act.wait_ge(s_sorted, g + 1)
                    act.sem_inc(s_gate, 1)
                    nc.scalar.activation(recS[:, bass.ds(G * g, G), :],
                                         bank[4 + half][:, 0:G * REC].rearrange("p (t r) -> p t r", r=REC), ACT.Copy).then_inc(s_perm, 1)
            act.wait_ge(s_perm, GROUPS)
            act.sem_inc(s_recs, 1)

            asks = [0]

            def answer(dst_ap, src_ap, func, **kw):
                act.wait_ge(s_sq_in, asks[0] + 1)
                nc.scalar.activation(dst_ap, src_ap, func, **kw).then_inc(s_sq_out, 1)
                asks[0] += 1

            def root():
                answer(stat[:, 3, :], stat[:, 2, :], ACT.Sqrt)

            def oht_copies(k, g):
                b = groups_before(k, ("score", "attn"))
                act.wait_ge(s_tp, b + g + 1)
                if b or there(g - 1):
                    act.wait_ge(s_got, b + g)
                act.sem_inc(s_gate, 1)
                for q in range(2):
                    nc.scalar.activation(OHT[:, 4 * q:4 * q + 4, :].rearrange("p t n -> p (t n)"),
                                         transposed(k, q), ACT.Copy).then_inc(s_oht, 1)

            def score_pass(k):
                b16 = groups_before(k, ("score",)) // 2

                def keep_scores(p):
                    act.wait_ge(s_sg, 2 * (b16 + p) + 2)
                    act.sem_inc(s_gate, 1)
                    nc.scalar.activation(S[:, bass.ds(2 * G * H * p, 2 * G * H)],
                                         sg16[:, slot(p), :, :].rearrange("p t h -> p (t h)"), ACT.Copy).then_inc(s_sl, 1)

                def destinations(p):
                    act.wait_ge(s_rowT, b16 + p + 1)
                    if b16 or there(p - 1):
                        act.wait_ge(s_runT, b16 + p)
                    act.sem_inc(s_gate, 1)
                    nc.scalar.activation(dlT[:, :], bank[3][:, 0:P], ACT.Copy).then_inc(s_dlT, 1)

                oht_copies(k, 0)
                for i in rounds(act, ITERS):
                    for q in range(RING):
                        g = RING * i + q
                        slot = lambda p: (q // 2 + q % 2 + 1) % 2
                        if there(g + 1):
                            oht_copies(k, g + 1)
                        if q % 2 == 1:
                            slot = lambda p: q // 2
                            keep_scores(2 * i + q // 2)
                        elif there(g - 2):
                            destinations(2 * i + q // 2 - 1)
                destinations(PAIRS - 1)

            def attn_pass(k):
                b = groups_before(k, ("attn",))
                oht_copies(k, 0)
                for i in rounds(act, ITERS):
                    for q in range(RING):
                        g = RING * i + q
                        if there(g + 1):
                            oht_copies(k, g + 1)
                        act.wait_ge(s_sm, b + g + 1)
                        if b or there(g - 1):
                            act.wait_ge(s_part, groups_before(k, ("sum", "attn")) + g)
                        act.sem_inc(s_gate, 1)
                        nc.scalar.activation(msg[:, :, D:AW], sm[:, :, :], ACT.Exp).then_inc(s_ex, 1)

            for c, n in enumerate([4, 3]):
                evac(wT[:, 4 * c:4 * c + n, :].rearrange("p b f -> p (b f)"), bank_of()[:, 0:n * P])
            root(); root()
            root()
            transposes(feat)
            for layer in range(3):
                for c, n in T_CH:
                    evac(ZT[:, c * 512:c * 512 + n * P], bank_of()[:, 0:n * P], ACT.Identity, bias=cols[:, layer:layer + 1])
                answer(bnv[:, 3:4], bnv[:, 2:3], ACT.Sqrt)
                answer(HT if layer == 0 else FT[:, :], ZT, ACT.Relu, scale=bnv[:, 5:6], bias=bnv[:, 6:7])
                transposes(back)
                if layer < 2:
                    transposes(feat)
            root()
            transposes(feat)
            for c, n in L1_CH:
                evac(TAB[:, 3 * c:3 * c + n, :].rearrange("p b f -> p (b f)"), bank_of()[:, 0:n * AW])
            score_pass(2)
            attn_pass(3)
            answer(stat[:, 4:8, :].rearrange("p h b -> p b h"), m3[:, :, 0:4], ACT.Exp, scale=-1.0)
            root()
            transposes(feat)
            for c in range(NB):
                act.wait_ge(s_pe_chunk, chunks[0] + 1)
                link(nc.scalar.activation(QKV[:, c, 0:D], bank_of()[:, 0:D], ACT.Copy, scale=0.25))
                nc.scalar.activation(QKV[:, c, D:3 * D], bank_of()[:, D:3 * D], ACT.Copy).then_inc(s_ev_chunk, 1)
                chunks[0] += 1
            score_pass(4)
            attn_pass(5)
            transposes(feat)
            for c, n in T_CH:
                evac(HN[:, 4 * c:4 * c + n, :].rearrange("p b f -> p (b f)"), bank_of()[:, 0:n * P])
            root()
            for layer in range(2):
                transposes(feat)
                for c, n in T_CH:
                    evac(HN[:, 4 * c:4 * c + n, :].rearrange("p b f -> p (b f)"), bank_of()[:, 0:n * P])
                answer(stat[:, 1, :], stat[:, 0, :], ACT.Tanh, bias=bgb[:, layer:layer + 1])
            assert chunks[0] == CH0[-1]

        @block.tensor
        def _(pe):
            chunks = [0]

            def chunk(fill):
                if chunks[0] >= 2:
                    pe.wait_ge(s_ev_chunk, chunks[0] - 1)
                fill(bank[chunks[0] % 2]).then_inc(s_pe_chunk, 1)
                chunks[0] += 1

            feats = [0]

            def need_feat():
                feats[0] += 1
                pe.wait_ge(s_feat, feats[0])

            def transposes(src_of):
                for c, n in T_CH:
                    def fill(b):
                        for q in range(n):
                            last = nc.tensor.transpose(b[:, q * P:(q + 1) * P], src_of(4 * c + q), ident[:, :])
                        return last
                    chunk(fill)

            def node(b):
                return HN[:, b, :]

            def product_T(w):
                pe.wait_ge(s_ev_chunk, chunks[0])
                for c, n in T_CH:
                    chunk(lambda b: nc.tensor.matmul(b[:, 0:n * P], w, FT[:, c * 512:c * 512 + n * P], start=True, stop=True))

            def fblock(b):
                return FT[:, b * P:(b + 1) * P]

            def product_bias(w, bias):
                pe.wait_ge(s_ev_chunk, chunks[0])
                for c, n in T_CH:
                    def fill(b):
                        for q in range(n):
                            nc.tensor.matmul(b[:, q * P:(q + 1) * P], fblock(4 * c + q), w, start=True, stop=False)
                            last = nc.tensor.matmul(b[:, q * P:(q + 1) * P], ones[0:1, :], bias, start=False, stop=True)
                        return last
                    chunk(fill)

            pe.wait_ge(s_tot, NB)
            pe.wait_ge(s_consts, 1)
            nc.tensor.matmul(bank[6][:, 0:NB], tri[0:LANES, :], tot[:, :], start=True, stop=True)
            nc.tensor.matmul(bank[6][:, 32:32 + NB], ones[0:LANES, :], tot[:, :], start=True, stop=True).then_inc(s_pre, 1)
            pe.wait_ge(s_load_w, 16 * 42)
            nc.tensor.matmul(bank[7][:, 0:4], wedge[:, :, :].rearrange("p a f -> p (a f)"), abd[:, 8:12], start=True, stop=True).then_inc(s_uemm, 1)
            pe.wait_ge(s_ue, 1)
            for i in steps(pe, COLS // 16):
                for half in range(2):
                    g = 2 * i + half
                    pe.wait_ge(s_ea[half], 16 * i + 16)
                    if not isinstance(i, int):
                        pe.wait_ge(s_eaTc, g - 1)
                    for j in range(4):
                        last = nc.tensor.transpose(bank[half][:, j * LANES:(j + 1) * LANES],
                                                   ea[:, half, j * P:(j + 1) * P], ident[0:LANES, 0:LANES])
                    last.then_inc(s_eaT, 1)
                    pe.wait_ge(s_eaTc, g + 1)
                    if not isinstance(i, int):
                        pe.wait_ge(s_esc, g - 1)
                    for j in range(4):
                        last = nc.tensor.matmul(bank[2 + half][0:LANES, 8 * j:8 * j + 8],
                                                eaT[:, half, j * LANES:(j + 1) * LANES], ue2[:, :], start=True, stop=True)
                    last.then_inc(s_es, 1)
            for i in steps(pe, COLS // G // 2):
                for both in range(2):
                    for kind in range(2):
                        pe.wait_ge(s_hoh, 4 * i + 2 * both + kind + 1)
                        if kind == 0 and both + (0 if isinstance(i, int) else 1):
                            pe.wait_ge(s_hacc, 2 * i + both)
                        for j in range(G):
                            last = nc.tensor.matmul(bank[6][:, kind * 32 + 64:kind * 32 + 64 + NB],
                                                    ohlo[:, kind * 1024 + j * P:kind * 1024 + (j + 1) * P],
                                                    ohhi[:, kind, j, :], start=(j == 0), stop=(j == G - 1))
                        last.then_inc(s_hmm, 1)
            for i in steps(pe, PAIRS):
                for half in range(2):
                    g = 2 * i + half
                    pe.wait_ge(s_dg, g + 1)
                    for q in range(2):
                        last = nc.tensor.matmul(bank[2 * half + q][:, :], ones[:, :], OHT32[:, 4 * q:4 * q + 4, :].rearrange("p t n -> p (t n)"),
                                                start=True, stop=True)
                    last.then_inc(s_keyb, 1)
                    pe.wait_ge(s_rk, g + 1)
                    if not isinstance(i, int):
                        pe.wait_ge(s_perm, g - 1)
                    for j in range(G):
                        last = nc.tensor.matmul(bank[4 + half][:, REC * j:REC * (j + 1)], OH[:, half, j, :],
                                                recU[:, bass.ds(G * g + j, 1), :].rearrange("p t r -> p (t r)"), start=True, stop=True)
                    last.then_inc(s_sorted, 1)

            def onehot_transposes(k, g, slot):
                b = groups_before(k, ("score", "attn"))
                pe.wait_ge(s_oh, GROUPS * k + g + 1)
                if b or there(g - 1):
                    pe.wait_ge(s_oht, 2 * (b + g))
                for j in range(G):
                    one, i_ = (OHB[:, slot % 2, j, :], identb) if PASSES[k] == "score" else (OH[:, slot, j, :], ident)
                    last = nc.tensor.transpose(transposed(k, j // 4)[:, (j % 4) * P:(j % 4 + 1) * P], one, i_[:, :])
                last.then_inc(s_tp, 1)
                pe.wait_ge(s_oht, 2 * (b + g) + 2)

            def block_regs(g):
                _, vals = nc.values_load_multi_w_load_instructions(
                    blk_i[0:1, bass.ds(G * g, G)], engines=[pe.engine], min_val=0, max_val=NB - 1,
                    skip_runtime_bounds_check_because="the table holds min(count of blocks, NB - 1)")
                return vals

            def sum_pass(k):
                own = groups_before(k, ("sum",))
                parts = groups_before(k, ("sum", "attn"))
                for i in steps(pe, ITERS):
                    for q in range(RING):
                        g = RING * i + q
                        pe.wait_ge(s_ohw, own + g + 1)
                        if parts or there(g - 2):
                            pe.wait_ge(s_acc, G * (parts + g - 1))
                        pe.wait_ge(s_rows[q], 16 * G * (k * ITERS + i + 1))
                        for j in range(G):
                            last = nc.tensor.matmul(bank[4 + 2 * (q % 2) + j // 4][:, (j % 4) * P:(j % 4 + 1) * P], OH[:, q, j, :],
                                                    rows[:, q, j, :], start=True, stop=True)
                        last.then_inc(s_part, 1)

            def score_pass(k):
                b16 = groups_before(k, ("score",)) // 2

                def fetch(g, q):
                    vals = block_regs(g)
                    onehot_transposes(k, g, q)
                    if b16 or there(g - 1):
                        pe.wait_ge(s_prod, 2 * b16 + g)
                    for j in range(G):
                        if k == 2:
                            last = nc.tensor.matmul(bank[2][:, 12 * j:12 * j + 12], OHT[:, j, :],
                                                    at3[:, bass.ds(vals[j], 1), :, :].rearrange("p b s h -> p (b s h)"), start=True, stop=True)
                        else:
                            for s_ in range(3):
                                last = nc.tensor.matmul(bank[4 + j // 4][:, (j % 4) * P:(j % 4 + 1) * P], OHT[:, j, :],
                                                        q3[s_][:, bass.ds(vals[j] * D, D)], start=(s_ == 0), stop=(s_ == 2))
                    last.then_inc(s_got, 1)

                def turn(p, sl):
                    pe.wait_ge(s_dl, b16 + p + 1)
                    pe.wait_ge(s_sg, 2 * (b16 + p) + 2)
                    if b16 or there(p - 1):
                        pe.wait_ge(s_fwd, 3 * (b16 + p))
                        pe.wait_ge(s_dlT, b16 + p)
                    pe.sem_inc(s_gate, 1)
                    nc.tensor.transpose(bank[3][:, 0:P], dl16[:, :, :].rearrange("p t h -> p (t h)"), ident[:, :])
                    nc.tensor.transpose(bank[3][:, P:2 * P], sg16[:, sl, :, :].rearrange("p t h -> p (t h)"), ident[:, :]).then_inc(s_rowT, 1)

                def maxima(p):
                    pe.wait_ge(s_runT, b16 + p + 1)
                    if b16 or there(p - 1):
                        pe.wait_ge(s_ms3, b16 + p)
                    pe.sem_inc(s_gate, 1)
                    nc.tensor.transpose(bank[3][:, 2 * P:3 * P], runmax[:, :], ident[:, :]).then_inc(s_runTT, 1)
                    pe.wait_ge(s_ms3, b16 + p + 1)
                    pe.wait_ge(s_oh16, b16 + p + 1)
                    if b16 or there(p - 1):
                        pe.wait_ge(s_mt, b16 + p)
                    for j in range(2 * G):
                        for s_ in range(3):
                            nc.tensor.matmul(bank[7][:, H * j:H * j + H], OH16[:, j, :], ms3[:, j, s_, :], start=(s_ == 0), stop=(s_ == 2))
                        last = nc.tensor.matmul(bank[6][:, j:j + 1], OH16[:, j, :], cnt1[:, :], start=True, stop=True)
                    last.then_inc(s_mpart, 1)

                fetch(0, 0)
                for i in rounds(pe, ITERS):
                    for q in range(RING):
                        g = RING * i + q
                        if there(g + 1):
                            fetch(g + 1, q + 1)
                        if there(g - 2):
                            if q % 2 == 0:
                                turn(2 * i + q // 2 - 1, (q // 2 + 1) % 2)
                            else:
                                maxima(2 * i + q // 2 - 1)
                turn(PAIRS - 1, (PAIRS - 1) % 2)
                maxima(PAIRS - 1)

            def attn_pass(k):
                b = groups_before(k, ("attn",))
                parts = groups_before(k, ("sum", "attn"))

                def fetch(g, q):
                    vals = block_regs(g)
                    onehot_transposes(k, g, q % RING)
                    if b or there(g - 1):
                        pe.wait_ge(s_sm, b + g)
                    for j in range(G):
                        last = nc.tensor.matmul(bank[2][:, 3 * H * j:3 * H * (j + 1)], OHT[:, j, :],
                                                m3p[:, bass.ds(vals[j], 1), :, :].rearrange("p b s h -> p (b s h)"), start=True, stop=True)
                    last.then_inc(s_got, 1)

                fetch(0, 0)
                for i in rounds(pe, ITERS):
                    for q in range(RING):
                        g = RING * i + q
                        if there(g + 1):
                            fetch(g + 1, q + 1)
                        pe.wait_ge(s_acc, G * (parts + g))
                        pe.wait_ge(s_msg, b + g + 1)
                        for j in range(G):
                            last = nc.tensor.matmul(bank[4 + j // 3][:, (j % 3) * AW:(j % 3 + 1) * AW], OH[:, q, j, :],
                                                    msg[:, j, :], start=True, stop=True)
                        last.then_inc(s_part, 1)

            pe.wait_ge(s_consts, 1)
            for c, n in enumerate([4, 3]):
                def fill(b):
                    for q in range(n):
                        last = nc.tensor.transpose(b[:, q * P:(q + 1) * P], wraw[:, 4 * c + q, :], ident[:, :])
                    return last
                chunk(fill)
            nc.tensor.matmul(bank[7][:, 8:16], wraw[:, 0, :], abd[:, 0:8], start=True, stop=True).then_inc(s_uemm, 1)
            need_feat()
            transposes(node)
            for layer in range(3):
                product_T(wfc[:, layer, :])
                need_feat()
                transposes(lambda b: HT[:, b * P:(b + 1) * P])
                if layer < 2:
                    sum_pass(layer)
                    need_feat()
                    transposes(node)
            need_feat()
            transposes(node)
            pe.wait_ge(s_ev_chunk, chunks[0])
            for c, n in L1_CH:
                def fill(b):
                    for q in range(n):
                        nc.tensor.matmul(b[:, q * AW:q * AW + D], fblock(3 * c + q), wT[:, 0, :], start=True, stop=True)
                        last = nc.tensor.matmul(b[:, q * AW + D:(q + 1) * AW], fblock(3 * c + q), ust[:, :], start=True, stop=True)
                    return last
                chunk(fill)
            need_feat()
            score_pass(2)
            need_feat()
            attn_pass(3)
            need_feat()
            transposes(node)
            pe.wait_ge(s_ev_chunk, chunks[0])
            for c in range(NB):
                def fill(b):
                    nc.tensor.matmul(b[:, 0:3 * D], fblock(c), wT[:, 1:4, :].rearrange("p a f -> p (a f)"), start=True, stop=False)
                    return nc.tensor.matmul(b[:, 0:3 * D], ones[0:1, :], brow[:, 0:3, :].rearrange("p a f -> p (a f)"), start=False, stop=True)
                chunk(fill)
            need_feat()
            score_pass(4)
            need_feat()
            attn_pass(5)
            need_feat()
            transposes(node)
            product_bias(wT[:, 4, :], brow[:, 3, :])
            for layer in range(2):
                need_feat()
                transposes(node)
                product_bias(wT[:, 5 + layer, :], brow[:, 4 + layer, :])
                sum_pass(6 + layer)
            assert chunks[0] == CH0[-1]

        @block.vector
        def _(dve):
            done = [0]
            asked = [0]
            v = nc.vector

            def link(ins):
                done[0] += 1
                ins.then_inc(s_dve, 1)
                dve.wait_ge(s_dve, done[0])

            def ask():
                dve.sem_inc(s_sq_in, 1)
                asked[0] += 1
                dve.wait_ge(s_sq_out, asked[0])

            link(v.memset(abd[:, :], 0.0))
            dve.sem_inc(s_abd0, 1)
            dve.wait_ge(s_iota, 2)
            link(v.tensor_copy(iota[:, :], iota_i[:, :]))
            link(v.tensor_copy(lane[:, :], lane_i[:, :]))
            link(v.tensor_scalar(ident[:, :], iota[:, 0:P], lane[:, 0:1], None, ALU.is_equal))
            link(v.tensor_scalar(tri[:, :], iota[:, 0:P], lane[:, 0:1], None, ALU.is_gt))
            link(v.memset(ones[:, :], 1.0))
            link(v.memset(ue2[:, :], 0.0))
            link(v.memset(X[:, NB - 1, :], 0.0))
            link(v.memset(edge_of[:, :], 1.0))
            link(v.memset(cnt1[:, :], 1.0))
            link(v.tensor_copy(identb[:, :], ident[:, :]))
            link(v.memset(sg16[:, :, :, :], 0.0))
            link(v.memset(hist[:, :, :], 0.0))
            dve.sem_inc(s_consts, 1)
            link(v.memset(recS[:, :, :], 0.0))
            link(v.memset(recS[:, :, R_DST], float(P)))
            dve.sem_inc(s_recdef, 1)

            dve.wait_ge(s_load_e, 48)
            link(v.memset(rec[:, :, :], 0.0))
            for ends, blk, loc in ((e_dst, e_blk[:, :], rec[:, :, R_DST]), (e_src, e_sblk[:, :], e_sloc[:, :])):
                link(v.tensor_single_scalar(e_int[:, :], ends[:, :], 7, ALU.arith_shift_right))
                link(v.tensor_copy(blk, e_int[:, :]))
                link(v.tensor_copy(e_rank[:, :], ends[:, :]))
                link(v.scalar_tensor_tensor(loc, blk, -float(P), e_rank[:, :], ALU.mult, ALU.add))
            link(v.tensor_copy(rec[:, :, R_SRC], e_rank[:, :]))
            link(v.tensor_scalar(e_rank[:, :], e_w[:, :], F_MAX, None, ALU.is_le))
            link(v.scalar_tensor_tensor(e_int[:, :], e_w[:, :], -F_MAX, e_rank[:, :], ALU.is_ge, ALU.mult))
            link(v.copy_predicated(rec[:, :, R_W], e_int[:, :], e_w[:, :]))
            with dve.Fori(0, NB, 1) as b:
                v.tensor_scalar(e_rank[:, :], e_blk[:, :], iota[0:LANES, bass.ds(b, 1)], 0.0, ALU.is_equal, ALU.add,
                                accum_out=tot[:, bass.ds(b, 1)]).then_inc(s_tot, 1)
                dve.wait_ge(s_tot, b + 1)
            dve.wait_ge(s_pre, 1)
            link(v.tensor_scalar(tcount_i[:, :], bank[6][:, 32:32 + NB], float(P - 1), None, ALU.add))
            link(v.tensor_single_scalar(tcount_i[:, :], tcount_i[:, :], 7, ALU.arith_shift_right))
            link(v.tensor_copy(tcount[:, 0, :], tcount_i[:, :]))
            link(v.memset(tcount[:, 3, :], 0.0))
            link(v.tensor_tensor_scan(tcount[:, 1, :], tcount[:, 3, :], tcount[:, 0, :], 0.0, ALU.add, ALU.add))
            link(v.tensor_tensor(tcount[:, 2, :], tcount[:, 1, :], tcount[:, 0, :], ALU.subtract))
            link(v.tensor_scalar(tcount[:, 2, :], tcount[:, 2, :], float(P), -1.0, ALU.mult, ALU.add))
            link(v.tensor_tensor(base_pos[:, :], bank[6][0:LANES, 0:NB], tcount[0:LANES, 2, :], ALU.add))
            link(v.memset(e_pos[:, :], 0.0))
            link(v.memset(e_w[:, :], 0.0))
            with dve.Fori(0, NB, 1) as b:
                v.tensor_scalar(e_int[:, :], e_blk[:, :], iota[0:LANES, bass.ds(b, 1)], None, ALU.is_equal).then_inc(s_rank, 1)
                dve.wait_ge(s_rank, b * 3 + 1)
                v.tensor_tensor_scan(e_rank[:, :], e_w[:, :], e_int[:, :], base_pos[:, bass.ds(b, 1)], ALU.add, ALU.add).then_inc(s_rank, 1)
                dve.wait_ge(s_rank, b * 3 + 2)
                dve.sem_inc(s_gate, 1)
                v.copy_predicated(e_pos[:, :], e_int[:, :], e_rank[:, :]).then_inc(s_rank, 1)
                dve.wait_ge(s_rank, b * 3 + 3)
            link(v.tensor_copy(e_int[:, :], e_pos[:, :]))
            link(v.tensor_single_scalar(e_int[:, :], e_int[:, :], 7, ALU.arith_shift_right))
            link(v.tensor_copy(e_rank[:, :], e_int[:, :]))
            link(v.scalar_tensor_tensor(e_pos[:, :], e_rank[:, :], -float(P), e_pos[:, :], ALU.mult, ALU.add))
            link(v.scalar_tensor_tensor(e_row[:, :], e_pos[:, :], float(TILES), e_rank[:, :], ALU.mult, ALU.add))
            dve.sem_inc(s_placed, 1)
            link(v.memset(tblk[:, :], 0.0))
            with dve.Fori(0, NB, 1) as b:
                v.scalar_tensor_tensor(tblk[:, :], iota[:, 0:TILES], tcount[:, 1, bass.ds(b, 1)], tblk[:, :],
                                       ALU.is_ge, ALU.add).then_inc(s_masked, 1)
                dve.wait_ge(s_masked, b + 1)
            link(v.tensor_scalar(tblk[:, :], tblk[:, :], float(NB - 1), None, ALU.min))
            link(v.tensor_copy(blk_i[:, :], tblk[:, :]))
            link(v.tensor_tensor(mreset[:, 1:TILES], tblk[:, 1:TILES], tblk[:, 0:TILES - 1], ALU.not_equal))
            link(v.memset(mreset[:, 0:1], 1.0))
            link(v.tensor_scalar(mreset[:, :], mreset[:, :], -BIG, None, ALU.mult))
            link(v.tensor_scalar(tlast_i[:, :], tcount[:, 1, :], -1.0, 0.0, ALU.add, ALU.max))

            for i in steps(dve, COLS // G // 2):
                for both in range(2):
                    g = 2 * i + both
                    for kind, (blk, loc) in enumerate(((e_blk[:, :], rec[:, :, R_DST]), (e_sblk[:, :], e_sloc[:, :]))):
                        if both + (0 if isinstance(i, int) else 1):
                            dve.wait_ge(s_hmm, 2 * g - 1 + kind)
                        v.tensor_tensor(ohlo[:, kind * 1024:(kind + 1) * 1024].rearrange("p (g n) -> p g n", g=G),
                                        iota[0:LANES, 0:P].unsqueeze(1).to_broadcast([LANES, G, P]),
                                        loc[:, bass.ds(G * g, G)].unsqueeze(2).to_broadcast([LANES, G, P]), ALU.is_equal).then_inc(s_rank, 1)
                        v.tensor_tensor(ohhi[:, kind, :, :],
                                        iota[0:LANES, 0:NB].unsqueeze(1).to_broadcast([LANES, G, NB]),
                                        blk[:, bass.ds(G * g, G)].unsqueeze(2).to_broadcast([LANES, G, NB]), ALU.is_equal).then_inc(s_rank, 1)
                        dve.wait_ge(s_rank, 3 * NB + 4 * g + 2 * kind + 2)
                        dve.sem_inc(s_hoh, 1)
                    dve.wait_ge(s_hmm, 2 * g + 2)
                    v.tensor_tensor(hist[:, :, :], hist[:, :, :],
                                    bank[6][:, 64:128].rearrange("p (k b) -> p k b", k=2)[:, :, 0:NB], ALU.add).then_inc(s_hacc, 1)
                    dve.wait_ge(s_hacc, g + 1)

            dve.wait_ge(s_recl, 16)
            link(v.tensor_scalar(key[:, :], recU[:, :, R_DST], float(P), lane[:, 0:1], ALU.mult, ALU.add))
            for i in steps(dve, PAIRS):
                for half in range(2):
                    g = 2 * i + half
                    kg = key[:, bass.ds(G * g, G)].unsqueeze(2).to_broadcast([P, G, P])
                    if half + (0 if isinstance(i, int) else 1):
                        dve.wait_ge(s_keyb, g)
                    v.tensor_tensor(OHT32[:, :, :], ident[:, :].unsqueeze(1).to_broadcast([P, G, P]), kg, ALU.mult).then_inc(s_dg, 1)
                    dve.wait_ge(s_keyb, g + 1)
                    if not isinstance(i, int):
                        dve.wait_ge(s_sorted, g - 1)
                    for q in range(2):
                        v.tensor_tensor(OH[:, half, 4 * q:4 * q + 4, :], bank[2 * half + q][:, :].rearrange("p (g n) -> p g n", g=4),
                                        key[:, bass.ds(G * g + 4 * q, 4)].unsqueeze(2).to_broadcast([P, 4, P]), ALU.is_lt).then_inc(s_cmp, 1)
                    dve.wait_ge(s_cmp, 3 * g + 2)
                    v.tensor_reduce(pen[:, half * G:(half + 1) * G], OH[:, half, :, :], AX, ALU.add).then_inc(s_cmp, 1)
                    dve.wait_ge(s_cmp, 3 * g + 3)
                    v.tensor_tensor(OH[:, half, :, :], iota[:, 0:P].unsqueeze(1).to_broadcast([P, G, P]),
                                    pen[:, half * G:(half + 1) * G].unsqueeze(2).to_broadcast([P, G, P]), ALU.is_equal).then_inc(s_rk, 1)

            link(v.tensor_scalar(stat[:, 2, :], hist[:, 0, :], 1.0, None, ALU.max))
            ask()
            link(v.reciprocal(stat[:, 0, :], stat[:, 3, :]))
            link(v.tensor_scalar(stat[:, 1, :], hist[:, 0, :], 0.0, None, ALU.is_gt))
            link(v.tensor_tensor(dinv_in[:, :], stat[:, 0, :], stat[:, 1, :], ALU.mult))
            link(v.tensor_scalar(stat[:, 2, :], hist[:, 1, :], 1.0, None, ALU.max))
            ask()
            link(v.reciprocal(dinv_out[:, :], stat[:, 3, :]))

            def per_node(s):
                return s.unsqueeze(2).to_broadcast([P, NB, D])

            ft3 = FT[:, :].rearrange("p (b f) -> p b f", b=NB)

            def layernorm():
                link(v.tensor_reduce(stat[:, 0, :], X[:, :, :], AX, ALU.add))
                link(v.tensor_scalar(stat[:, 0, :], stat[:, 0, :], 1.0 / D, None, ALU.mult))
                link(v.tensor_tensor(HN[:, :, :], X[:, :, :], per_node(stat[:, 0, :]), ALU.subtract))
                link(v.tensor_tensor(ft3, HN[:, :, :], HN[:, :, :], ALU.mult))
                link(v.tensor_reduce(stat[:, 1, :], ft3, AX, ALU.add))
                link(v.tensor_scalar(stat[:, 2, :], stat[:, 1, :], 1.0 / D, EPS, ALU.mult, ALU.add))
                ask()
                link(v.reciprocal(stat[:, 4, :], stat[:, 3, :]))
                link(v.tensor_tensor(HN[:, :, :], HN[:, :, :], per_node(stat[:, 4, :]), ALU.mult))
                link(v.tensor_scalar(HN[:, :, :], HN[:, :, :], 0.0, None, ALU.max))
                dve.sem_inc(s_feat, 1)

            def onehots(k, g, q):
                to = OHB[:, q % 2, :, :] if PASSES[k] == "score" else OH[:, q % RING, :, :]
                if PASSES[k] == "score":
                    b = groups_before(k, ("score", "attn"))
                    if there(g - 2):
                        dve.wait_ge(s_tp, b + g - 1)
                elif there(g - RING):
                    dve.wait_ge(s_part, groups_before(k, ("sum", "attn")) + g - RING + 1)
                v.tensor_tensor(to, iota[:, 0:P].unsqueeze(1).to_broadcast([P, G, P]),
                                recS[:, bass.ds(G * g, G), R_DST].unsqueeze(2).to_broadcast([P, G, P]),
                                ALU.is_equal).then_inc(s_oh, 1)

            def block_regs(g):
                _, vals = nc.values_load_multi_w_load_instructions(
                    blk_i[0:1, bass.ds(G * g, G)], engines=[dve.engine], min_val=0, max_val=NB - 1,
                    skip_runtime_bounds_check_because="the table holds min(count of blocks, NB - 1)")
                return vals

            def split(parts, x, residue):
                link(v.tensor_copy(parts[0], x))
                link(v.tensor_tensor(residue, x, parts[0], ALU.subtract))
                link(v.tensor_copy(parts[1], residue))
                link(v.tensor_tensor(parts[2], residue, parts[1], ALU.subtract))

            def sum_pass(k, weighted):
                own = groups_before(k, ("sum",))
                parts = groups_before(k, ("sum", "attn"))

                def prepare(g, q):
                    onehots(k, g, q)
                    dve.wait_ge(s_oh, GROUPS * k + g + 1)
                    if weighted:
                        o = OH[:, q % RING, :, :]
                        v.tensor_tensor(o, o, recS[:, bass.ds(G * g, G), R_W].unsqueeze(2).to_broadcast([P, G, P]),
                                        ALU.mult).then_inc(s_ohw, 1)
                    else:
                        dve.sem_inc(s_ohw, 1)

                link(v.memset(ACC[:, :], 0.0))
                prepare(0, 0)
                for i in rounds(dve, ITERS):
                    for q in range(RING):
                        g = RING * i + q
                        vals = block_regs(g)
                        if there(g + 1):
                            prepare(g + 1, q + 1)
                        dve.wait_ge(s_part, parts + g + 1)
                        dve.sem_inc(s_rowfree, 1)
                        for j in range(G):
                            acc = ACC[:, bass.ds(vals[j] * AW, D)]
                            dve.wait_ge(s_acc, G * (parts + g) + j) if (parts or there(g - 1) or j) else None
                            v.tensor_tensor(acc, acc, bank[4 + 2 * (q % 2) + j // 4][:, (j % 4) * P:(j % 4 + 1) * P], ALU.add).then_inc(s_acc, 1)
                dve.wait_ge(s_acc, G * (parts + GROUPS))

            def score_pass(k):
                b16 = groups_before(k, ("score",)) // 2
                bg_ = groups_before(k, ("score", "attn"))

                def scores(g, i, q):
                    r = rows[:, q, :, :]
                    sg = sg16[:, q // 2, (q % 2) * G:(q % 2 + 1) * G, :]
                    dve.wait_ge(s_got, bg_ + g + 1)
                    if q % 2 == 0 and (b16 or there(g - 4)):
                        dve.wait_ge(s_sl, b16 + 2 * i + q // 2 - 1)
                    dve.wait_ge(s_rows[q], 16 * G * (k * ITERS + i + 1))
                    if k == 2:
                        v.tensor_reduce(sm[:, :, 4:8], bank[2][:, 0:12 * G].rearrange("p (t s h) -> p t h s", s=3, h=4), AX, ALU.add).then_inc(s_prod, 1)
                        dve.wait_ge(s_prod, 2 * b16 + g + 1)
                        v.tensor_tensor(sm[:, :, 0:4], sm[:, :, 4:8], r[:, :, 0:4], ALU.add).then_inc(s_edge, 1)
                        dve.wait_ge(s_edge, 2 * g + 1)
                        dve.sem_inc(s_rowfree, 1)
                        v.tensor_tensor(sm[:, :, 4:8], sm[:, :, 0:4], recS[:, bass.ds(G * g, G), R_E:R_E + 4], ALU.add).then_inc(s_edge, 1)
                        dve.wait_ge(s_edge, 2 * g + 2)
                        v.scalar_tensor_tensor(sg[:, :, 0:4], sm[:, :, 4:8], 0.2, sm[:, :, 4:8], ALU.mult, ALU.max).then_inc(s_sg, 1)
                    else:
                        for c in range(2):
                            v.tensor_tensor(msg[:, 4 * c:4 * c + 4, 0:D], bank[4 + c][:, :].rearrange("p (t f) -> p t f", t=4),
                                            r[:, 4 * c:4 * c + 4, :], ALU.mult).then_inc(s_cmp, 1)
                        dve.wait_ge(s_cmp, 3 * GROUPS + 2 * g + 2)
                        dve.sem_inc(s_prod, 1)
                        dve.sem_inc(s_rowfree, 1)
                        v.tensor_reduce(sg, msg[:, :, 0:D].rearrange("p t (h d) -> p t h d", h=H), AX, ALU.add).then_inc(s_sg, 1)
                    dve.wait_ge(s_sg, 2 * b16 + g + 1)

                def pair_starts(p):
                    if b16 or there(p - 1):
                        dve.wait_ge(s_rowT, b16 + p)
                    v.tensor_copy(dl16[:, :, :], recS[:, bass.ds(2 * G * p, 2 * G), R_DST].unsqueeze(2).to_broadcast([P, 2 * G, H])).then_inc(s_dl, 1)

                def pair_onehots(p):
                    if b16 or there(p - 1):
                        dve.wait_ge(s_mpart, b16 + p)
                    v.tensor_tensor(OH16, iota[:, 0:P].unsqueeze(1).to_broadcast([P, 2 * G, P]),
                                    recS[:, bass.ds(2 * G * p, 2 * G), R_DST].unsqueeze(2).to_broadcast([P, 2 * G, P]),
                                    ALU.is_equal).then_inc(s_oh16, 1)

                def runs(p):
                    n = b16 + p
                    dve.wait_ge(s_dlT, n + 1)
                    v.tensor_tensor(edge_of[:, 1:P], dlT[:, 1:P], dlT[:, 0:P - 1], ALU.not_equal).then_inc(s_fwd, 1)
                    dve.wait_ge(s_fwd, 3 * n + 1)
                    v.tensor_scalar(rst[:, :], edge_of[:, 0:P], -BIG, None, ALU.mult).then_inc(s_fwd, 1)
                    dve.wait_ge(s_fwd, 3 * n + 2)
                    v.tensor_tensor_scan(fwd[:, :], rst[:, :], bank[3][:, P:2 * P], 0.0, ALU.add, ALU.max).then_inc(s_fwd, 1)
                    dve.wait_ge(s_fwd, 3 * n + 3)
                    if b16 or there(p - 1):
                        dve.wait_ge(s_runTT, n)
                    v.tensor_tensor(runmax[:, :], fwd[:, :], edge_of[:, 1:P + 1], ALU.mult).then_inc(s_runT, 1)

                def split_runs(p):
                    n = b16 + p
                    run = bank[3][:, 2 * P:3 * P].rearrange("p (t h) -> p t h", h=H)
                    res = res1[:, :].rearrange("p (t h) -> p t h", h=H)
                    dve.wait_ge(s_runTT, n + 1)
                    if b16 or there(p - 1):
                        dve.wait_ge(s_mpart, n)
                    v.tensor_copy(ms3[:, :, 0, :], run).then_inc(s_split, 1)
                    dve.wait_ge(s_split, 3 * n + 1)
                    v.tensor_tensor(res, run, ms3[:, :, 0, :], ALU.subtract).then_inc(s_split, 1)
                    dve.wait_ge(s_split, 3 * n + 2)
                    v.tensor_copy(ms3[:, :, 1, :], res).then_inc(s_split, 1)
                    dve.wait_ge(s_split, 3 * n + 3)
                    v.tensor_tensor(ms3[:, :, 2, :], res, ms3[:, :, 1, :], ALU.subtract).then_inc(s_ms3, 1)

                def tile_maxima(p):
                    n = b16 + p
                    dve.wait_ge(s_mpart, n + 1)
                    v.tensor_scalar(pen[:, :], bank[6][:, 0:2 * G], 1.0, -1.0, ALU.min, ALU.add).then_inc(s_pen, 1)
                    dve.wait_ge(s_pen, n + 1)
                    v.scalar_tensor_tensor(MT[:, bass.ds(2 * G * H * p, 2 * G * H)].rearrange("p (t h) -> p t h", h=H),
                                           pen[:, :].unsqueeze(2).to_broadcast([P, 2 * G, H]), BIG,
                                           bank[7][:, 0:2 * G * H].rearrange("p (t h) -> p t h", h=H), ALU.mult, ALU.add).then_inc(s_mt, 1)

                onehots(k, 0, 0)
                for i in rounds(dve, ITERS):
                    for q in range(RING):
                        g = RING * i + q
                        if there(g + 1):
                            onehots(k, g + 1, q + 1)
                        if q % 2 == 0 and there(g - 4):
                            tile_maxima(2 * i + q // 2 - 2)
                        scores(g, i, q)
                        if q % 2:
                            pair_starts(2 * i + q // 2)
                        if there(g - 2):
                            if q % 2 == 0:
                                pair_onehots(2 * i + q // 2 - 1)
                                runs(2 * i + q // 2 - 1)
                            else:
                                split_runs(2 * i + q // 2 - 1)
                tile_maxima(PAIRS - 2)
                pair_onehots(PAIRS - 1)
                runs(PAIRS - 1)
                split_runs(PAIRS - 1)
                tile_maxima(PAIRS - 1)
                dve.wait_ge(s_mt, b16 + PAIRS)
                mt3 = MT[:, :].rearrange("p (t h) -> p t h", h=H)
                s3 = key[:, :]
                for h in range(4 if k == 2 else H):
                    link(v.tensor_tensor_scan(s3, mreset[:, :], mt3[:, :, h], 0.0, ALU.add, ALU.max))
                    link(v.tensor_copy(mt3[:, :, h], s3))
                for b0 in range(0, NB, G):
                    n = min(G, NB - b0)
                    _, lasts = nc.values_load_multi_w_load_instructions(
                        tlast_i[0:1, b0:b0 + n], engines=[dve.engine], min_val=0, max_val=TILES - 1,
                        skip_runtime_bounds_check_because="a block's last tile lies between 0 and TILES - 1")
                    for j in range(n):
                        ins = v.tensor_copy(M[:, H * (b0 + j):H * (b0 + j + 1)], MT[:, bass.ds(lasts[j] * H, H)])
                        if j == n - 1:
                            link(ins)
                        else:
                            ins.then_inc(s_mall, 1)
                dve.wait_ge(s_mall, (NB - (NB + G - 1) // G) * (1 if k == 2 else 2))
                if k == 2:
                    link(v.tensor_scalar(M[:, :], M[:, :], 0.0, None, ALU.max))
                    link(v.tensor_scalar(stat[:, 0, :], hist[:, 0, :], 1.0, None, ALU.min))
                    link(v.tensor_tensor(m3[:, :, :], m3[:, :, :], stat[:, 0, :].unsqueeze(2).to_broadcast([P, NB, H]), ALU.mult))
                split([m3p[:, :, s_, :] for s_ in range(3)], m3[:, :, :], MT[:, 0:NB * H].rearrange("p (b h) -> p b h", h=H))
                dve.sem_inc(s_feat, 1)

            def attn_pass(k):
                b = groups_before(k, ("attn",))
                bg_ = groups_before(k, ("score", "attn"))
                parts = groups_before(k, ("sum", "attn"))
                heads = 4 if k == 3 else 8
                w = D // heads

                def add_parts(g, vals):
                    dve.wait_ge(s_part, parts + g + 1)
                    for j in range(G):
                        acc = ACC[:, bass.ds(vals[j] * AW, AW)]
                        dve.wait_ge(s_acc, G * (parts + g) + j)
                        v.tensor_tensor(acc, acc, bank[4 + j // 3][:, (j % 3) * AW:(j % 3 + 1) * AW], ALU.add).then_inc(s_acc, 1)

                link(v.memset(ACC[:, :], 0.0))
                onehots(k, 0, 0)
                for i in rounds(dve, ITERS):
                    for q in range(RING):
                        g = RING * i + q
                        vals = block_regs(g - 1) if there(g - 1) else None
                        if there(g + 1):
                            onehots(k, g + 1, q + 1)
                        n = 3 * (b + g)
                        dve.wait_ge(s_got, bg_ + g + 1)
                        got3 = sm3[:, :, :]
                        v.tensor_reduce(got3, bank[2][:, 0:3 * G * H].rearrange("p (t s h) -> p t h s", s=3, h=H), AX, ALU.add).then_inc(s_d16, 1)
                        dve.wait_ge(s_d16, 2 * (b + g) + 1)
                        v.tensor_tensor(got3, S[:, bass.ds(G * H * g, G * H)].rearrange("p (t h) -> p t h", h=H), got3, ALU.subtract).then_inc(s_d16, 1)
                        dve.wait_ge(s_d16, 2 * (b + g) + 2)
                        if b or there(g - 1):
                            dve.wait_ge(s_ex, b + g)
                        v.tensor_scalar(sm[:, :, :], got3, 60.0, None, ALU.min).then_inc(s_sm, 1)
                        dve.wait_ge(s_ex, b + g + 1)
                        dve.wait_ge(s_rows[q], 16 * G * (k * ITERS + i + 1))
                        dve.sem_inc(s_gate, 1)
                        v.tensor_tensor(msg[:, :, 0:D].rearrange("p t (h d) -> p t h d", h=heads),
                                        rows[:, q, :, :].rearrange("p t (h d) -> p t h d", h=heads),
                                        msg[:, :, D:D + heads].unsqueeze(3).to_broadcast([P, G, heads, w]), ALU.mult).then_inc(s_msg, 1)
                        if there(g - 1):
                            add_parts(g - 1, vals)
                        dve.wait_ge(s_msg, b + g + 1)
                        dve.sem_inc(s_rowfree, 1)
                add_parts(GROUPS - 1, block_regs(GROUPS - 1))
                dve.wait_ge(s_acc, G * (parts + GROUPS))

            dve.wait_ge(s_load_x, 32)
            dve.wait_ge(s_load_w, 16 * 42)
            dve.wait_ge(s_uemm, 2)
            link(v.tensor_copy(ust[:, :], bank[7][:, 8:16]))
            layernorm()
            ev = lambda stage: dve.wait_ge(s_ev_chunk, CH0[stage + 1])
            for layer in range(3):
                ev(2 + 3 * layer)
                for c in range(7):
                    link(v.bn_stats(bnst[:, c, :], ZT[:, c * 512:min(N, c * 512 + 512)]))
                link(v.bn_aggr(bnv[:, 0:2], bnst[:, :, :].rearrange("p a b -> p (a b)")))
                link(v.tensor_scalar(bnv[:, 2:3], bnv[:, 1:2], EPS, None, ALU.add))
                ask()
                link(v.reciprocal(bnv[:, 4:5], bnv[:, 3:4]))
                link(v.tensor_tensor(bnv[:, 5:6], bnv[:, 4:5], cols[:, 3 + layer:4 + layer], ALU.mult))
                link(v.tensor_tensor(bnv[:, 7:8], bnv[:, 0:1], bnv[:, 5:6], ALU.mult))
                link(v.tensor_tensor(bnv[:, 6:7], cols[:, 6 + layer:7 + layer], bnv[:, 7:8], ALU.subtract))
                ask()
                if layer:
                    link(v.tensor_tensor(HT, HT, FT[:, :], ALU.add))
                dve.sem_inc(s_feat, 1)
                ev(3 + 3 * layer)
                if layer < 2:
                    link(v.tensor_tensor(TAB[:, :, 0:D], HN[:, :, :], per_node(dinv_in[:, :]), ALU.mult))
                    dve.sem_inc(s_table, 1)
                    sum_pass(layer, True)
                    link(v.tensor_tensor(HN[:, :, :], acc3[:, :, 0:D], per_node(dinv_in[:, :]), ALU.mult))
                    dve.sem_inc(s_feat, 1)
            link(v.tensor_tensor(X[:, :, :], X[:, :, :], HN[:, :, :], ALU.add))
            layernorm()
            ev(11)
            split([at3[:, :, s_, :] for s_ in range(3)], TAB[:, :, D + 4:D + 8], M[:, 0:4 * NB].rearrange("p (b h) -> p b h", h=4))
            dve.sem_inc(s_feat, 1)
            dve.sem_inc(s_table, 1)
            dve.sem_inc(s_table, 1)
            score_pass(2)
            attn_pass(3)
            ask()
            link(v.tensor_scalar(stat[:, 0, :], hist[:, 0, :], -1.0, float(E), ALU.mult, ALU.add))
            link(v.tensor_tensor(stat[:, 4:8, :], stat[:, 4:8, :], stat[:, 0, :].unsqueeze(1).to_broadcast([P, 4, NB]), ALU.mult))
            den = acc3[:, :, D:D + 4]
            link(v.tensor_tensor(den, den, stat[:, 4:8, :].rearrange("p h b -> p b h"), ALU.add))
            link(v.reciprocal(den, den))
            for h in range(4):
                link(v.tensor_tensor(HN[:, :, 32 * h:32 * h + 32], acc3[:, :, 32 * h:32 * h + 32],
                                     acc3[:, :, D + h:D + h + 1].to_broadcast([P, NB, 32]), ALU.mult))
            link(v.tensor_tensor(X[:, :, :], X[:, :, :], HN[:, :, :], ALU.add))
            layernorm()
            ev(13)
            dve.sem_inc(s_table, 1)
            dve.sem_inc(s_table, 1)
            split([q_.rearrange("p (b f) -> p b f", b=NB) for q_ in q3], QKV[:, :, 0:D], acc3[:, :, 0:D])
            dve.sem_inc(s_feat, 1)
            score_pass(4)
            attn_pass(5)
            den = acc3[:, :, D:AW]
            link(v.tensor_scalar(den, den, 1.0e-30, None, ALU.max))
            link(v.reciprocal(den, den))
            for h in range(8):
                link(v.tensor_tensor(HN[:, :, 16 * h:16 * h + 16], acc3[:, :, 16 * h:16 * h + 16],
                                     acc3[:, :, D + h:D + h + 1].to_broadcast([P, NB, 16]), ALU.mult))
            dve.sem_inc(s_feat, 1)
            ev(15)
            link(v.tensor_tensor(X[:, :, :], X[:, :, :], HN[:, :, :], ALU.add))
            layernorm()
            for layer in range(2):
                ev(17 + 2 * layer)
                link(v.tensor_tensor(ft3, HN[:, :, :], wgb[:, layer:layer + 1, :].to_broadcast([P, NB, D]), ALU.mult))
                link(v.tensor_reduce(stat[:, 0, :], ft3, AX, ALU.add))
                ask()
                link(v.tensor_tensor(stat[:, 1, :], stat[:, 1, :], dinv_out[:, :], ALU.mult))
                link(v.tensor_tensor(TAB[:, :, 0:D], HN[:, :, :], per_node(stat[:, 1, :]), ALU.mult))
                dve.sem_inc(s_table, 1)
                sum_pass(6 + layer, False)
                link(v.tensor_tensor(ft3, acc3[:, :, 0:D], per_node(dinv_out[:, :]), ALU.mult))
                link(v.tensor_tensor(HN[:, :, :], HN[:, :, :], ft3, ALU.add))
                link(v.tensor_scalar(HN[:, :, :], HN[:, :, :], 0.0, None, ALU.max))
                dve.sem_inc(s_feat, 1)
            link(v.tensor_tensor(X[:, :, :], X[:, :, :], HN[:, :, :], ALU.add))
            dve.sem_inc(s_table, 1)


_INS = ['x', 'src', 'dst', 'edge_attr_64', 'edge_weight', 'L0_gnn_fc_w', 'L0_gnn_fc_b', 'L0_gnn_conv_w', 'L0_gnn_conv_b',
        'L0_gnn_bn_gamma', 'L0_gnn_bn_beta', 'L1_gnn_W_node', 'L1_gnn_W_edge', 'L1_gnn_a', 'L2_gnn_Wq', 'L2_gnn_bq',
        'L2_gnn_Wk', 'L2_gnn_bk', 'L2_gnn_Wv', 'L2_gnn_bv', 'L2_gnn_Wo', 'L2_gnn_bo', 'L3_gnn_Wt', 'L3_gnn_bt',
        'L3_gnn_Wg', 'L3_gnn_bg']


def kernel(**inputs):
    import numpy as _np
    import concourse.bacc as _bacc
    from concourse import mybir as _mybir
    from concourse.bass_utils import run_bass_kernel_spmd as _run

    nc = _bacc.Bacc("TRN2", target_bir_lowering=False, num_devices=1)
    arrays, args = {}, []
    for name in _INS:
        a = _np.ascontiguousarray(inputs[name])
        arrays[f"in_{name}_dram"] = a
        args.append(nc.dram_tensor(f"in_{name}_dram", a.shape, _mybir.dt.from_np(a.dtype), kind="ExternalInput").ap())
    args.append(nc.dram_tensor("out_dram", (N, D), _mybir.dt.float32, kind="ExternalOutput").ap())
    gnn_kernel(nc, *args)
    r = _run(nc, [arrays], core_ids=[0])
    return r.results[0]["out_dram"]
```

```python
import concourse.bass as bass
from concourse import mybir
from contextlib import ExitStack

F32 = mybir.dt.float32
BF16 = mybir.dt.bfloat16
I32 = mybir.dt.int32
U32 = mybir.dt.uint32
ALU = mybir.AluOpType
ACT = mybir.ActivationFunctionType
AX = mybir.AxisListType.X

P = 128
D = 128
N = 3125
E = 50000
NB = (N + P - 1) // P
NP = NB * P
TAIL = N - (NB - 1) * P
LANES = 125
COLS = E // LANES
TILES = (E // P + NB + 15) // 16 * 16
G = 8
PAIRS = TILES // (2 * G)
GROUPS = TILES // G
RING = 4
ITERS = GROUPS // RING
REC = 8
R_SRC, R_DST, R_W, R_E = 0, 1, 2, 4
H = 8
AW = D + H
BIG = 1.0e30
EPS = 1e-5
F_MAX = 3.4028234e38

PASSES = ["sum", "sum", "score", "attn", "score", "attn", "sum", "sum"]


def groups_before(k, kinds):
    return sum(GROUPS for q in PASSES[:k] if q in kinds)


def steps(eng, n):
    yield 0
    with eng.Fori(1, n, 1) as i:
        yield i


def rounds(eng, n):
    yield 0
    with eng.Fori(1, n - 1, 1) as i:
        yield i
    yield n - 1


def edge_loads(eng):
    for i in range(3):
        yield i, i % 2, i // 2 + 1
    with eng.Fori(0, (COLS // 16 - 5) // 2, 1) as j:
        yield 2 * j + 3, 1, j + 2
        yield 2 * j + 4, 0, j + 3
    for i in range(COLS // 16 - 2, COLS // 16):
        yield i, i % 2, i // 2 + 1


def there(g, before=GROUPS):
    return not isinstance(g, int) or 0 <= g < before


def gnn_kernel(nc, x, src, dst, edge_attr, edge_weight, fc_w, fc_b, conv_w, conv_b, bn_gamma, bn_beta,
               W_node, W_edge, a_vec, Wq, bq, Wk, bk, Wv, bv, Wo, bo, Wt, bt, Wg, bg, out):
    ctx = ExitStack()
    with ctx:
        def sb(name, shape, dt=F32):
            return ctx.enter_context(nc.sbuf_tensor(name, shape, dt))

        def sem(name):
            return ctx.enter_context(nc.semaphore(name))

        rec_dram = nc.dram_tensor("rec_dram", (P * TILES, REC), F32).ap()
        tab_dram = [nc.dram_tensor(f"tab{k}_dram", (N, 4 if k == 2 else D), F32).ap() for k in range(len(PASSES))]

        lane_i = sb("lane_i", [P, 1], I32)
        iota = sb("iota", [P, 512])
        lane = sb("lane", [P, 1])
        ident = sb("ident", [P, P])
        tri = sb("tri", [P, P])
        ones = sb("ones", [P, P])
        X = sb("X", [P, NB, D])
        HN = sb("HN", [P, NB, D])
        FT = sb("FT", [P, NP])
        big = sb("big", [P, 3 * NB * D + NB * 8])
        ZT = big[:, 0:NP]
        HT = big[:, NP:2 * NP]
        TAB = big[:, 2 * NP:2 * NP + NB * AW].rearrange("p (b f) -> p b f", b=NB)
        QKV = big[:, 0:3 * NP].rearrange("p (b f) -> p b f", b=NB)
        ACC = sb("ACC", [P, NB * AW])
        acc3 = ACC[:, :].rearrange("p (b f) -> p b f", b=NB)
        M = sb("M", [P, NB * H])
        m3 = M[:, :].rearrange("p (b h) -> p b h", b=NB)
        stat = sb("stat", [P, 8, NB])
        lnst = M[:, 0:NB * 6].rearrange("p (b s) -> p b s", s=6)
        meanvar = stat[:, 0:2, :].rearrange("p a b -> p (a b)").rearrange("p (b s) -> p b s", s=2)
        bnst = sb("bnst", [P, 7, 6])
        bnv = sb("bnv", [P, 8])
        hist = sb("hist", [P, 2, NB])
        dinv_in = sb("dinv_in", [P, NB])
        dinv_out = sb("dinv_out", [P, NB])
        wraw = sb("wraw", [P, 7, D])
        wT = sb("wT", [P, 8, D])
        wfc = sb("wfc", [P, 3, D])
        ust = sb("ust", [P, 8])
        wedge = sb("wedge", [P, 2, 64])
        abd = sb("abd", [P, 12])
        ue2 = sb("ue2", [P, 8])
        cols = sb("cols", [P, 9])
        brow = sb("brow", [1, 6, D])
        wgb = sb("wgb", [P, 2, D])
        bgb = sb("bgb", [P, 2])
        recS = sb("recS", [P, TILES, REC])
        S = sb("S", [P, TILES * H])
        recU = S[:, :].rearrange("p (t r) -> p t r", r=REC)
        key = sb("key", [P, TILES])
        blk_i = sb("blk_i", [P, TILES], I32)
        MT = sb("MT", [P, TILES * H])
        rec = MT[0:LANES, 0:COLS * REC].rearrange("p (c r) -> p c r", r=REC)
        e_dst = FT[0:LANES, 0:COLS].bitcast(I32)
        e_src = FT[0:LANES, COLS:2 * COLS].bitcast(I32)
        e_w = FT[0:LANES, 2 * COLS:3 * COLS]
        e_int = FT[0:LANES, 3 * COLS:4 * COLS].bitcast(I32)
        e_blk = ACC[0:LANES, 0 * COLS:1 * COLS]
        e_sblk = ACC[0:LANES, 1 * COLS:2 * COLS]
        e_sloc = ACC[0:LANES, 2 * COLS:3 * COLS]
        e_pos = ACC[0:LANES, 3 * COLS:4 * COLS]
        e_rank = ACC[0:LANES, 4 * COLS:5 * COLS]
        e_row = ACC[0:LANES, 5 * COLS:6 * COLS].bitcast(U32)
        tot = sb("tot", [LANES, NB])
        base_pos = sb("base_pos", [LANES, NB])
        tcount = sb("tcount", [P, 4, NB])
        tcount_i = sb("tcount_i", [P, NB], I32)
        tblk = sb("tblk", [P, TILES])
        hn1 = HN[:, :, :].rearrange("p b f -> p (b f)")
        ea = hn1[0:LANES, 0:2048].rearrange("p (a f) -> p a f", a=2)
        eaT = hn1[:, 2048:2048 + 8 * LANES].rearrange("p (a f) -> p a f", a=2)
        stg = sb("stg", [P, RING, G], U32)
        stg_rec = sb("stg_rec", [LANES, 2, G, REC])
        rows = sb("rows", [P, RING, G, D])
        iota_i = rows[:, 0, 0:4, :].rearrange("p a f -> p (a f)").bitcast(I32)
        OH = sb("OH", [P, RING, G, P])
        OHT32 = sb("OHT32", [P, G, P])
        OHT = OHT32[:, :, :].rearrange("p t n -> p (t n)").bitcast(BF16)[:, 0:G * P].rearrange("p (t n) -> p t n", n=P)
        ohw = OH[:, :, :, :].rearrange("p a t n -> p (a t n)").bitcast(BF16)
        OHB = ohw[:, 0:2 * G * P].rearrange("p (a t n) -> p a t n", a=2, n=P)
        OH16 = ohw[:, 2 * G * P:4 * G * P].rearrange("p (t n) -> p t n", n=P)
        sortw = big[:, 2 * NP:2 * NP + 3 * G * P].bitcast(BF16).rearrange("p (u a t n) -> p u a t n", u=3, a=2, n=P)
        dgb, signs, permb = sortw[:, 0], sortw[:, 1], sortw[:, 2]
        rec3 = [FT[:, 0:TILES * REC // 2].bitcast(BF16), ZT[:, 0:TILES * REC // 2].bitcast(BF16), hn1[:, 0:TILES * REC // 2].bitcast(BF16)]
        onesb = sb("onesb", [P, P], BF16)
        c128b = sb("c128b", [P, P], BF16)
        lane_diag = sb("lane_diag", [P, 4, P], BF16)
        iota2 = sb("iota2", [P, P])
        sgnsum = sb("sgnsum", [P, 2, G])
        identb = sb("identb", [P, P], BF16)
        at3 = sb("at3", [P, NB, 3, 4], BF16)
        m3p = sb("m3p", [P, NB, 3, H], BF16)
        ms3 = sb("ms3", [P, 2 * G, 3, H], BF16)
        res1 = sb("res1", [P, 2 * G * H])
        cnt1 = sb("cnt1", [P, 1], BF16)
        q3 = [FT[:, 0:NP // 2].bitcast(BF16), FT[:, NP // 2:NP].bitcast(BF16), hn1[:, 0:NP // 2].bitcast(BF16)]
        mreset = sb("mreset", [P, TILES])
        tlast_i = sb("tlast_i", [P, NB], I32)
        msg = sb("msg", [P, G, AW])
        msgs = [msg[:, :, :], FT[:, 0:G * AW].rearrange("p (t f) -> p t f", f=AW)]
        sg16 = sb("sg16", [P, 2, 2 * G, H])
        dl16 = sb("dl16", [P, 2 * G, H])
        dlT = sb("dlT", [P, P])
        edge_of = sb("edge_of", [P, P + 1])
        rst = sb("rst", [P, P])
        fwd = sb("fwd", [P, P])
        runmax = sb("runmax", [P, P])
        pen = sb("pen", [P, 2 * G])
        sm = sb("sm", [P, G, H])
        sm3 = sb("sm3", [P, G, H])
        ohlo = ohw[0:LANES, :]
        inside = rows[0:LANES, :, :, :].rearrange("p a t f -> p (a t f)")[:, 0:5 * COLS].bitcast(I32).rearrange("p (c e) -> p c e", e=COLS)
        ranks = OH[0:LANES, :, :, :].rearrange("p a t f -> p (a t f)")[:, 0:5 * COLS].rearrange("p (c e) -> p c e", e=COLS)
        ohhi = sb("ohhi", [LANES, 2, G, NB], BF16)

        bank = [ctx.enter_context(nc.psum_tensor(f"bank{i}", [P, 512], F32)) for i in range(8)]

        s_iota = sem("s_iota")
        s_load_x = sem("s_load_x")
        s_load_a = sem("s_load_a")
        s_load_w = sem("s_load_w")
        s_load_e = sem("s_load_e")
        s_consts = sem("s_consts")
        s_abd0 = sem("s_abd0")
        s_tot = sem("s_tot")
        s_pre = sem("s_pre")
        s_rank = sem("s_rank")
        s_masked = sem("s_masked")
        s_placed = sem("s_placed")
        s_recbase = sem("s_recbase")
        s_recinit = sem("s_recinit")
        s_recdef = sem("s_recdef")
        s_uemm = sem("s_uemm")
        s_ue = sem("s_ue")
        s_ea = [sem(f"s_ea{i}") for i in range(2)]
        s_eaT = sem("s_eaT")
        s_eaTc = sem("s_eaTc")
        s_es = sem("s_es")
        s_esc = sem("s_esc")
        s_sstage = [sem(f"s_sstage{i}") for i in range(2)]
        s_scat = [sem(f"s_scat{i}") for i in range(2)]
        s_hoh = sem("s_hoh")
        s_hmm = sem("s_hmm")
        s_hacc = sem("s_hacc")
        s_recl = sem("s_recl")
        s_dg = sem("s_dg")
        s_keyb = sem("s_keyb")
        s_cmp = sem("s_cmp")
        s_rk = sem("s_rk")
        s_perm = sem("s_perm")
        s_sorted = sem("s_sorted")
        s_sign = sem("s_sign")
        s_recs = sem("s_recs")
        s_pe_chunk = sem("s_pe_chunk")
        s_ev_chunk = sem("s_ev_chunk")
        s_table = sem("s_table")
        s_stored = [sem(f"s_stored{k}") for k in range(len(PASSES))]
        s_stage = sem("s_stage")
        s_gate = sem("s_gate")
        s_rows = [sem(f"s_rows{i}") for i in range(RING)]
        s_rowfree = sem("s_rowfree")
        s_oh = sem("s_oh")
        s_ohw = sem("s_ohw")
        s_part = sem("s_part")
        s_bank = sem("s_bank")
        s_acc = sem("s_acc")
        s_tp = sem("s_tp")
        s_oht = sem("s_oht")
        s_got = sem("s_got")
        s_prod = sem("s_prod")
        s_sg = sem("s_sg")
        s_sl = sem("s_sl")
        s_dl = sem("s_dl")
        s_rowT = sem("s_rowT")
        s_dlT = sem("s_dlT")
        s_edge = sem("s_edge")
        s_fwd = sem("s_fwd")
        s_runT = sem("s_runT")
        s_runTT = sem("s_runTT")
        s_ms3 = sem("s_ms3")
        s_split = sem("s_split")
        s_d16 = sem("s_d16")
        s_mall = sem("s_mall")
        s_oh16 = sem("s_oh16")
        s_mpart = sem("s_mpart")
        s_pen = sem("s_pen")
        s_mt = sem("s_mt")
        s_sm = sem("s_sm")
        s_ex = sem("s_ex")
        s_msg = sem("s_msg")
        s_feat = sem("s_feat")
        s_sq_in = sem("s_sq_in")
        s_sq_out = sem("s_sq_out")
        s_dve = sem("s_dve")
        s_act = sem("s_act")
        s_out = sem("s_out")

        block = ctx.enter_context(nc.Block())

        ea_v = edge_attr.rearrange("(p c) f -> p (c f)", p=LANES)

        def records(k):
            return recU if k == 0 else recS

        def transposed(k, q):
            if PASSES[k] == "score":
                return bank[q][:, 0:2 * P].bitcast(BF16)
            return bank[q][:, :]

        T_CH = [(c, min(4, NB - 4 * c)) for c in range((NB + 3) // 4)]
        L1_CH = [(c, min(3, NB - 3 * c)) for c in range((NB + 2) // 3)]
        STAGES = [("wT", 2), ("T", 7), ("Z", 7), ("T", 7),
                  ("T", 7), ("Z", 7), ("T", 7),
                  ("T", 7), ("Z", 7), ("T", 7),
                  ("T", 7), ("L1", len(L1_CH)),
                  ("T", 7), ("QKV", NB),
                  ("T", 7), ("O", 7),
                  ("T", 7), ("O", 7),
                  ("T", 7), ("O", 7)]
        CH0 = [sum(n for _, n in STAGES[:k]) for k in range(len(STAGES) + 1)]

        @block.sync
        def _(sp):
            sp.dma_start(e_dst[:, :], dst.rearrange("(p c) -> p c", p=LANES)).then_inc(s_load_e, 16)
            sp.dma_start(e_src[:, :], src.rearrange("(p c) -> p c", p=LANES)).then_inc(s_load_e, 16)
            sp.dma_start(e_w[:, :], edge_weight.rearrange("(p c) -> p c", p=LANES)).then_inc(s_load_e, 16)
            for k in range(2):
                sp.dma_start(wedge[:, k, :], W_edge).then_inc(s_load_a, 16)
            sp.wait_ge(s_abd0, 1)
            for part in range(3):
                for h in range(4):
                    sp.dma_start(abd[32 * h:32 * h + 32, 4 * part + h:4 * part + h + 1],
                                 a_vec[h, 32 * part:32 * part + 32].rearrange("(p o) -> p o", o=1)).then_inc(s_load_a, 16)
            for i in range(2):
                sp.dma_start(ea[:, i, :], ea_v[:, i * 1024:(i + 1) * 1024]).then_inc(s_ea[i], 16)
            sp.wait_ge(s_consts, 1)
            sp.dma_start(X[:, 0:NB - 1, :], x[0:(NB - 1) * P, :].rearrange("(b p) f -> p b f", p=P)).then_inc(s_load_x, 16)
            sp.dma_start(X[0:TAIL, NB - 1, :], x[(NB - 1) * P:N, :]).then_inc(s_load_x, 16)
            sp.wait_ge(s_recdef, 1)
            sp.dma_start(rec_dram.rearrange("(p t) r -> p (t r)", p=P), recS[:, :, :].rearrange("p t r -> p (t r)")).then_inc(s_recinit, 16)
            sp.wait_ge(s_placed, 1)
            for i in steps(sp, COLS // 16):
                for half in range(2):
                    sp.wait_ge(s_esc, 2 * i + half + 1)
                    sp.sem_inc(s_gate, 1)
                    if not isinstance(i, int):
                        sp.wait_ge(s_scat[half], 16 * G * i)
                    sp.dma_start(stg_rec[:, half, :, :], rec[:, bass.ds(G * (2 * i + half), G), :]).then_inc(s_sstage[half], 16)
                    sp.dma_start(stg[0:LANES, half, :], e_row[:, bass.ds(G * (2 * i + half), G)]).then_inc(s_sstage[half], 16)
            for half in range(2):
                sp.wait_ge(s_scat[half], 16 * G * (COLS // 16))
            sp.dma_start(recU.rearrange("p t r -> p (t r)"), rec_dram.rearrange("(p t) r -> p (t r)", p=P)).then_inc(s_recl, 16)
            TABS = {0: TAB[:, :, 0:D], 1: TAB[:, :, 0:D], 2: TAB[:, :, D:D + 4], 3: TAB[:, :, 0:D],
                    4: QKV[:, :, D:2 * D], 5: QKV[:, :, 2 * D:3 * D], 6: TAB[:, :, 0:D], 7: TAB[:, :, 0:D]}
            for k in range(len(PASSES)):
                sp.wait_ge(s_table, k + 1)
                t = TABS[k]
                sp.dma_start(tab_dram[k][0:(NB - 1) * P, :].rearrange("(b p) f -> p b f", p=P), t[:, 0:NB - 1, :]).then_inc(s_stored[k], 16)
                sp.dma_start(tab_dram[k][(NB - 1) * P:N, :], t[0:TAIL, NB - 1, :]).then_inc(s_stored[k], 16)
            sp.wait_ge(s_table, len(PASSES) + 1)
            sp.dma_start(out[0:(NB - 1) * P, :].rearrange("(b p) f -> p b f", p=P), X[:, 0:NB - 1, :]).then_inc(s_out, 16)
            sp.dma_start(out[(NB - 1) * P:N, :], X[0:TAIL, NB - 1, :]).then_inc(s_out, 16)
            sp.wait_ge(s_out, 32)
            for k in range(len(PASSES)):
                sp.wait_ge(s_stored[k], 32)

        @block.gpsimd
        def _(pool):
            nc.gpsimd.iota(iota_i[:, :], pattern=[[1, 512]], base=0, channel_multiplier=0).then_inc(s_iota, 1)
            nc.gpsimd.iota(lane_i[:, :], pattern=[[0, 1]], base=0, channel_multiplier=1).then_inc(s_iota, 1)
            pool.wait_ge(s_recinit, 16)
            for i in steps(pool, COLS // 16):
                for half in range(2):
                    pool.wait_ge(s_sstage[half], 32 * (i + 1))
                    pool.sem_inc(s_gate, 1)
                    for j in range(G):
                        nc.gpsimd.indirect_dma_start(
                            rec_dram, bass.IndirectOffsetOnAxis(ap=stg[0:LANES, half, j:j + 1], axis=0),
                            stg_rec[:, half, j, :], None).then_inc(s_scat[half], 16)
            pool.wait_ge(s_recl, 16)
            for k in range(len(PASSES)):
                pool.wait_ge(s_stored[k], 32)
                if k == 1:
                    pool.wait_ge(s_recs, 1)
                width = 4 if k == 2 else D
                for i in steps(pool, ITERS):
                    for q in range(RING):
                        g = RING * i + q
                        if k or not isinstance(i, int):
                            pool.wait_ge(s_rowfree, k * GROUPS + g - RING + 1)
                            pool.wait_ge(s_rows[q], 16 * G * (k * ITERS + i))
                            pool.sem_inc(s_gate, 1)
                        nc.gpsimd.tensor_copy(stg[:, q, :], records(k)[:, bass.ds(G * g, G), R_SRC]).then_inc(s_stage, 1)
                        pool.wait_ge(s_stage, k * GROUPS + g + 1)
                        pool.sem_inc(s_gate, 1)
                        for j in range(G):
                            nc.gpsimd.indirect_dma_start(
                                rows[:, q, j, 0:width], None, tab_dram[k],
                                bass.IndirectOffsetOnAxis(ap=stg[:, q, j:j + 1], axis=0)).then_inc(s_rows[q], 16)

        @block.scalar
        def _(act):
            done = [0]
            chunks = [0]
            for k, w in enumerate([W_node, Wq, Wk, Wv, Wo, Wt[0], Wt[1]]):
                act.dma_start(wraw[:, k, :], w).then_inc(s_load_w, 16)
            for k, w in enumerate([fc_w, conv_w[0], conv_w[1]]):
                act.dma_start(wfc[:, k, :], w).then_inc(s_load_w, 16)
            for k, v in enumerate([fc_b, conv_b[0], conv_b[1], bn_gamma[0], bn_gamma[1], bn_gamma[2],
                                   bn_beta[0], bn_beta[1], bn_beta[2]]):
                act.dma_start(cols[:, k:k + 1], v.rearrange("(p o) -> p o", o=1)).then_inc(s_load_w, 16)
            for k, v in enumerate([bq, bk, bv, bo, bt[0], bt[1]]):
                act.dma_start(brow[:, k, :], v.rearrange("(o f) -> o f", o=1)).then_inc(s_load_w, 16)
            for k in range(2):
                act.dma_start(wgb[:, k, :], Wg[k].rearrange("(o f) -> o f", o=1).broadcast_to([P, D])).then_inc(s_load_w, 16)
            act.dma_start(bgb[:, :], bg.rearrange("(o f) -> o f", o=1).broadcast_to([P, 2])).then_inc(s_load_w, 16)

            def link(ins):
                done[0] += 1
                ins.then_inc(s_act, 1)
                act.wait_ge(s_act, done[0])

            def evac(dst_ap, src_ap, func=ACT.Copy, **kw):
                act.wait_ge(s_pe_chunk, chunks[0] + 1)
                nc.scalar.activation(dst_ap, src_ap, func, **kw).then_inc(s_ev_chunk, 1)
                chunks[0] += 1

            def bank_of():
                return bank[chunks[0] % 2]

            def transposes(to):
                for c, n in T_CH:
                    evac(to(c, n), bank_of()[:, 0:n * P])

            def feat(c, n):
                return FT[:, c * 512:c * 512 + n * P]

            def back(c, n):
                return HN[:, 4 * c:4 * c + n, :].rearrange("p b f -> p (b f)")

            act.wait_ge(s_uemm, 1)
            act.wait_ge(s_consts, 1)
            link(nc.scalar.activation(ue2[0:64, 0:4], bank[7][0:64, 0:4], ACT.Copy))
            link(nc.scalar.activation(ue2[64:128, 4:8], bank[7][64:128, 0:4], ACT.Copy))
            act.sem_inc(s_ue, 1)
            act.wait_ge(s_recbase, 1)

            def edge_scores(g, half):
                act.wait_ge(s_es, g + 1)
                act.sem_inc(s_gate, 1)
                nc.scalar.activation(rec[:, bass.ds(G * g, G), R_E:R_E + 4],
                                     bank[2 + half][0:LANES, 0:32].rearrange("p (c h) -> p c h", h=4), ACT.Copy).then_inc(s_esc, 1)

            for i, buf, loads in edge_loads(act):
                for half in range(2):
                    g = 2 * i + half
                    act.wait_ge(s_eaT, g + 1)
                    if half and there(i + 2, COLS // 16):
                        act.dma_start(ea[:, buf, :], ea_v[:, bass.ds((i + 2) * 1024, 1024)]).then_inc(s_ea[buf], 16)
                    if there(g - 2):
                        act.wait_ge(s_es, g - 1)
                    nc.scalar.activation(eaT[:, half, :], bank[half][:, 0:4 * LANES], ACT.Copy).then_inc(s_eaTc, 1)
                    if there(g - 1):
                        edge_scores(g - 1, 1 - half)
            edge_scores(COLS // G - 1, 1)

            def sort_records():
                def keep(g, half):
                    act.wait_ge(s_sorted, g + 1)
                    act.sem_inc(s_gate, 1)
                    nc.scalar.activation(recS[:, bass.ds(G * g, G), :],
                                         bank[2 + half][:, 0:G * REC].rearrange("p (t r) -> p t r", r=REC), ACT.Copy).then_inc(s_perm, 1)

                for i in steps(act, PAIRS):
                    for half in range(2):
                        g = 2 * i + half
                        act.wait_ge(s_keyb, g + 1)
                        if not isinstance(i, int):
                            act.wait_ge(s_rk, g - 1)
                            act.wait_ge(s_sign, G * (g - 1))
                        act.sem_inc(s_gate, 1)
                        for j in range(G):
                            nc.scalar.activation(signs[:, half, j, :], bank[j // 4][:, (j % 4) * P:(j % 4 + 1) * P], ACT.Sign,
                                                 scale=-1.0, bias=key[:, bass.ds(G * g + j, 1)],
                                                 accum_out=sgnsum[:, half, j:j + 1]).then_inc(s_sign, 1)
                        if there(g - 1):
                            keep(g - 1, 1 - half)
                keep(GROUPS - 1, 1)
                act.wait_ge(s_perm, GROUPS)
                act.sem_inc(s_recs, 1)

            asks = [0]

            def answer(dst_ap, src_ap, func, **kw):
                act.wait_ge(s_sq_in, asks[0] + 1)
                nc.scalar.activation(dst_ap, src_ap, func, **kw).then_inc(s_sq_out, 1)
                asks[0] += 1

            def root():
                answer(stat[:, 3, :], stat[:, 2, :], ACT.Sqrt)

            def oht_copies(k, g):
                b = groups_before(k, ("score", "attn"))
                act.wait_ge(s_tp, b + g + 1)
                if b or there(g - 1):
                    act.wait_ge(s_got, b + g)
                act.sem_inc(s_gate, 1)
                for q in range(2):
                    nc.scalar.activation(OHT[:, 4 * q:4 * q + 4, :].rearrange("p t n -> p (t n)"),
                                         transposed(k, q), ACT.Copy).then_inc(s_oht, 1)

            def score_pass(k):
                b16 = groups_before(k, ("score",)) // 2

                def keep_scores(p, half):
                    act.wait_ge(s_sg, 2 * (b16 + p) + 2)
                    act.sem_inc(s_gate, 1)
                    nc.scalar.activation(S[:, bass.ds(2 * G * H * p, 2 * G * H)],
                                         sg16[:, half, :, :].rearrange("p t h -> p (t h)"), ACT.Copy).then_inc(s_sl, 1)

                def destinations(p):
                    act.wait_ge(s_rowT, b16 + p + 1)
                    if b16 or there(p - 1):
                        act.wait_ge(s_runT, b16 + p)
                    act.sem_inc(s_gate, 1)
                    nc.scalar.activation(dlT[:, :], bank[3][:, 0:P], ACT.Copy).then_inc(s_dlT, 1)

                oht_copies(k, 0)
                for i in rounds(act, ITERS):
                    for q in range(RING):
                        g = RING * i + q
                        if there(g + 1):
                            oht_copies(k, g + 1)
                        if q % 2 == 1:
                            keep_scores(2 * i + q // 2, q // 2)
                        elif there(g - 2):
                            destinations(2 * i + q // 2 - 1)
                destinations(PAIRS - 1)

            def attn_pass(k):
                b = groups_before(k, ("attn",))
                oht_copies(k, 0)
                for i in rounds(act, ITERS):
                    for q in range(RING):
                        g = RING * i + q
                        act.wait_ge(s_sm, b + g + 1)
                        if there(g - 2):
                            act.wait_ge(s_part, groups_before(k, ("sum", "attn")) + g - 1)
                        act.sem_inc(s_gate, 1)
                        nc.scalar.activation(msgs[q % 2][:, :, D:AW], sm[:, :, :], ACT.Exp).then_inc(s_ex, 1)
                        if there(g + 1):
                            oht_copies(k, g + 1)

            for c, n in enumerate([4, 3]):
                evac(wT[:, 4 * c:4 * c + n, :].rearrange("p b f -> p (b f)"), bank_of()[:, 0:n * P])
            root(); root()
            root()
            transposes(feat)
            for layer in range(3):
                for c, n in T_CH:
                    evac(ZT[:, c * 512:c * 512 + n * P], bank_of()[:, 0:n * P], ACT.Identity, bias=cols[:, layer:layer + 1])
                answer(bnv[:, 3:4], bnv[:, 2:3], ACT.Sqrt)
                answer(HT if layer == 0 else FT[:, :], ZT, ACT.Relu, scale=bnv[:, 5:6], bias=bnv[:, 6:7])
                transposes(back)
                if layer == 0:
                    sort_records()
                if layer < 2:
                    transposes(feat)
            root()
            transposes(feat)
            for c, n in L1_CH:
                evac(TAB[:, 3 * c:3 * c + n, :].rearrange("p b f -> p (b f)"), bank_of()[:, 0:n * AW])
            score_pass(2)
            attn_pass(3)
            answer(stat[:, 4:8, :].rearrange("p h b -> p b h"), m3[:, :, 0:4], ACT.Exp, scale=-1.0)
            root()
            transposes(feat)
            for c in range(NB):
                act.wait_ge(s_pe_chunk, chunks[0] + 1)
                link(nc.scalar.activation(QKV[:, c, 0:D], bank_of()[:, 0:D], ACT.Copy, scale=0.25))
                nc.scalar.activation(QKV[:, c, D:3 * D], bank_of()[:, D:3 * D], ACT.Copy).then_inc(s_ev_chunk, 1)
                chunks[0] += 1
            score_pass(4)
            attn_pass(5)
            transposes(feat)
            for c, n in T_CH:
                evac(HN[:, 4 * c:4 * c + n, :].rearrange("p b f -> p (b f)"), bank_of()[:, 0:n * P])
            root()
            for layer in range(2):
                transposes(feat)
                for c, n in T_CH:
                    evac(HN[:, 4 * c:4 * c + n, :].rearrange("p b f -> p (b f)"), bank_of()[:, 0:n * P])
                answer(stat[:, 1, :], stat[:, 0, :], ACT.Tanh, bias=bgb[:, layer:layer + 1])
            assert chunks[0] == CH0[-1]

        @block.tensor
        def _(pe):
            chunks = [0]

            def chunk(fill):
                if chunks[0] >= 2:
                    pe.wait_ge(s_ev_chunk, chunks[0] - 1)
                fill(bank[chunks[0] % 2]).then_inc(s_pe_chunk, 1)
                chunks[0] += 1

            feats = [0]

            def need_feat():
                feats[0] += 1
                pe.wait_ge(s_feat, feats[0])

            def transposes(src_of):
                for c, n in T_CH:
                    def fill(b):
                        for q in range(n):
                            last = nc.tensor.transpose(b[:, q * P:(q + 1) * P], src_of(4 * c + q), ident[:, :])
                        return last
                    chunk(fill)

            def node(b):
                return HN[:, b, :]

            def product_T(w):
                pe.wait_ge(s_ev_chunk, chunks[0])
                for c, n in T_CH:
                    chunk(lambda b: nc.tensor.matmul(b[:, 0:n * P], w, FT[:, c * 512:c * 512 + n * P], start=True, stop=True))

            def fblock(b):
                return FT[:, b * P:(b + 1) * P]

            def product_bias(w, bias):
                pe.wait_ge(s_ev_chunk, chunks[0])
                for c, n in T_CH:
                    def fill(b):
                        for q in range(n):
                            nc.tensor.matmul(b[:, q * P:(q + 1) * P], fblock(4 * c + q), w, start=True, stop=False)
                            last = nc.tensor.matmul(b[:, q * P:(q + 1) * P], ones[0:1, :], bias, start=False, stop=True)
                        return last
                    chunk(fill)

            def prefixes():
                pe.wait_ge(s_tot, NB)
                nc.tensor.matmul(bank[6][:, 0:NB], tri[0:LANES, :], tot[:, :], start=True, stop=True)
                nc.tensor.matmul(bank[6][:, 32:32 + NB], ones[0:LANES, :], tot[:, :], start=True, stop=True).then_inc(s_pre, 1)

            pe.wait_ge(s_consts, 1)
            pe.wait_ge(s_load_a, 16 * 14)
            nc.tensor.matmul(bank[7][:, 0:4], wedge[:, :, :].rearrange("p a f -> p (a f)"), abd[:, 8:12], start=True, stop=True).then_inc(s_uemm, 1)
            pe.wait_ge(s_ue, 1)

            def edge_transposes(g, half, buf):
                if there(g - 2):
                    pe.wait_ge(s_eaTc, g - 1)
                for j in range(4):
                    last = nc.tensor.transpose(bank[half][:, j * LANES:(j + 1) * LANES],
                                               ea[:, buf, half * 512 + j * P:half * 512 + (j + 1) * P], ident[0:LANES, 0:LANES])
                last.then_inc(s_eaT, 1)

            def edge_products(g, half):
                pe.wait_ge(s_eaTc, g + 1)
                if there(g - 2):
                    pe.wait_ge(s_esc, g - 1)
                for j in range(4):
                    last = nc.tensor.matmul(bank[2 + half][0:LANES, 8 * j:8 * j + 8],
                                            eaT[:, half, j * LANES:(j + 1) * LANES], ue2[:, :], start=True, stop=True)
                last.then_inc(s_es, 1)

            for i, buf, loads in edge_loads(pe):
                pe.wait_ge(s_ea[buf], 16 * loads)
                edge_transposes(2 * i, 0, buf)
                if there(2 * i - 1):
                    edge_products(2 * i - 1, 1)
                edge_transposes(2 * i + 1, 1, buf)
                edge_products(2 * i, 0)
                if isinstance(i, int) and i == 2:
                    prefixes()
            edge_products(COLS // G - 1, 1)
            for i in steps(pe, COLS // G // 2):
                for both in range(2):
                    for kind in range(2):
                        pe.wait_ge(s_hoh, 4 * i + 2 * both + kind + 1)
                        if kind == 0 and both + (0 if isinstance(i, int) else 1):
                            pe.wait_ge(s_hacc, 2 * i + both)
                        for j in range(G):
                            last = nc.tensor.matmul(bank[6][:, kind * 32 + 64:kind * 32 + 64 + NB],
                                                    ohlo[:, kind * 1024 + j * P:kind * 1024 + (j + 1) * P],
                                                    ohhi[:, kind, j, :], start=(j == 0), stop=(j == G - 1))
                        last.then_inc(s_hmm, 1)
            def sort_keys(g, half):
                pe.wait_ge(s_dg, g + 1)
                if there(g - 1):
                    pe.wait_ge(s_sign, G * g)
                for q in range(2):
                    nc.tensor.matmul(bank[q][:, :], onesb[:, :], lane_diag[:, :, :].rearrange("p t n -> p (t n)"),
                                     start=True, stop=False)
                    last = nc.tensor.matmul(bank[q][:, :], c128b[:, :],
                                            dgb[:, half, 4 * q:4 * q + 4, :].rearrange("p t n -> p (t n)"), start=False, stop=True)
                last.then_inc(s_keyb, 1)

            def sort_products(g, half):
                pe.wait_ge(s_rk, g + 1)
                if there(g - 2):
                    pe.wait_ge(s_perm, g - 1)
                for j in range(G):
                    for part in range(3):
                        last = nc.tensor.matmul(bank[2 + half][:, REC * j:REC * (j + 1)], permb[:, half, j, :],
                                                rec3[part][:, bass.ds(REC * (G * g + j), REC)], start=(part == 0), stop=(part == 2))
                last.then_inc(s_sorted, 1)

            def onehot_transposes(k, g, slot):
                b = groups_before(k, ("score", "attn"))
                pe.wait_ge(s_oh, GROUPS * k + g + 1)
                if b or there(g - 1):
                    pe.wait_ge(s_oht, 2 * (b + g))
                for j in range(G):
                    one, i_ = (OHB[:, slot % 2, j, :], identb) if PASSES[k] == "score" else (OH[:, slot, j, :], ident)
                    last = nc.tensor.transpose(transposed(k, j // 4)[:, (j % 4) * P:(j % 4 + 1) * P], one, i_[:, :])
                last.then_inc(s_tp, 1)
                pe.wait_ge(s_oht, 2 * (b + g) + 2)

            def block_regs(g):
                _, vals = nc.values_load_multi_w_load_instructions(
                    blk_i[0:1, bass.ds(G * g, G)], engines=[pe.engine], min_val=0, max_val=NB - 1,
                    skip_runtime_bounds_check_because="the table holds min(count of blocks, NB - 1)")
                return vals

            def sum_pass(k):
                own = groups_before(k, ("sum",))
                parts = groups_before(k, ("sum", "attn"))
                if k == 0:
                    pe.wait_ge(s_ev_chunk, chunks[0])
                for i in steps(pe, ITERS):
                    for q in range(RING):
                        g = RING * i + q
                        pe.wait_ge(s_ohw, own + g + 1)
                        if parts or there(g - 2):
                            pe.wait_ge(s_acc, G * (parts + g - 1))
                        pe.wait_ge(s_rows[q], 16 * G * (k * ITERS + i + 1))
                        for j in range(G):
                            last = nc.tensor.matmul(bank[4 + 2 * (q % 2) + j // 4][:, (j % 4) * P:(j % 4 + 1) * P], OH[:, q, j, :],
                                                    rows[:, q, j, :], start=True, stop=True)
                        last.then_inc(s_part, 1)
                        if k == 0:
                            sort_keys(g, q % 2)
                            if there(g - 1):
                                sort_products(g - 1, 1 - q % 2)
                if k == 0:
                    sort_products(GROUPS - 1, 1)

            def score_pass(k):
                b16 = groups_before(k, ("score",)) // 2

                def fetch(g, q):
                    vals = block_regs(g)
                    onehot_transposes(k, g, q)
                    if b16 or there(g - 1):
                        pe.wait_ge(s_prod, 2 * b16 + g)
                    for j in range(G):
                        if k == 2:
                            last = nc.tensor.matmul(bank[2][:, 12 * j:12 * j + 12], OHT[:, j, :],
                                                    at3[:, bass.ds(vals[j], 1), :, :].rearrange("p b s h -> p (b s h)"), start=True, stop=True)
                        else:
                            for s_ in range(3):
                                last = nc.tensor.matmul(bank[4 + j // 4][:, (j % 4) * P:(j % 4 + 1) * P], OHT[:, j, :],
                                                        q3[s_][:, bass.ds(vals[j] * D, D)], start=(s_ == 0), stop=(s_ == 2))
                    last.then_inc(s_got, 1)

                def turn(p, sl):
                    pe.wait_ge(s_dl, b16 + p + 1)
                    pe.wait_ge(s_sg, 2 * (b16 + p) + 2)
                    if b16 or there(p - 1):
                        pe.wait_ge(s_fwd, 3 * (b16 + p))
                        pe.wait_ge(s_dlT, b16 + p)
                    pe.sem_inc(s_gate, 1)
                    nc.tensor.transpose(bank[3][:, 0:P], dl16[:, :, :].rearrange("p t h -> p (t h)"), ident[:, :])
                    nc.tensor.transpose(bank[3][:, P:2 * P], sg16[:, sl, :, :].rearrange("p t h -> p (t h)"), ident[:, :]).then_inc(s_rowT, 1)

                def maxima(p):
                    pe.wait_ge(s_runT, b16 + p + 1)
                    if b16 or there(p - 1):
                        pe.wait_ge(s_ms3, b16 + p)
                    pe.sem_inc(s_gate, 1)
                    nc.tensor.transpose(bank[3][:, 2 * P:3 * P], runmax[:, :], ident[:, :]).then_inc(s_runTT, 1)
                    pe.wait_ge(s_ms3, b16 + p + 1)
                    pe.wait_ge(s_oh16, b16 + p + 1)
                    if b16 or there(p - 1):
                        pe.wait_ge(s_mt, b16 + p)
                    for j in range(2 * G):
                        for s_ in range(3):
                            nc.tensor.matmul(bank[7][:, H * j:H * j + H], OH16[:, j, :], ms3[:, j, s_, :], start=(s_ == 0), stop=(s_ == 2))
                        last = nc.tensor.matmul(bank[6][:, j:j + 1], OH16[:, j, :], cnt1[:, :], start=True, stop=True)
                    last.then_inc(s_mpart, 1)

                fetch(0, 0)
                for i in rounds(pe, ITERS):
                    for q in range(RING):
                        g = RING * i + q
                        if there(g + 1):
                            fetch(g + 1, q + 1)
                        if there(g - 2):
                            if q % 2 == 0:
                                turn(2 * i + q // 2 - 1, (q // 2 + 1) % 2)
                            else:
                                maxima(2 * i + q // 2 - 1)
                turn(PAIRS - 1, (PAIRS - 1) % 2)
                maxima(PAIRS - 1)

            def attn_pass(k):
                b = groups_before(k, ("attn",))
                parts = groups_before(k, ("sum", "attn"))

                def fetch(g, q):
                    vals = block_regs(g)
                    onehot_transposes(k, g, q % RING)
                    if b or there(g - 1):
                        pe.wait_ge(s_sm, b + g)
                    for j in range(G):
                        last = nc.tensor.matmul(bank[2][:, 3 * H * j:3 * H * (j + 1)], OHT[:, j, :],
                                                m3p[:, bass.ds(vals[j], 1), :, :].rearrange("p b s h -> p (b s h)"), start=True, stop=True)
                    last.then_inc(s_got, 1)

                fetch(0, 0)
                for i in rounds(pe, ITERS):
                    for q in range(RING):
                        g = RING * i + q
                        if there(g + 1):
                            fetch(g + 1, q + 1)
                        pe.wait_ge(s_msg, b + g + 1)
                        for j in range(G):
                            if j % 3 == 0:
                                pe.wait_ge(s_acc, G * (parts + g - 1) + min(j + 3, G))
                            last = nc.tensor.matmul(bank[4 + j // 3][:, (j % 3) * AW:(j % 3 + 1) * AW], OH[:, q, j, :],
                                                    msgs[q % 2][:, j, :], start=True, stop=True)
                            if j in (2, 5):
                                last.then_inc(s_bank, 1)
                        last.then_inc(s_part, 1)

            pe.wait_ge(s_load_w, 16 * 28)
            pe.wait_ge(s_esc, COLS // G)
            for c, n in enumerate([4, 3]):
                def fill(b):
                    for q in range(n):
                        last = nc.tensor.transpose(b[:, q * P:(q + 1) * P], wraw[:, 4 * c + q, :], ident[:, :])
                    return last
                chunk(fill)
            nc.tensor.matmul(bank[7][:, 8:16], wraw[:, 0, :], abd[:, 0:8], start=True, stop=True).then_inc(s_uemm, 1)
            need_feat()
            transposes(node)
            for layer in range(3):
                product_T(wfc[:, layer, :])
                need_feat()
                transposes(lambda b: HT[:, b * P:(b + 1) * P])
                if layer < 2:
                    sum_pass(layer)
                    need_feat()
                    transposes(node)
            need_feat()
            transposes(node)
            pe.wait_ge(s_ev_chunk, chunks[0])
            for c, n in L1_CH:
                def fill(b):
                    for q in range(n):
                        nc.tensor.matmul(b[:, q * AW:q * AW + D], fblock(3 * c + q), wT[:, 0, :], start=True, stop=True)
                        last = nc.tensor.matmul(b[:, q * AW + D:(q + 1) * AW], fblock(3 * c + q), ust[:, :], start=True, stop=True)
                    return last
                chunk(fill)
            need_feat()
            score_pass(2)
            need_feat()
            attn_pass(3)
            need_feat()
            transposes(node)
            pe.wait_ge(s_ev_chunk, chunks[0])
            for c in range(NB):
                def fill(b):
                    nc.tensor.matmul(b[:, 0:3 * D], fblock(c), wT[:, 1:4, :].rearrange("p a f -> p (a f)"), start=True, stop=False)
                    return nc.tensor.matmul(b[:, 0:3 * D], ones[0:1, :], brow[:, 0:3, :].rearrange("p a f -> p (a f)"), start=False, stop=True)
                chunk(fill)
            need_feat()
            score_pass(4)
            need_feat()
            attn_pass(5)
            need_feat()
            transposes(node)
            product_bias(wT[:, 4, :], brow[:, 3, :])
            for layer in range(2):
                need_feat()
                transposes(node)
                product_bias(wT[:, 5 + layer, :], brow[:, 4 + layer, :])
                sum_pass(6 + layer)
            assert chunks[0] == CH0[-1]

        @block.vector
        def _(dve):
            done = [0]
            asked = [0]
            v = nc.vector

            def link(ins):
                done[0] += 1
                ins.then_inc(s_dve, 1)
                dve.wait_ge(s_dve, done[0])

            def queued(ins):
                done[0] += 1
                ins.then_inc(s_dve, 1)

            def ask():
                dve.sem_inc(s_sq_in, 1)
                asked[0] += 1
                dve.wait_ge(s_sq_out, asked[0])

            link(v.memset(abd[:, :], 0.0))
            dve.sem_inc(s_abd0, 1)
            dve.wait_ge(s_iota, 2)
            link(v.tensor_copy(iota[:, :], iota_i[:, :]))
            link(v.tensor_copy(lane[:, :], lane_i[:, :]))
            link(v.tensor_scalar(ident[:, :], iota[:, 0:P], lane[:, 0:1], None, ALU.is_equal))
            link(v.tensor_scalar(tri[:, :], iota[:, 0:P], lane[:, 0:1], None, ALU.is_gt))
            link(v.memset(ones[:, :], 1.0))
            link(v.memset(ue2[:, :], 0.0))
            link(v.memset(X[:, NB - 1, :], 0.0))
            link(v.memset(edge_of[:, :], 1.0))
            link(v.memset(cnt1[:, :], 1.0))
            link(v.tensor_copy(identb[:, :], ident[:, :]))
            link(v.memset(sg16[:, :, :, :], 0.0))
            link(v.memset(hist[:, :, :], 0.0))
            link(v.memset(onesb[:, :], 1.0))
            link(v.memset(c128b[:, :], float(P)))
            link(v.tensor_scalar(lane_diag[:, :, :], ident[:, :].unsqueeze(1).to_broadcast([P, 4, P]), lane[:, 0:1], None, ALU.mult))
            link(v.tensor_scalar(iota2[:, :], iota[:, 0:P], 2.0, -float(P - 1), ALU.mult, ALU.add))
            dve.sem_inc(s_consts, 1)
            link(v.memset(recS[:, :, :], 0.0))
            link(v.memset(recS[:, :, R_DST], float(P)))
            dve.sem_inc(s_recdef, 1)

            dve.wait_ge(s_load_e, 48)
            link(v.memset(rec[:, :, :], 0.0))
            dve.sem_inc(s_recbase, 1)
            for ends, blk, loc in ((e_dst, e_blk[:, :], rec[:, :, R_DST]), (e_src, e_sblk[:, :], e_sloc[:, :])):
                link(v.tensor_single_scalar(e_int[:, :], ends[:, :], 7, ALU.arith_shift_right))
                link(v.tensor_copy(blk, e_int[:, :]))
                link(v.tensor_copy(e_rank[:, :], ends[:, :]))
                link(v.scalar_tensor_tensor(loc, blk, -float(P), e_rank[:, :], ALU.mult, ALU.add))
            link(v.tensor_copy(rec[:, :, R_SRC], e_rank[:, :]))
            link(v.tensor_scalar(e_rank[:, :], e_w[:, :], F_MAX, None, ALU.is_le))
            link(v.scalar_tensor_tensor(e_int[:, :], e_w[:, :], -F_MAX, e_rank[:, :], ALU.is_ge, ALU.mult))
            link(v.copy_predicated(rec[:, :, R_W], e_int[:, :], e_w[:, :]))
            scratch = [e_rank[:, :], e_pos[:, :]]
            with dve.Fori(0, NB // 5, 1) as b5:
                for c in range(5):
                    b = 5 * b5 + c
                    v.tensor_scalar(scratch[c % 2], e_blk[:, :], iota[0:LANES, bass.ds(b, 1)], 0.0, ALU.is_equal, ALU.add,
                                    accum_out=tot[:, bass.ds(b, 1)]).then_inc(s_tot, 1)
                    if c:
                        dve.wait_ge(s_tot, b)
                dve.wait_ge(s_tot, 5 * b5 + 5)
            dve.wait_ge(s_pre, 1)
            link(v.tensor_scalar(tcount_i[:, :], bank[6][:, 32:32 + NB], float(P - 1), None, ALU.add))
            link(v.tensor_single_scalar(tcount_i[:, :], tcount_i[:, :], 7, ALU.arith_shift_right))
            link(v.tensor_copy(tcount[:, 0, :], tcount_i[:, :]))
            link(v.memset(tcount[:, 3, :], 0.0))
            link(v.tensor_tensor_scan(tcount[:, 1, :], tcount[:, 3, :], tcount[:, 0, :], 0.0, ALU.add, ALU.add))
            link(v.tensor_tensor(tcount[:, 2, :], tcount[:, 1, :], tcount[:, 0, :], ALU.subtract))
            link(v.tensor_scalar(tcount[:, 2, :], tcount[:, 2, :], float(P), -1.0, ALU.mult, ALU.add))
            link(v.tensor_tensor(base_pos[:, :], bank[6][0:LANES, 0:NB], tcount[0:LANES, 2, :], ALU.add))
            link(v.memset(e_pos[:, :], 0.0))
            link(v.memset(e_w[:, :], 0.0))
            with dve.Fori(0, NB // 5, 1) as b5:
                for c in range(5):
                    v.tensor_scalar(inside[:, c, :], e_blk[:, :], iota[0:LANES, bass.ds(5 * b5 + c, 1)], None, ALU.is_equal).then_inc(s_rank, 1)
                for c in range(5):
                    dve.wait_ge(s_rank, 15 * b5 + c + 1)
                    v.tensor_tensor_scan(ranks[:, c, :], e_w[:, :], inside[:, c, :], base_pos[:, bass.ds(5 * b5 + c, 1)],
                                         ALU.add, ALU.add).then_inc(s_rank, 1)
                for c in range(5):
                    dve.wait_ge(s_rank, 15 * b5 + 10 + c)
                    dve.sem_inc(s_gate, 1)
                    v.copy_predicated(e_pos[:, :], inside[:, c, :], ranks[:, c, :]).then_inc(s_rank, 1)
                dve.wait_ge(s_rank, 15 * b5 + 15)
            link(v.tensor_copy(e_int[:, :], e_pos[:, :]))
            link(v.tensor_single_scalar(e_int[:, :], e_int[:, :], 7, ALU.arith_shift_right))
            link(v.tensor_copy(e_rank[:, :], e_int[:, :]))
            link(v.scalar_tensor_tensor(e_pos[:, :], e_rank[:, :], -float(P), e_pos[:, :], ALU.mult, ALU.add))
            link(v.scalar_tensor_tensor(e_row[:, :], e_pos[:, :], float(TILES), e_rank[:, :], ALU.mult, ALU.add))
            dve.sem_inc(s_placed, 1)
            link(v.memset(tblk[:, :], 0.0))
            with dve.Fori(0, NB, 1) as b:
                v.scalar_tensor_tensor(tblk[:, :], iota[:, 0:TILES], tcount[:, 1, bass.ds(b, 1)], tblk[:, :],
                                       ALU.is_ge, ALU.add).then_inc(s_masked, 1)
                dve.wait_ge(s_masked, b + 1)
            link(v.tensor_scalar(tblk[:, :], tblk[:, :], float(NB - 1), None, ALU.min))
            link(v.tensor_copy(blk_i[:, :], tblk[:, :]))
            link(v.tensor_tensor(mreset[:, 1:TILES], tblk[:, 1:TILES], tblk[:, 0:TILES - 1], ALU.not_equal))
            link(v.memset(mreset[:, 0:1], 1.0))
            link(v.tensor_scalar(mreset[:, :], mreset[:, :], -BIG, None, ALU.mult))
            link(v.tensor_scalar(tlast_i[:, :], tcount[:, 1, :], -1.0, 0.0, ALU.add, ALU.max))

            for i in steps(dve, COLS // G // 2):
                for both in range(2):
                    g = 2 * i + both
                    for kind, (blk, loc) in enumerate(((e_blk[:, :], rec[:, :, R_DST]), (e_sblk[:, :], e_sloc[:, :]))):
                        if both + (0 if isinstance(i, int) else 1):
                            dve.wait_ge(s_hmm, 2 * g - 1 + kind)
                        v.tensor_tensor(ohlo[:, kind * 1024:(kind + 1) * 1024].rearrange("p (g n) -> p g n", g=G),
                                        iota[0:LANES, 0:P].unsqueeze(1).to_broadcast([LANES, G, P]),
                                        loc[:, bass.ds(G * g, G)].unsqueeze(2).to_broadcast([LANES, G, P]), ALU.is_equal).then_inc(s_rank, 1)
                        v.tensor_tensor(ohhi[:, kind, :, :],
                                        iota[0:LANES, 0:NB].unsqueeze(1).to_broadcast([LANES, G, NB]),
                                        blk[:, bass.ds(G * g, G)].unsqueeze(2).to_broadcast([LANES, G, NB]), ALU.is_equal).then_inc(s_rank, 1)
                        dve.wait_ge(s_rank, 3 * NB + 4 * g + 2 * kind + 2)
                        dve.sem_inc(s_hoh, 1)
                    dve.wait_ge(s_hmm, 2 * g + 2)
                    v.tensor_tensor(hist[:, :, :], hist[:, :, :],
                                    bank[6][:, 64:128].rearrange("p (k b) -> p k b", k=2)[:, :, 0:NB], ALU.add).then_inc(s_hacc, 1)
                    dve.wait_ge(s_hacc, g + 1)

            link(v.tensor_scalar(stat[:, 2, :], hist[:, 0, :], 1.0, None, ALU.max))
            ask()
            link(v.reciprocal(stat[:, 0, :], stat[:, 3, :]))
            link(v.tensor_scalar(stat[:, 1, :], hist[:, 0, :], 0.0, None, ALU.is_gt))
            link(v.tensor_tensor(dinv_in[:, :], stat[:, 0, :], stat[:, 1, :], ALU.mult))
            link(v.tensor_scalar(stat[:, 2, :], hist[:, 1, :], 1.0, None, ALU.max))
            ask()
            link(v.reciprocal(dinv_out[:, :], stat[:, 3, :]))

            def per_node(s):
                return s.unsqueeze(2).to_broadcast([P, NB, D])

            ft3 = FT[:, :].rearrange("p (b f) -> p b f", b=NB)

            def layernorm():
                for b in range(NB):
                    queued(v.bn_stats(lnst[:, b, :], X[:, b, :]))
                dve.wait_ge(s_dve, done[0])
                for b in range(NB):
                    queued(v.bn_aggr(meanvar[:, b, :], lnst[:, b, :]))
                dve.wait_ge(s_dve, done[0])
                link(v.tensor_scalar(stat[:, 2, :], meanvar[:, :, 1], EPS, None, ALU.add))
                dve.sem_inc(s_sq_in, 1)
                asked[0] += 1
                link(v.tensor_tensor(HN[:, :, :], X[:, :, :], meanvar[:, :, 0:1].to_broadcast([P, NB, D]), ALU.subtract))
                dve.wait_ge(s_sq_out, asked[0])
                link(v.reciprocal(stat[:, 4, :], stat[:, 3, :]))
                link(v.scalar_tensor_tensor(HN[:, :, :], HN[:, :, :], 0.0, per_node(stat[:, 4, :]), ALU.max, ALU.mult))
                dve.sem_inc(s_feat, 1)

            def onehots(k, g, q):
                to = OHB[:, q % 2, :, :] if PASSES[k] == "score" else OH[:, q % RING, :, :]
                if PASSES[k] == "score":
                    b = groups_before(k, ("score", "attn"))
                    if there(g - 2):
                        dve.wait_ge(s_tp, b + g - 1)
                elif there(g - RING):
                    dve.wait_ge(s_part, groups_before(k, ("sum", "attn")) + g - RING + 1)
                v.tensor_tensor(to, iota[:, 0:P].unsqueeze(1).to_broadcast([P, G, P]),
                                records(k)[:, bass.ds(G * g, G), R_DST].unsqueeze(2).to_broadcast([P, G, P]),
                                ALU.is_equal).then_inc(s_oh, 1)

            def block_regs(g):
                _, vals = nc.values_load_multi_w_load_instructions(
                    blk_i[0:1, bass.ds(G * g, G)], engines=[dve.engine], min_val=0, max_val=NB - 1,
                    skip_runtime_bounds_check_because="the table holds min(count of blocks, NB - 1)")
                return vals

            def split(parts, x, residue):
                link(v.tensor_copy(parts[0], x))
                link(v.tensor_tensor(residue, x, parts[0], ALU.subtract))
                link(v.tensor_copy(parts[1], residue))
                link(v.tensor_tensor(parts[2], residue, parts[1], ALU.subtract))

            def diagonals(g, half):
                if there(g - 2):
                    dve.wait_ge(s_keyb, g - 1)
                v.tensor_tensor(dgb[:, half, :, :], ident[:, :].unsqueeze(1).to_broadcast([P, G, P]),
                                recU[:, bass.ds(G * g, G), R_DST].unsqueeze(2).to_broadcast([P, G, P]), ALU.mult).then_inc(s_dg, 1)

            def permutations(g, half):
                dve.wait_ge(s_sign, G * (g + 1))
                if there(g - 2):
                    dve.wait_ge(s_sorted, g - 1)
                v.tensor_tensor(permb[:, half, :, :], iota2[:, :].unsqueeze(1).to_broadcast([P, G, P]),
                                sgnsum[:, half, :].unsqueeze(2).to_broadcast([P, G, P]), ALU.is_equal).then_inc(s_rk, 1)

            def sum_pass(k, weighted):
                own = groups_before(k, ("sum",))
                parts = groups_before(k, ("sum", "attn"))

                def prepare(g, q):
                    onehots(k, g, q)
                    dve.wait_ge(s_oh, GROUPS * k + g + 1)
                    if weighted:
                        o = OH[:, q % RING, :, :]
                        v.tensor_tensor(o, o, records(k)[:, bass.ds(G * g, G), R_W].unsqueeze(2).to_broadcast([P, G, P]),
                                        ALU.mult).then_inc(s_ohw, 1)
                    else:
                        dve.sem_inc(s_ohw, 1)

                if k == 0:
                    dve.wait_ge(s_recl, 16)
                link(v.memset(ACC[:, :], 0.0))
                prepare(0, 0)
                if k == 0:
                    link(v.tensor_scalar(key[:, :], recU[:, :, R_DST], float(P), lane[:, 0:1], ALU.mult, ALU.add))
                    split(rec3, S[:, :], MT[:, 0:TILES * REC])
                    dve.wait_ge(s_stored[0], 32)
                    diagonals(0, 0)
                for i in rounds(dve, ITERS):
                    for q in range(RING):
                        g = RING * i + q
                        vals = block_regs(g)
                        if there(g + 1):
                            prepare(g + 1, q + 1)
                        if k == 0:
                            if there(g + 1):
                                diagonals(g + 1, 1 - q % 2)
                            if there(g - 1):
                                permutations(g - 1, 1 - q % 2)
                        dve.wait_ge(s_part, parts + g + 1)
                        dve.sem_inc(s_rowfree, 1)
                        for j in range(G):
                            acc = ACC[:, bass.ds(vals[j] * AW, D)]
                            if parts or there(g - 1) or j:
                                dve.wait_ge(s_acc, G * (parts + g) + j)
                            v.tensor_tensor(acc, acc, bank[4 + 2 * (q % 2) + j // 4][:, (j % 4) * P:(j % 4 + 1) * P], ALU.add).then_inc(s_acc, 1)
                if k == 0:
                    permutations(GROUPS - 1, 1)
                    dve.wait_ge(s_recs, 1)
                dve.wait_ge(s_acc, G * (parts + GROUPS))

            def score_pass(k):
                b16 = groups_before(k, ("score",)) // 2
                bg_ = groups_before(k, ("score", "attn"))

                def scores(g, i, q):
                    r = rows[:, q, :, :]
                    sg = sg16[:, q // 2, (q % 2) * G:(q % 2 + 1) * G, :]
                    dve.wait_ge(s_got, bg_ + g + 1)
                    if q % 2 == 0 and (b16 or there(g - 4)):
                        dve.wait_ge(s_sl, b16 + 2 * i + q // 2 - 1)
                    dve.wait_ge(s_rows[q], 16 * G * (k * ITERS + i + 1))
                    if k == 2:
                        v.tensor_reduce(sm[:, :, 4:8], bank[2][:, 0:12 * G].rearrange("p (t s h) -> p t h s", s=3, h=4), AX, ALU.add).then_inc(s_prod, 1)
                        dve.wait_ge(s_prod, 2 * b16 + g + 1)
                        v.tensor_tensor(sm[:, :, 0:4], sm[:, :, 4:8], r[:, :, 0:4], ALU.add).then_inc(s_edge, 1)
                        dve.wait_ge(s_edge, 2 * g + 1)
                        dve.sem_inc(s_rowfree, 1)
                        v.tensor_tensor(sm[:, :, 4:8], sm[:, :, 0:4], recS[:, bass.ds(G * g, G), R_E:R_E + 4], ALU.add).then_inc(s_edge, 1)
                        dve.wait_ge(s_edge, 2 * g + 2)
                        v.scalar_tensor_tensor(sg[:, :, 0:4], sm[:, :, 4:8], 0.2, sm[:, :, 4:8], ALU.mult, ALU.max).then_inc(s_sg, 1)
                    else:
                        for c in range(2):
                            v.tensor_tensor(msg[:, 4 * c:4 * c + 4, 0:D], bank[4 + c][:, :].rearrange("p (t f) -> p t f", t=4),
                                            r[:, 4 * c:4 * c + 4, :], ALU.mult).then_inc(s_cmp, 1)
                        dve.wait_ge(s_cmp, 2 * g + 2)
                        dve.sem_inc(s_prod, 1)
                        dve.sem_inc(s_rowfree, 1)
                        v.tensor_reduce(sg, msg[:, :, 0:D].rearrange("p t (h d) -> p t h d", h=H), AX, ALU.add).then_inc(s_sg, 1)
                    dve.wait_ge(s_sg, 2 * b16 + g + 1)

                def pair_starts(p):
                    if b16 or there(p - 1):
                        dve.wait_ge(s_rowT, b16 + p)
                    v.tensor_copy(dl16[:, :, :], recS[:, bass.ds(2 * G * p, 2 * G), R_DST].unsqueeze(2).to_broadcast([P, 2 * G, H])).then_inc(s_dl, 1)

                def pair_onehots(p):
                    if b16 or there(p - 1):
                        dve.wait_ge(s_mpart, b16 + p)
                    v.tensor_tensor(OH16, iota[:, 0:P].unsqueeze(1).to_broadcast([P, 2 * G, P]),
                                    recS[:, bass.ds(2 * G * p, 2 * G), R_DST].unsqueeze(2).to_broadcast([P, 2 * G, P]),
                                    ALU.is_equal).then_inc(s_oh16, 1)

                def runs(p):
                    n = b16 + p
                    dve.wait_ge(s_dlT, n + 1)
                    v.tensor_tensor(edge_of[:, 1:P], dlT[:, 1:P], dlT[:, 0:P - 1], ALU.not_equal).then_inc(s_fwd, 1)
                    dve.wait_ge(s_fwd, 3 * n + 1)
                    v.tensor_scalar(rst[:, :], edge_of[:, 0:P], -BIG, None, ALU.mult).then_inc(s_fwd, 1)
                    dve.wait_ge(s_fwd, 3 * n + 2)
                    v.tensor_tensor_scan(fwd[:, :], rst[:, :], bank[3][:, P:2 * P], 0.0, ALU.add, ALU.max).then_inc(s_fwd, 1)
                    dve.wait_ge(s_fwd, 3 * n + 3)
                    if b16 or there(p - 1):
                        dve.wait_ge(s_runTT, n)
                    v.tensor_tensor(runmax[:, :], fwd[:, :], edge_of[:, 1:P + 1], ALU.mult).then_inc(s_runT, 1)

                def split_runs(p):
                    n = b16 + p
                    run = bank[3][:, 2 * P:3 * P].rearrange("p (t h) -> p t h", h=H)
                    res = res1[:, :].rearrange("p (t h) -> p t h", h=H)
                    dve.wait_ge(s_runTT, n + 1)
                    if b16 or there(p - 1):
                        dve.wait_ge(s_mpart, n)
                    v.tensor_copy(ms3[:, :, 0, :], run).then_inc(s_split, 1)
                    dve.wait_ge(s_split, 3 * n + 1)
                    v.tensor_tensor(res, run, ms3[:, :, 0, :], ALU.subtract).then_inc(s_split, 1)
                    dve.wait_ge(s_split, 3 * n + 2)
                    v.tensor_copy(ms3[:, :, 1, :], res).then_inc(s_split, 1)
                    dve.wait_ge(s_split, 3 * n + 3)
                    v.tensor_tensor(ms3[:, :, 2, :], res, ms3[:, :, 1, :], ALU.subtract).then_inc(s_ms3, 1)

                def tile_maxima(p):
                    n = b16 + p
                    dve.wait_ge(s_mpart, n + 1)
                    v.tensor_scalar(pen[:, :], bank[6][:, 0:2 * G], 1.0, -1.0, ALU.min, ALU.add).then_inc(s_pen, 1)
                    dve.wait_ge(s_pen, n + 1)
                    v.scalar_tensor_tensor(MT[:, bass.ds(2 * G * H * p, 2 * G * H)].rearrange("p (t h) -> p t h", h=H),
                                           pen[:, :].unsqueeze(2).to_broadcast([P, 2 * G, H]), BIG,
                                           bank[7][:, 0:2 * G * H].rearrange("p (t h) -> p t h", h=H), ALU.mult, ALU.add).then_inc(s_mt, 1)

                onehots(k, 0, 0)
                for i in rounds(dve, ITERS):
                    for q in range(RING):
                        g = RING * i + q
                        if there(g + 1):
                            onehots(k, g + 1, q + 1)
                        if q % 2 == 0 and there(g - 4):
                            tile_maxima(2 * i + q // 2 - 2)
                        scores(g, i, q)
                        if q % 2:
                            pair_starts(2 * i + q // 2)
                        if there(g - 2):
                            if q % 2 == 0:
                                pair_onehots(2 * i + q // 2 - 1)
                                runs(2 * i + q // 2 - 1)
                            else:
                                split_runs(2 * i + q // 2 - 1)
                tile_maxima(PAIRS - 2)
                pair_onehots(PAIRS - 1)
                runs(PAIRS - 1)
                split_runs(PAIRS - 1)
                tile_maxima(PAIRS - 1)
                dve.wait_ge(s_mt, b16 + PAIRS)
                mt3 = MT[:, :].rearrange("p (t h) -> p t h", h=H)
                s3 = key[:, :]
                for h in range(4 if k == 2 else H):
                    link(v.tensor_tensor_scan(s3, mreset[:, :], mt3[:, :, h], 0.0, ALU.add, ALU.max))
                    link(v.tensor_copy(mt3[:, :, h], s3))
                for b0 in range(0, NB, G):
                    n = min(G, NB - b0)
                    _, lasts = nc.values_load_multi_w_load_instructions(
                        tlast_i[0:1, b0:b0 + n], engines=[dve.engine], min_val=0, max_val=TILES - 1,
                        skip_runtime_bounds_check_because="a block's last tile lies between 0 and TILES - 1")
                    for j in range(n):
                        ins = v.tensor_copy(M[:, H * (b0 + j):H * (b0 + j + 1)], MT[:, bass.ds(lasts[j] * H, H)])
                        if j == n - 1:
                            link(ins)
                        else:
                            ins.then_inc(s_mall, 1)
                dve.wait_ge(s_mall, (NB - (NB + G - 1) // G) * (1 if k == 2 else 2))
                if k == 2:
                    link(v.tensor_scalar(M[:, :], M[:, :], 0.0, None, ALU.max))
                    link(v.tensor_scalar(stat[:, 0, :], hist[:, 0, :], 1.0, None, ALU.min))
                    link(v.tensor_tensor(m3[:, :, :], m3[:, :, :], stat[:, 0, :].unsqueeze(2).to_broadcast([P, NB, H]), ALU.mult))
                split([m3p[:, :, s_, :] for s_ in range(3)], m3[:, :, :], MT[:, 0:NB * H].rearrange("p (b h) -> p b h", h=H))
                dve.sem_inc(s_feat, 1)

            def attn_pass(k):
                b = groups_before(k, ("attn",))
                bg_ = groups_before(k, ("score", "attn"))
                parts = groups_before(k, ("sum", "attn"))
                heads = 4 if k == 3 else 8
                w = D // heads

                def add_parts(g, vals):
                    for j in range(G):
                        if j == 6:
                            dve.wait_ge(s_part, parts + g + 1)
                        elif j % 3 == 0:
                            dve.wait_ge(s_bank, 2 * (b + g) + j // 3 + 1)
                        acc = ACC[:, bass.ds(vals[j] * AW, AW)]
                        dve.wait_ge(s_acc, G * (parts + g) + j)
                        v.tensor_tensor(acc, acc, bank[4 + j // 3][:, (j % 3) * AW:(j % 3 + 1) * AW], ALU.add).then_inc(s_acc, 1)

                link(v.memset(ACC[:, :], 0.0))
                onehots(k, 0, 0)
                for i in rounds(dve, ITERS):
                    for q in range(RING):
                        g = RING * i + q
                        if there(g - 1):
                            vals = block_regs(g - 1)
                        if there(g + 1):
                            onehots(k, g + 1, q + 1)
                        dve.wait_ge(s_got, bg_ + g + 1)
                        got3 = sm3[:, :, :]
                        v.tensor_reduce(got3, bank[2][:, 0:3 * G * H].rearrange("p (t s h) -> p t h s", s=3, h=H), AX, ALU.add).then_inc(s_d16, 1)
                        dve.wait_ge(s_d16, 2 * (b + g) + 1)
                        v.tensor_tensor(got3, S[:, bass.ds(G * H * g, G * H)].rearrange("p (t h) -> p t h", h=H), got3, ALU.subtract).then_inc(s_d16, 1)
                        dve.wait_ge(s_d16, 2 * (b + g) + 2)
                        if b or there(g - 1):
                            dve.wait_ge(s_ex, b + g)
                        v.tensor_scalar(sm[:, :, :], got3, 60.0, None, ALU.min).then_inc(s_sm, 1)
                        dve.wait_ge(s_ex, b + g + 1)
                        dve.wait_ge(s_rows[q], 16 * G * (k * ITERS + i + 1))
                        dve.sem_inc(s_gate, 1)
                        v.tensor_tensor(msgs[q % 2][:, :, 0:D].rearrange("p t (h d) -> p t h d", h=heads),
                                        rows[:, q, :, :].rearrange("p t (h d) -> p t h d", h=heads),
                                        msgs[q % 2][:, :, D:D + heads].unsqueeze(3).to_broadcast([P, G, heads, w]), ALU.mult).then_inc(s_msg, 1)
                        if there(g - 1):
                            add_parts(g - 1, vals)
                        dve.wait_ge(s_msg, b + g + 1)
                        dve.sem_inc(s_rowfree, 1)
                add_parts(GROUPS - 1, block_regs(GROUPS - 1))
                dve.wait_ge(s_acc, G * (parts + GROUPS))

            dve.wait_ge(s_load_x, 32)
            dve.wait_ge(s_load_w, 16 * 28)
            dve.wait_ge(s_uemm, 2)
            dve.wait_ge(s_esc, COLS // G)
            link(v.tensor_copy(ust[:, :], bank[7][:, 8:16]))
            layernorm()

            def ev(stage):
                dve.wait_ge(s_ev_chunk, CH0[stage + 1])

            for layer in range(3):
                ev(2 + 3 * layer)
                for c in range(7):
                    link(v.bn_stats(bnst[:, c, :], ZT[:, c * 512:min(N, c * 512 + 512)]))
                link(v.bn_aggr(bnv[:, 0:2], bnst[:, :, :].rearrange("p a b -> p (a b)")))
                link(v.tensor_scalar(bnv[:, 2:3], bnv[:, 1:2], EPS, None, ALU.add))
                ask()
                link(v.reciprocal(bnv[:, 4:5], bnv[:, 3:4]))
                link(v.tensor_tensor(bnv[:, 5:6], bnv[:, 4:5], cols[:, 3 + layer:4 + layer], ALU.mult))
                link(v.tensor_tensor(bnv[:, 7:8], bnv[:, 0:1], bnv[:, 5:6], ALU.mult))
                link(v.tensor_tensor(bnv[:, 6:7], cols[:, 6 + layer:7 + layer], bnv[:, 7:8], ALU.subtract))
                ask()
                if layer:
                    link(v.tensor_tensor(HT, HT, FT[:, :], ALU.add))
                dve.sem_inc(s_feat, 1)
                ev(3 + 3 * layer)
                if layer < 2:
                    link(v.tensor_tensor(TAB[:, :, 0:D], HN[:, :, :], per_node(dinv_in[:, :]), ALU.mult))
                    dve.sem_inc(s_table, 1)
                    sum_pass(layer, True)
                    link(v.tensor_tensor(HN[:, :, :], acc3[:, :, 0:D], per_node(dinv_in[:, :]), ALU.mult))
                    dve.sem_inc(s_feat, 1)
            link(v.tensor_tensor(X[:, :, :], X[:, :, :], HN[:, :, :], ALU.add))
            layernorm()
            ev(11)
            split([at3[:, :, s_, :] for s_ in range(3)], TAB[:, :, D + 4:D + 8], M[:, 0:4 * NB].rearrange("p (b h) -> p b h", h=4))
            dve.sem_inc(s_feat, 1)
            dve.sem_inc(s_table, 1)
            dve.sem_inc(s_table, 1)
            score_pass(2)
            attn_pass(3)
            ask()
            link(v.tensor_scalar(stat[:, 0, :], hist[:, 0, :], -1.0, float(E), ALU.mult, ALU.add))
            link(v.tensor_tensor(stat[:, 4:8, :], stat[:, 4:8, :], stat[:, 0, :].unsqueeze(1).to_broadcast([P, 4, NB]), ALU.mult))
            den = acc3[:, :, D:D + 4]
            link(v.tensor_tensor(den, den, stat[:, 4:8, :].rearrange("p h b -> p b h"), ALU.add))
            link(v.reciprocal(den, den))
            for h in range(4):
                link(v.tensor_tensor(HN[:, :, 32 * h:32 * h + 32], acc3[:, :, 32 * h:32 * h + 32],
                                     acc3[:, :, D + h:D + h + 1].to_broadcast([P, NB, 32]), ALU.mult))
            link(v.tensor_tensor(X[:, :, :], X[:, :, :], HN[:, :, :], ALU.add))
            layernorm()
            ev(13)
            dve.sem_inc(s_table, 1)
            dve.sem_inc(s_table, 1)
            split([q_.rearrange("p (b f) -> p b f", b=NB) for q_ in q3], QKV[:, :, 0:D], acc3[:, :, 0:D])
            dve.sem_inc(s_feat, 1)
            score_pass(4)
            attn_pass(5)
            den = acc3[:, :, D:AW]
            link(v.tensor_scalar(den, den, 1.0e-30, None, ALU.max))
            link(v.reciprocal(den, den))
            for h in range(8):
                link(v.tensor_tensor(HN[:, :, 16 * h:16 * h + 16], acc3[:, :, 16 * h:16 * h + 16],
                                     acc3[:, :, D + h:D + h + 1].to_broadcast([P, NB, 16]), ALU.mult))
            dve.sem_inc(s_feat, 1)
            ev(15)
            link(v.tensor_tensor(X[:, :, :], X[:, :, :], HN[:, :, :], ALU.add))
            layernorm()
            for layer in range(2):
                ev(17 + 2 * layer)
                link(v.tensor_tensor(ft3, HN[:, :, :], wgb[:, layer:layer + 1, :].to_broadcast([P, NB, D]), ALU.mult))
                link(v.tensor_reduce(stat[:, 0, :], ft3, AX, ALU.add))
                ask()
                link(v.tensor_tensor(stat[:, 1, :], stat[:, 1, :], dinv_out[:, :], ALU.mult))
                link(v.tensor_tensor(TAB[:, :, 0:D], HN[:, :, :], per_node(stat[:, 1, :]), ALU.mult))
                dve.sem_inc(s_table, 1)
                sum_pass(6 + layer, False)
                link(v.tensor_tensor(ft3, acc3[:, :, 0:D], per_node(dinv_out[:, :]), ALU.mult))
                link(v.tensor_tensor(HN[:, :, :], HN[:, :, :], ft3, ALU.add))
                if layer == 0:
                    link(v.tensor_scalar(HN[:, :, :], HN[:, :, :], 0.0, None, ALU.max))
                    dve.sem_inc(s_feat, 1)
            link(v.scalar_tensor_tensor(X[:, :, :], HN[:, :, :], 0.0, X[:, :, :], ALU.max, ALU.add))
            dve.sem_inc(s_table, 1)


_INS = ['x', 'src', 'dst', 'edge_attr_64', 'edge_weight', 'L0_gnn_fc_w', 'L0_gnn_fc_b', 'L0_gnn_conv_w', 'L0_gnn_conv_b',
        'L0_gnn_bn_gamma', 'L0_gnn_bn_beta', 'L1_gnn_W_node', 'L1_gnn_W_edge', 'L1_gnn_a', 'L2_gnn_Wq', 'L2_gnn_bq',
        'L2_gnn_Wk', 'L2_gnn_bk', 'L2_gnn_Wv', 'L2_gnn_bv', 'L2_gnn_Wo', 'L2_gnn_bo', 'L3_gnn_Wt', 'L3_gnn_bt',
        'L3_gnn_Wg', 'L3_gnn_bg']


def kernel(**inputs):
    import numpy as _np
    import concourse.bacc as _bacc
    from concourse import mybir as _mybir
    from concourse.bass_utils import run_bass_kernel_spmd as _run

    nc = _bacc.Bacc("TRN2", target_bir_lowering=False, num_devices=1)
    arrays, args = {}, []
    for name in _INS:
        a = _np.ascontiguousarray(inputs[name])
        arrays[f"in_{name}_dram"] = a
        args.append(nc.dram_tensor(f"in_{name}_dram", a.shape, _mybir.dt.from_np(a.dtype), kind="ExternalInput").ap())
    args.append(nc.dram_tensor("out_dram", (N, D), _mybir.dt.float32, kind="ExternalOutput").ap())
    gnn_kernel(nc, *args)
    r = _run(nc, [arrays], core_ids=[0])
    return r.results[0]["out_dram"]
```
